# Optimizing a Trainium2 kernel written in Bass

```python
import numpy as np
import jax
import jax.numpy as jnp

def _softmax(x, axis=-1):
    return jax.nn.softmax(x, axis=axis)

def _gelu(x):
    return jax.nn.gelu(x, approximate=True)

def _silu(x):
    return jax.nn.silu(x)

def _sigmoid(x):
    return jax.nn.sigmoid(x)

def _layernorm(x, axis=-1, eps=1e-05):
    m = jnp.mean(x, axis=axis, keepdims=True)
    v = jnp.var(x, axis=axis, keepdims=True)
    return (x - m) / jnp.sqrt(v + eps)

def _scatter_add(tgt, idx, src, axis=0):
    return tgt.at[idx].add(src)

def _segment_sum(src, seg, n):
    return jax.ops.segment_sum(src, seg, n)
kernel_name = 'mk_prb_d1_jaxref_r4_29a738'

def setup_inputs(seed: int=0):
    np.random.seed(seed)
    _w = jnp.asarray

    def _L0_attn_setup():
        import jax, jax.numpy as jnp
        import numpy as np
        import math
        B, T, E, H = (4, 512, 256, 16)
        D = E // H
        rng = jax.random.key(seed)
        k1, k2, k3, k4, k5 = jax.random.split(rng, 5)
        scale_w = 1.0 / math.sqrt(E)
        return {'query': jax.random.normal(k1, (B, T, E), jnp.float32), 'key': jax.random.normal(k2, (B, T, E), jnp.float32), 'value': jax.random.normal(k3, (B, T, E), jnp.float32), 'in_proj_weight': jax.random.normal(k4, (3 * E, E), jnp.float32) * scale_w, 'out_proj_weight': jax.random.normal(k5, (E, E), jnp.float32) * scale_w}
    _L0_attn_in = _L0_attn_setup()

    def _L0_ffn_setup():
        import jax, jax.numpy as jnp
        import numpy as np
        DIM = 256
        DEPTH = 2
        HEADS = 8
        DIM_HEAD = 64
        WINDOW = 128
        INNER = HEADS * DIM_HEAD
        HID = int(DIM * 4 * 2 / 3)
        B, N = (2, 2048)
        QK_SCALE = 8.0

        def shift_token(t):
            t1, t2 = jnp.split(t, 2, axis=-1)
            t2 = jnp.pad(t2, ((0, 0), (1, 0), (0, 0)))[:, :-1]
            return jnp.concatenate([t1, t2], axis=-1)

        def l2norm(t):
            return t / jnp.clip(jnp.linalg.norm(t, axis=-1, keepdims=True), 1e-12)

        def rotate_half(x):
            x1, x2 = jnp.split(x, 2, axis=-1)
            return jnp.concatenate([-x2, x1], axis=-1)

        def rotary_xpos(q, k):
            n = q.shape[-2]
            half_idx = jnp.arange(0, DIM_HEAD, 2, dtype=jnp.float32)
            inv_freq = 1.0 / 10000.0 ** (half_idx / DIM_HEAD)
            t = jnp.arange(n, dtype=jnp.float32)
            freqs = t[:, None] * inv_freq[None, :]
            freqs = jnp.concatenate([freqs, freqs], axis=-1)
            base = (half_idx + 0.4 * DIM_HEAD) / (1.4 * DIM_HEAD)
            power = (t - n // 2) / float(WINDOW // 2)
            scale = base[None, :] ** power[:, None]
            scale = jnp.concatenate([scale, scale], axis=-1)
            cos, sin = (jnp.cos(freqs), jnp.sin(freqs))
            q = q * cos * scale + rotate_half(q) * sin * scale
            k = k * cos / scale + rotate_half(k) * sin / scale
            return (q, k)

        def local_attention(q, k, v):
            b, h, n, d = q.shape
            w = n // WINDOW
            bq = q.reshape(b, h, w, WINDOW, d) * QK_SCALE
            bk = k.reshape(b, h, w, WINDOW, d)
            bv = v.reshape(b, h, w, WINDOW, d)

            def look_around(t):
                p = jnp.pad(t, ((0, 0), (0, 0), (1, 0), (0, 0), (0, 0)))
                return jnp.concatenate([p[:, :, :w], p[:, :, 1:]], axis=3)
            bk, bv = (look_around(bk), look_around(bv))
            bt = jnp.arange(n).reshape(w, WINDOW)
            btp = jnp.pad(bt, ((1, 0), (0, 0)), constant_values=-1)
            btk = jnp.concatenate([btp[:w], btp[1:]], axis=1)
            sim = jnp.einsum('bhwid,bhwjd->bhwij', bq, bk)
            i = bt[:, :, None]
            j = btk[:, None, :]
            mask = (i < j) | (i > j + WINDOW) | (j == -1)
            sim = jnp.where(mask, -jnp.finfo(sim.dtype).max, sim)
            attn = jax.nn.softmax(sim, axis=-1)
            out = jnp.einsum('bhwij,bhwjd->bhwid', attn, bv)
            return out.reshape(b, h, n, d)

        def _layer(x, wqkv, qs, ksc, wo, lg, lb, w1, b1, w2, b2):
            b, n, _ = x.shape
            h = shift_token(x)
            qkv = h @ wqkv
            q, k, v = jnp.split(qkv, 3, axis=-1)
            to_heads = lambda t: t.reshape(b, n, HEADS, DIM_HEAD).transpose(0, 2, 1, 3)
            q, k, v = (to_heads(q), to_heads(k), to_heads(v))
            q = l2norm(q) * qs
            k = l2norm(k) * ksc
            q, k = rotary_xpos(q, k)
            o = local_attention(q, k, v)
            o = o.transpose(0, 2, 1, 3).reshape(b, n, INNER)
            x = x + o @ wo
            h = shift_token(x)
            mu = h.mean(-1, keepdims=True)
            var = h.var(-1, keepdims=True)
            h = (h - mu) / jnp.sqrt(var + 1e-05) * lg + lb
            h = h @ w1 + b1
            a, g = jnp.split(h, 2, axis=-1)
            h = a * jax.nn.gelu(g, approximate=False)
            x = x + h @ w2 + b2
            return x
        key = jax.random.key(seed)
        ks = jax.random.split(key, 6)
        return {'x': jax.random.normal(ks[0], (B, N, DIM), jnp.float32), 'wqkv': jax.random.normal(ks[1], (DEPTH, DIM, 3 * INNER), jnp.float32) * 0.02, 'q_scale': jnp.ones((DEPTH, DIM_HEAD), jnp.float32), 'k_scale': jnp.ones((DEPTH, DIM_HEAD), jnp.float32), 'wo': jax.random.normal(ks[2], (DEPTH, INNER, DIM), jnp.float32) * 0.02, 'ln_g': jnp.ones((DEPTH, DIM), jnp.float32), 'ln_b': jnp.zeros((DEPTH, DIM), jnp.float32), 'w1': jax.random.normal(ks[3], (DEPTH, DIM, 2 * HID), jnp.float32) * 0.02, 'b1': jnp.zeros((DEPTH, 2 * HID), jnp.float32), 'w2': jax.random.normal(ks[4], (DEPTH, HID, DIM), jnp.float32) * 0.02, 'b2': jnp.zeros((DEPTH, DIM), jnp.float32)}
    _L0_ffn_in = _L0_ffn_setup()
    _d = {'L0_attn_query': _L0_attn_in['query'], 'L0_attn_key': _L0_attn_in['key'], 'L0_attn_value': _L0_attn_in['value'], 'L0_attn_in_proj_weight': _L0_attn_in['in_proj_weight'], 'L0_attn_out_proj_weight': _L0_attn_in['out_proj_weight'], 'L0_ffn_wqkv': _L0_ffn_in['wqkv'], 'L0_ffn_q_scale': _L0_ffn_in['q_scale'], 'L0_ffn_k_scale': _L0_ffn_in['k_scale'], 'L0_ffn_wo': _L0_ffn_in['wo'], 'L0_ffn_ln_g': _L0_ffn_in['ln_g'], 'L0_ffn_ln_b': _L0_ffn_in['ln_b'], 'L0_ffn_w1': _L0_ffn_in['w1'], 'L0_ffn_b1': _L0_ffn_in['b1'], 'L0_ffn_w2': _L0_ffn_in['w2'], 'L0_ffn_b2': _L0_ffn_in['b2']}
    _x0 = _d['L0_attn_query']
    _d['L0_attn_query'] = jax.random.normal(jax.random.fold_in(jax.random.key(seed), 1), (4, 1024, 256), dtype=_x0.dtype)
    del _x0
    return _d

def reference(L0_attn_query, L0_attn_key, L0_attn_value, L0_attn_in_proj_weight, L0_attn_out_proj_weight, L0_ffn_wqkv, L0_ffn_q_scale, L0_ffn_k_scale, L0_ffn_wo, L0_ffn_ln_g, L0_ffn_ln_b, L0_ffn_w1, L0_ffn_b1, L0_ffn_w2, L0_ffn_b2):

    def _L0_attn_ref(query, key, value, in_proj_weight, out_proj_weight):
        import jax, jax.numpy as jnp
        import numpy as np
        import math
        B, T, E, H = (4, 512, 256, 16)
        D = E // H
        b, t, e = query.shape
        qkv = jnp.einsum('bte,fe->btf', query, in_proj_weight).reshape(b, t, 3, H, D)
        q = jnp.transpose(qkv[:, :, 0], (0, 2, 1, 3))
        k = jnp.transpose(qkv[:, :, 1], (0, 2, 1, 3))
        v = jnp.transpose(qkv[:, :, 2], (0, 2, 1, 3))
        q = q / math.sqrt(D)
        scores = jnp.einsum('bhqd,bhkd->bhqk', q, k)
        pos = jnp.arange(t)
        causal = pos[:, None] >= pos[None, :]
        scores = jnp.where(causal[None, None], scores, jnp.float32(-jnp.inf))
        attn = jax.nn.softmax(scores, axis=-1)
        out = jnp.einsum('bhqk,bhkd->bhqd', attn, v)
        out = jnp.transpose(out, (0, 2, 1, 3)).reshape(b, t, e)
        out = jnp.einsum('bte,fe->btf', out, out_proj_weight)
        return out

    def _L0_ffn_ref(x, wqkv, q_scale, k_scale, wo, ln_g, ln_b, w1, b1, w2, b2):
        import jax, jax.numpy as jnp
        import numpy as np
        DIM = 256
        DEPTH = 2
        HEADS = 8
        DIM_HEAD = 64
        WINDOW = 128
        INNER = HEADS * DIM_HEAD
        HID = int(DIM * 4 * 2 / 3)
        B, N = (2, 2048)
        QK_SCALE = 8.0

        def shift_token(t):
            t1, t2 = jnp.split(t, 2, axis=-1)
            t2 = jnp.pad(t2, ((0, 0), (1, 0), (0, 0)))[:, :-1]
            return jnp.concatenate([t1, t2], axis=-1)

        def l2norm(t):
            return t / jnp.clip(jnp.linalg.norm(t, axis=-1, keepdims=True), 1e-12)

        def rotate_half(x):
            x1, x2 = jnp.split(x, 2, axis=-1)
            return jnp.concatenate([-x2, x1], axis=-1)

        def rotary_xpos(q, k):
            n = q.shape[-2]
            half_idx = jnp.arange(0, DIM_HEAD, 2, dtype=jnp.float32)
            inv_freq = 1.0 / 10000.0 ** (half_idx / DIM_HEAD)
            t = jnp.arange(n, dtype=jnp.float32)
            freqs = t[:, None] * inv_freq[None, :]
            freqs = jnp.concatenate([freqs, freqs], axis=-1)
            base = (half_idx + 0.4 * DIM_HEAD) / (1.4 * DIM_HEAD)
            power = (t - n // 2) / float(WINDOW // 2)
            scale = base[None, :] ** power[:, None]
            scale = jnp.concatenate([scale, scale], axis=-1)
            cos, sin = (jnp.cos(freqs), jnp.sin(freqs))
            q = q * cos * scale + rotate_half(q) * sin * scale
            k = k * cos / scale + rotate_half(k) * sin / scale
            return (q, k)

        def local_attention(q, k, v):
            b, h, n, d = q.shape
            w = n // WINDOW
            bq = q.reshape(b, h, w, WINDOW, d) * QK_SCALE
            bk = k.reshape(b, h, w, WINDOW, d)
            bv = v.reshape(b, h, w, WINDOW, d)

            def look_around(t):
                p = jnp.pad(t, ((0, 0), (0, 0), (1, 0), (0, 0), (0, 0)))
                return jnp.concatenate([p[:, :, :w], p[:, :, 1:]], axis=3)
            bk, bv = (look_around(bk), look_around(bv))
            bt = jnp.arange(n).reshape(w, WINDOW)
            btp = jnp.pad(bt, ((1, 0), (0, 0)), constant_values=-1)
            btk = jnp.concatenate([btp[:w], btp[1:]], axis=1)
            sim = jnp.einsum('bhwid,bhwjd->bhwij', bq, bk)
            i = bt[:, :, None]
            j = btk[:, None, :]
            mask = (i < j) | (i > j + WINDOW) | (j == -1)
            sim = jnp.where(mask, -jnp.finfo(sim.dtype).max, sim)
            attn = jax.nn.softmax(sim, axis=-1)
            out = jnp.einsum('bhwij,bhwjd->bhwid', attn, bv)
            return out.reshape(b, h, n, d)

        def _layer(x, wqkv, qs, ksc, wo, lg, lb, w1, b1, w2, b2):
            b, n, _ = x.shape
            h = shift_token(x)
            qkv = h @ wqkv
            q, k, v = jnp.split(qkv, 3, axis=-1)
            to_heads = lambda t: t.reshape(b, n, HEADS, DIM_HEAD).transpose(0, 2, 1, 3)
            q, k, v = (to_heads(q), to_heads(k), to_heads(v))
            q = l2norm(q) * qs
            k = l2norm(k) * ksc
            q, k = rotary_xpos(q, k)
            o = local_attention(q, k, v)
            o = o.transpose(0, 2, 1, 3).reshape(b, n, INNER)
            x = x + o @ wo
            h = shift_token(x)
            mu = h.mean(-1, keepdims=True)
            var = h.var(-1, keepdims=True)
            h = (h - mu) / jnp.sqrt(var + 1e-05) * lg + lb
            h = h @ w1 + b1
            a, g = jnp.split(h, 2, axis=-1)
            h = a * jax.nn.gelu(g, approximate=False)
            x = x + h @ w2 + b2
            return x
        for l in range(DEPTH):
            x = _layer(x, wqkv[l], q_scale[l], k_scale[l], wo[l], ln_g[l], ln_b[l], w1[l], b1[l], w2[l], b2[l])
        return x
    x = L0_attn_query
    xn = _layernorm(x, axis=-1)
    x = x + _L0_attn_ref(xn, L0_attn_key, L0_attn_value, L0_attn_in_proj_weight, L0_attn_out_proj_weight) + _L0_ffn_ref(xn, L0_ffn_wqkv, L0_ffn_q_scale, L0_ffn_k_scale, L0_ffn_wo, L0_ffn_ln_g, L0_ffn_ln_b, L0_ffn_w1, L0_ffn_b1, L0_ffn_w2, L0_ffn_b2)
    return x

_drawn_inputs = setup_inputs


def setup_inputs(seed=0):
    import zlib

    import numpy as np

    out = dict(_drawn_inputs(seed))
    spreads = {'L0_ffn_q_scale': (1.0, 0.6),
     'L0_ffn_k_scale': (1.0, 0.6),
     'L0_ffn_ln_g': (1.0, 0.6),
     'L0_ffn_ln_b': (0.0, 0.8),
     'L0_ffn_b1': (0.0, 0.8),
     'L0_ffn_b2': (0.0, 0.1)}
    factors = {'L0_ffn_wqkv': 3.395, 'L0_ffn_wo': 3.323}
    for name, (base, spread) in spreads.items():
        noise = np.random.default_rng([zlib.crc32(name.encode()), seed]).standard_normal(out[name].shape)
        drawn = base * np.exp(spread * noise) if base else spread * noise
        out[name] = jnp.asarray(drawn.astype(out[name].dtype))
    for name, factor in factors.items():
        out[name] = (out[name] * factor).astype(out[name].dtype)
    return out
```

```python
from contextlib import ExitStack

import concourse.bass as bass
from concourse import mybir

F32 = mybir.dt.float32
F32R = mybir.dt.float32r
BF16 = mybir.dt.bfloat16
ALU = mybir.AluOpType
ACT = mybir.ActivationFunctionType
AX = mybir.AxisListType

P = 128
B, T, E = 4, 1024, 256
TILES = B * T // P
CHUNK = 512
CT = CHUNK // P
CHUNKS = B * T // CHUNK
KE = E // P
EPS = 1e-5
NEG = -3e38

HC, DC = 16, 16
UNITS = B * HC
KT = T // P
STACK = 4 * DC
KROWS = 96
VW = 32

DEPTH, HL, DL = 2, 8, 64
INNER = HL * DL
HID = 682
HT = 6
HIDP = HT * P
HI, LO = 0, 1
PRODUCTS = ((HI, HI), (HI, LO), (LO, HI))


class Chain:

    def __init__(self, engine, sem, base=0):
        self.engine, self.sem, self.base, self.n = engine, sem, base, 0

    def add(self, instruction):
        instruction.then_inc(self.sem, 1)
        self.n += 1

    def wait(self):
        self.engine.wait_ge(self.sem, self.base + self.n)


def build(nc, x, w_in, w_out, w_qkv, w_o, w1, w2, ln_gb, b1, b2, qk_scale, trig, out):
    layer_in = nc.dram_tensor("layer_in", (DEPTH + 1, B, 1 + T, E), F32, kind="Internal").ap()
    layer_mid = nc.dram_tensor("layer_mid", (DEPTH, B, 1 + T, E), F32, kind="Internal").ap()
    q_stack = nc.dram_tensor("q_stack", (UNITS, STACK, T), F32, kind="Internal").ap()
    k_stack = nc.dram_tensor("k_stack", (UNITS, STACK, T), F32, kind="Internal").ap()
    neg_max = nc.dram_tensor("neg_max", (4, 2, T), F32, kind="Internal").ap()
    attn_out = nc.dram_tensor("attn_out", (TILES, P, E), F32, kind="Internal").ap()

    with ExitStack() as top:
        def tensor(ctx, name, shape, dt=F32):
            return ctx.enter_context(nc.sbuf_tensor(name, shape, dt))

        def psum(ctx, name, shape):
            return ctx.enter_context(nc.psum_tensor(name, shape, F32))

        def sem(name):
            return top.enter_context(nc.semaphore(name))

        ident = tensor(top, "ident", [P, P])
        ident_bf = tensor(top, "ident_bf", [P, P], BF16)
        wout_s = tensor(top, "wout_s", [P, 2, KE, E], F32R)

        with ExitStack() as ctx:
            values = tensor(ctx, "values", [P, UNITS, KT, DC])
            zeros = tensor(ctx, "zeros", [12, T])
            causal_qk = tensor(ctx, "causal_qk", [P, P], BF16)
            causal_kq = tensor(ctx, "causal_kq", [P, P], BF16)
            with ExitStack() as inner:
                win_s = tensor(inner, "win_s", [P, 2, KE, 3 * E], F32R)
                project(nc, inner, tensor, psum, sem, x, w_in, w_out, layer_in, layer_mid, q_stack, k_stack,
                        ident, ident_bf, causal_qk, causal_kq, zeros, win_s, wout_s, values)
            with ExitStack() as inner:
                attend(nc, inner, tensor, psum, sem, q_stack, k_stack, neg_max, attn_out,
                       ident, ident_bf, causal_qk, causal_kq, zeros, values)
        with ExitStack() as ctx:
            local_layers(nc, ctx, tensor, psum, sem, layer_in, layer_mid, w_qkv, w_o, w1, w2, ln_gb, b1, b2,
                         qk_scale, trig, ident, ident_bf)
        with ExitStack() as ctx:
            finish(nc, ctx, tensor, psum, sem, x, layer_in, attn_out, ident, wout_s, out)


def project(nc, ctx, tensor, psum, sem, x, w_in, w_out, layer_in, layer_mid, q_stack, k_stack,
            ident, ident_bf, causal_qk, causal_kq, zeros, win_s, wout_s, values):
    w_raw = tensor(ctx, "w_raw", [P, KE, 4 * E])
    xin = [tensor(ctx, f"xin{j}", [P, CT, E]) for j in range(2)]
    xn = [tensor(ctx, f"xn{j}", [P, CT, E]) for j in range(2)]
    stats = tensor(ctx, "stats", [P, CT, 6])
    mean_var = tensor(ctx, "mean_var", [P, CT, 2])
    var_eps = tensor(ctx, "var_eps", [P, CT])
    rstd = tensor(ctx, "rstd", [P, CT])
    minus_half = tensor(ctx, "minus_half", [P, CT])
    xt = [tensor(ctx, f"xt{j}", [P, 2, KE, CHUNK], F32R) for j in range(2)]
    qk = [tensor(ctx, f"qk{j}", [P, 2, 4, CHUNK], F32R) for j in range(2)]
    ps_xt = psum(ctx, "ps_xt", [P, KE, CHUNK])
    ps_qk = psum(ctx, "ps_qk", [P, 4, CHUNK])
    ps_v = psum(ctx, "ps_v", [P, 2, 2, E])

    const_made = sem("p_const_made")
    w_loaded = sem("p_w_loaded")
    zero_rows = sem("p_zero_rows")
    w_split = sem("p_w_split")
    x_loaded = [sem(f"p_x_loaded{j}") for j in range(2)]
    dve_own = sem("p_dve_own")
    counted = sem("p_counted")
    var_ready = sem("p_var_ready")
    rstd_ready = sem("p_rstd_ready")
    xn_ready = sem("p_xn_ready")
    xn_stored = [sem(f"p_xn_stored{j}") for j in range(2)]
    xt_made = sem("p_xt_made")
    xt_hi = sem("p_xt_hi")
    xt_lo = sem("p_xt_lo")
    qk_made = sem("p_qk_made")
    qk_hi = sem("p_qk_hi")
    qk_lo = sem("p_qk_lo")
    v_made = sem("p_v_made")
    v_kept = sem("p_v_kept")
    qk_stored = [sem(f"p_qk_stored{j}") for j in range(2)]
    DVE_LN = 2 * CT

    with nc.Block() as block:

        @block.gpsimd
        def _(pool):
            for t in (ident, ident_bf, causal_qk, causal_kq, zeros):
                pool.memset(t[:], 0.0).then_inc(const_made, 1)
            pool.memset(minus_half[:], -0.5).then_inc(const_made, 1)
            pool.wait_ge(const_made, 6)
            for t in (ident, ident_bf):
                pool.affine_select(out=t[:], in_=t[:], compare_op=ALU.not_equal, fill=1.0, base=0,
                                   pattern=[[-1, P]], channel_multiplier=1).then_inc(const_made, 1)
            pool.affine_select(out=causal_qk[:], in_=causal_qk[:], compare_op=ALU.is_ge, fill=NEG, base=0,
                               pattern=[[-1, P]], channel_multiplier=1).then_inc(const_made, 1)
            pool.affine_select(out=causal_kq[:], in_=causal_kq[:], compare_op=ALU.is_ge, fill=NEG, base=0,
                               pattern=[[1, P]], channel_multiplier=-1).then_inc(const_made, 1)
            with pool.Fori(0, CHUNKS) as c:
                pool.wait_ge(var_ready, c + 1)
                pool.tensor_tensor(rstd[:], var_eps[:], minus_half[:], ALU.pow).then_inc(rstd_ready, 1)

        @block.sync
        def _(sp):
            sp.dma_start(w_raw[:, :, 0:3 * E], w_in.rearrange("(k p) n -> p k n", p=P)).then_inc(w_loaded, 16)
            sp.dma_start(w_raw[:, :, 3 * E:4 * E], w_out.rearrange("(k p) n -> p k n", p=P)).then_inc(w_loaded, 16)
            sp.wait_ge(const_made, 6)
            sp.dma_start(layer_in[:, :, 0:1, :].rearrange("l b r e -> (l b r) e"), zeros[0:12, 0:E]).then_inc(zero_rows, 16)
            sp.dma_start(layer_mid[:, :, 0:1, :].rearrange("l b r e -> (l b r) e"), zeros[0:8, 0:E]).then_inc(zero_rows, 16)

            def load_x(i, j):
                b, half = i, j
                sp.dma_start(xin[j][:], x[b, half * CHUNK:(half + 1) * CHUNK, :]
                             .rearrange("(q p) e -> p q e", p=P)).then_inc(x_loaded[j], 16)

            def store_xn(i, j):
                sp.wait_ge(xn_ready, 2 * i + j + 1)
                sp.dma_start(layer_in[0, i, 1 + j * CHUNK:1 + (j + 1) * CHUNK, :]
                             .rearrange("(q p) e -> p q e", p=P), xn[j][:]).then_inc(xn_stored[j], 16)

            def store_qk(i, j):
                for m in range(4):
                    dst, h0 = (q_stack, k_stack)[m // 2], i * HC + m % 2 * (HC // 2)
                    for part in (HI, LO):
                        sp.wait_ge((qk_hi, qk_lo)[part], 4 * (2 * i + j) + m + 1)
                        places = (part, part + 2) if m < 2 else (2 * part, 2 * part + 1)
                        for r in places:
                            sp.dma_start(dst[bass.ds(h0, HC // 2), r * DC:(r + 1) * DC, j * CHUNK:(j + 1) * CHUNK],
                                         qk[j][:, part, m, :].bitcast(F32)).then_inc(qk_stored[j], 16)

            for j in range(2):
                load_x(0, j)
            with sp.Fori(0, B - 1) as i:
                for j in range(2):
                    store_xn(i, j)
                    load_x(i + 1, j)
                    store_qk(i, j)
            for j in range(2):
                store_xn(B - 1, j)
                store_qk(B - 1, j)
            sp.wait_ge(zero_rows, 32)
            for j in range(2):
                sp.wait_ge(xn_stored[j], 16 * B)
                sp.wait_ge(qk_stored[j], 16 * 16 * B)

        @block.vector
        def _(dve):
            dve.wait_ge(w_loaded, 32)
            dve.tensor_copy(win_s[:, HI], w_raw[:, :, 0:3 * E]).then_inc(w_split, 1)
            dve.tensor_copy(wout_s[:, HI], w_raw[:, :, 3 * E:4 * E]).then_inc(w_split, 1)
            dve.wait_ge(w_split, 2)
            dve.tensor_tensor(win_s[:, LO], w_raw[:, :, 0:3 * E], win_s[:, HI], ALU.subtract).then_inc(w_split, 1)
            dve.tensor_tensor(wout_s[:, LO], w_raw[:, :, 3 * E:4 * E], wout_s[:, HI], ALU.subtract).then_inc(w_split, 1)
            with dve.Fori(0, B) as i:
                for j in range(2):
                    c = 2 * i + j
                    own = Chain(dve, dve_own, c * DVE_LN)
                    dve.wait_ge(x_loaded[j], 16 * (i + 1))
                    for q in range(CT):
                        own.add(dve.bn_stats(stats[:, q, :], xin[j][:, q, :]))
                    own.wait()
                    dve.sem_inc(counted, 1)
                    for q in range(CT):
                        own.add(dve.bn_aggr(mean_var[:, q, :], stats[:, q, :]))
                    own.wait()
                    dve.tensor_scalar(var_eps[:], mean_var[:, :, 1], EPS, None, ALU.add).then_inc(var_ready, 1)
                    dve.wait_ge(rstd_ready, c + 1)
                    dve.wait_ge(xn_stored[j], 16 * i)
                    dve.wait_ge(xt_made, 2 * c)
                    for q in range(CT):
                        last = dve.tensor_scalar(xn[j][:, q, :], xin[j][:, q, :], mean_var[:, q, 0:1], rstd[:, q:q + 1],
                                                 ALU.subtract, ALU.mult)
                    last.then_inc(xn_ready, 1)
                    for f in range(KE):
                        dve.wait_ge(xt_hi, KE * c + f + 1)
                        dve.tensor_tensor(xt[j][:, LO, f, :], ps_xt[:, f, :], xt[j][:, HI, f, :], ALU.subtract).then_inc(xt_lo, 1)
                    for m in range(4):
                        dve.wait_ge(qk_hi, 4 * c + m + 1)
                        dve.wait_ge(qk_stored[j], 256 * i)
                        dve.scalar_tensor_tensor(out=qk[j][:, LO, m, :], in0=ps_qk[:, m, :], scalar=DC ** -0.5 if m < 2 else 1.0,
                                                 in1=qk[j][:, HI, m, :], op0=ALU.mult, op1=ALU.subtract).then_inc(qk_lo, 1)

        @block.scalar
        def _(act):
            with act.Fori(0, B) as i:
                for j in range(2):
                    c = 2 * i + j
                    for f in range(KE):
                        act.wait_ge(xt_made, KE * c + f + 1)
                        act.activation(xt[j][:, HI, f, :], ps_xt[:, f, :], ACT.Copy).then_inc(xt_hi, 1)
                    act.wait_ge(qk_stored[j], 256 * i)
                    for m in range(4):
                        act.wait_ge(qk_made, 4 * c + m + 1)
                        act.activation(qk[j][:, HI, m, :], ps_qk[:, m, :], ACT.Copy, scale=DC ** -0.5 if m < 2 else 1.0).then_inc(qk_hi, 1)
                    for v in range(2):
                        act.wait_ge(v_made, 2 * c + v + 1)
                        kt0 = CT * j + 2 * v
                        act.activation(values[:, bass.ds(i * HC, HC), kt0:kt0 + 2, :].rearrange("p h t d -> p t h d"),
                                       ps_v[:, v].rearrange("p t (h d) -> p t h d", h=HC), ACT.Copy).then_inc(v_kept, 1)

        @block.tensor
        def _(pe):
            pe.wait_ge(const_made, 10)
            pe.wait_ge(w_split, 4)
            with pe.Fori(0, B) as i:
                for j in range(2):
                    c = 2 * i + j
                    pe.wait_ge(xn_ready, c + 1)
                    pe.wait_ge(xt_lo, KE * c)
                    for f in range(KE):
                        for q in range(CT):
                            mm = pe.transpose(ps_xt[:, f, q * P:(q + 1) * P], xn[j][:, q, f * P:(f + 1) * P], ident[:])
                        mm.then_inc(xt_made, 1)
                    pe.wait_ge(xt_lo, KE * c + KE)
                    pe.wait_ge(qk_lo, 4 * c)
                    for m in range(4):
                        products(pe, ps_qk[:, m, :], lambda part, f: win_s[:, part, f, m * P:(m + 1) * P],
                                 lambda part, f: xt[j][:, part, f, :], KE).then_inc(qk_made, 1)
                    pe.wait_ge(v_kept, 2 * c)
                    for q in range(CT):
                        mm = products(pe, ps_v[:, q // 2, q % 2, :], lambda part, f: xt[j][:, part, f, q * P:(q + 1) * P],
                                      lambda part, f: win_s[:, part, f, 2 * E:3 * E], KE)
                        if q % 2:
                            mm.then_inc(v_made, 1)


def products(pe, out, stationary, moving, tiles):
    steps = [(f, a, b) for f in range(tiles) for a, b in PRODUCTS]
    for n, (f, a, b) in enumerate(steps):
        mm = pe.matmul(out, stationary(a, f), moving(b, f), start=n == 0, stop=n == len(steps) - 1)
    return mm


PIECES = [(t, k0, min(CHUNK, (t + 1) * P - k0)) for t in range(KT) for k0 in range(0, (t + 1) * P, CHUNK)]
PIECES_AT = (3, 2, 2, 2, 2, 1, 0, 0)
AHEAD = 2
RING = 4
MAXIMUM_SLOTS = len(PIECES) + 1
SLOTS = MAXIMUM_SLOTS + 2


def first_slot(i, j):
    n = AHEAD * MAXIMUM_SLOTS - 2 + SLOTS * j
    if isinstance(i, int) and i == 0 and j == 0:
        n += 2
    if isinstance(i, int) and i == UNITS // RING - 1 and j > RING - AHEAD:
        n -= MAXIMUM_SLOTS * (j - (RING - AHEAD))
    return SLOTS * RING * i + n, n % 2


def uses(i, j):
    ahead = not (isinstance(i, int) and i == UNITS // RING - 1 and j >= RING - AHEAD)
    outputs = not (isinstance(i, int) and i == 0 and j == 0)
    listed, k = [], 0
    for kt in range(KT):
        if ahead:
            listed += [(kt, "piece", k + n) for n in range(PIECES_AT[kt])]
            k += PIECES_AT[kt]
        if outputs and kt == 1:
            listed += [(kt, "output", c) for c in range(2)]
    if ahead:
        listed.append((KT, "maxima", 0))
    return listed


def attend(nc, ctx, tensor, psum, sem, q_stack, k_stack, neg_max, attn_out,
           ident, ident_bf, causal_qk, causal_kq, zeros, values):
    qs = [tensor(ctx, f"qs{j}", [KROWS, T], F32R) for j in range(RING)]
    ks = [tensor(ctx, f"ks{j}", [KROWS, T], F32R) for j in range(RING)]
    vs = [tensor(ctx, f"vs{j}", [P, KT, VW]) for j in range(RING)]
    prob_a = tensor(ctx, "prob_a", [P, 4, T])
    prob_b = tensor(ctx, "prob_b", [P, 4, CHUNK])
    maxima = [tensor(ctx, f"maxima{j}", [P, KT + 4]) for j in range(2)]
    max_parts = [tensor(ctx, f"max_parts{j}", [KT, 2, P], F32R) for j in range(RING)]
    sums = [tensor(ctx, f"sums{j}", [P, T]) for j in range(2)]
    folded = tensor(ctx, "folded", [P, 2, CT, VW])
    rsum = tensor(ctx, "rsum", [P, 2, CT])
    heads_out = tensor(ctx, "heads_out", [P, TILES, E])
    ps_s = psum(ctx, "ps_s", [P, 2, CHUNK])
    ps_t = psum(ctx, "ps_t", [P, 2, T])
    ps_o = psum(ctx, "ps_o", [P, 2, CHUNK])

    rows_made = sem("a_rows_made")
    loaded = [sem(f"a_loaded{j}") for j in range(RING)]
    v_ready = sem("a_v_ready")
    slot_made = sem("a_slot_made")
    slot_used = sem("a_slot_used")
    part_hi = sem("a_part_hi")
    rsum_ready = sem("a_rsum_ready")
    max_ready = sem("a_max_ready")
    max_stored = [sem(f"a_max_stored{j}") for j in range(RING)]
    max_loaded = [sem(f"a_max_loaded{j}") for j in range(RING)]
    st_made = sem("a_st_made")
    p_ready = sem("a_p_ready")
    pv_done = sem("a_pv_done")
    sums_ready = sem("a_sums_ready")
    out_done = sem("a_out_done")
    attn_stored = sem("a_attn_stored")
    LOADS = 48

    with nc.Block() as block:

        @block.gpsimd
        def _(pool):
            constants = [(t[j][64:KROWS, :].bitcast(F32), 0.0) for j in range(RING) for t in (qs, ks)]
            constants += [(vs[j][:, :, DC:VW], 0.0) for j in range(RING)]
            constants += [(prob_a[:, r, 0:r * P], 0.0) for r in range(1, 4)]
            constants += [(ks[j][64:66, :].bitcast(F32), 1.0) for j in range(RING)]
            constants += [(vs[j][:, :, DC:DC + 1], 1.0) for j in range(RING)]
            for n, (rows, value) in enumerate(constants):
                pool.memset(rows, value).then_inc(rows_made, 1)
                pool.wait_ge(rows_made, n + 1)

            def values_of(u, j):
                pool.tensor_copy(vs[j][:, :, 0:DC], values[:, u]).then_inc(v_ready, 1)

            for j in range(RING):
                values_of(j, j)
            with pool.Fori(1, UNITS // RING) as i:
                for j in range(RING):
                    u = RING * i + j
                    pool.wait_ge(pv_done, KT * (u - RING + 1))
                    values_of(u, j)

        @block.sync
        def _(sp):
            sp.wait_ge(rows_made, 5 * RING + 3)

            def load(i, j):
                u = RING * i + j
                sp.dma_start(qs[j][0:STACK, :].bitcast(F32), q_stack[u]).then_inc(loaded[j], 16)
                sp.dma_start(ks[j][0:STACK, :].bitcast(F32), k_stack[u]).then_inc(loaded[j], 16)
                sp.dma_start(qs[j][64:66, :].bitcast(F32), zeros[0:2, :]).then_inc(loaded[j], 16)

            def maximum_rows(i, j, n):
                sp.wait_ge(slot_used, n + 1)
                sp.dma_start(neg_max[j].rearrange("s (t n) -> t s n", t=KT),
                             max_parts[j][:].bitcast(F32)).then_inc(max_stored[j], 16)
                sp.wait_ge(max_stored[j], 16 * (i + 1))
                sp.dma_start(qs[j][64:66, :].bitcast(F32), neg_max[j]).then_inc(max_loaded[j], 16)

            def step(i, last=False):
                for j in range(RING):
                    if not (last and j >= RING - AHEAD):
                        maximum_rows(i + (j + AHEAD) // RING, (j + AHEAD) % RING, first_slot(i, j)[0] + len(uses(i, j)) - 1)
                    if not last:
                        sp.wait_ge(st_made, KT * (RING * i + j + 1))
                        load(i + 1, j)

            for j in range(RING):
                load(0, j)
            for j in range(AHEAD):
                maximum_rows(0, j, MAXIMUM_SLOTS * (j + 1) - 1)
            step(0)
            with sp.Fori(1, UNITS // RING - 1) as i:
                step(i)
            step(UNITS // RING - 1, last=True)
            sp.wait_ge(out_done, 2 * UNITS)
            sp.dma_start(attn_out.rearrange("t p e -> p t e"), heads_out[:]).then_inc(attn_stored, 16)
            sp.wait_ge(attn_stored, 16)

        @block.tensor
        def _(pe):
            def free_bank(n):
                if not isinstance(n, int) or n >= 2:
                    pe.wait_ge(slot_used, n - 1)

            def piece(j, k, n, bank):
                t, k0, keys = PIECES[k]
                free_bank(n)
                diagonal = k0 + keys == (t + 1) * P
                mm = pe.matmul(ps_s[:, bank, 0:keys], qs[j][:, t * P:(t + 1) * P], ks[j][:, k0:k0 + keys],
                               start=True, stop=not diagonal)
                if diagonal:
                    mm = pe.matmul(ps_s[:, bank, keys - P:keys], ident_bf[:], causal_qk[:], start=False, stop=True)
                mm.then_inc(slot_made, 1)

            def turn_maxima(u, half, n, bank):
                pe.wait_ge(max_ready, u + 1)
                free_bank(n)
                pe.transpose(ps_s[0:KT, bank, 0:P], maxima[half][:, 0:KT], ident[:]).then_inc(slot_made, 1)

            def turn_output(u, half, c, n, bank):
                pe.wait_ge(sums_ready, u + 1)
                free_bank(n)
                for q in range(CT):
                    mm = pe.transpose(ps_s[:, bank, q * P:(q + 1) * P], sums[half][:, (CT * c + q) * P:(CT * c + q + 1) * P], ident[:])
                mm.then_inc(slot_made, 1)

            def scores_t(i, j, kt):
                n = KT * (RING * i + j) + kt
                if kt == 0:
                    pe.wait_ge(max_loaded[j], 16 * (i + 1))
                if not isinstance(n, int) or n >= 2:
                    pe.wait_ge(p_ready, n - 1)
                q0, half = kt * P, kt % 2
                for a in range(q0 // CHUNK, T // CHUNK):
                    lo, hi = max(q0, a * CHUNK), (a + 1) * CHUNK
                    diagonal = lo == q0
                    mm = pe.matmul(ps_t[:, half, lo:hi], ks[j][:, q0:q0 + P], qs[j][:, lo:hi], start=True, stop=not diagonal)
                    if diagonal:
                        mm = pe.matmul(ps_t[:, half, q0:q0 + P], ident_bf[:], causal_kq[:], start=False, stop=True)
                mm.then_inc(st_made, 1)

            def weighted(i, j, kt):
                u, r = RING * i + j, kt % 4
                g = (r + 2) % 4
                pe.wait_ge(p_ready, KT * u + kt + 1)
                if kt == 0:
                    pe.wait_ge(v_ready, u + 1)
                    pe.wait_ge(sums_ready, u)
                if kt < 4:
                    pe.matmul(ps_o[r * VW:(r + 1) * VW, 0, :], vs[j][:, kt, :], prob_a[:, r, 0:CHUNK], start=True, stop=True)
                    mm = pe.matmul(ps_o[g * VW:(g + 1) * VW, 1, :], vs[j][:, kt, :], prob_a[:, r, CHUNK:T], start=True, stop=False)
                else:
                    mm = pe.matmul(ps_o[g * VW:(g + 1) * VW, 1, r * P:CHUNK], vs[j][:, kt, :], prob_b[:, r, r * P:CHUNK],
                                   start=False, stop=True)
                mm.then_inc(pv_done, 1)

            def step(i):
                for j in range(RING):
                    u, listed = RING * i + j, uses(i, j)
                    n, bank = first_slot(i, j)
                    ja = (j + AHEAD) % RING
                    if any(kind == "piece" for _, kind, _ in listed):
                        pe.wait_ge(loaded[ja], LOADS * (i + (j + AHEAD) // RING + 1))
                    for kt in range(KT + 1):
                        if kt < KT:
                            scores_t(i, j, kt)
                        elif listed and listed[-1][1] == "maxima":
                            weighted(i, j, KT - 1)
                        for e, (at, kind, which) in enumerate(listed):
                            if at != kt:
                                continue
                            where = n + e, (bank + e) % 2
                            if kind == "piece":
                                piece(ja, which, *where)
                            elif kind == "output":
                                turn_output(u - 1, (j - 1) % 2, which, *where)
                            else:
                                turn_maxima(u + AHEAD, j % 2, *where)
                        if 1 <= kt < KT:
                            weighted(i, j, kt - 1)
                    if not (listed and listed[-1][1] == "maxima"):
                        weighted(i, j, KT - 1)

            pe.wait_ge(rows_made, 5 * RING + 3)
            for u in range(AHEAD):
                n = MAXIMUM_SLOTS * u
                pe.wait_ge(loaded[u], LOADS)
                for k in range(len(PIECES)):
                    piece(u, k, n + k, (n + k) % 2)
                n += len(PIECES)
                turn_maxima(u, u % 2, n, n % 2)
            step(0)
            with pe.Fori(1, UNITS // RING - 1) as i:
                step(i)
            step(UNITS // RING - 1)
            n = SLOTS * UNITS - 2
            for c in range(2):
                turn_output(UNITS - 1, (RING - 1) % 2, c, n + c, (n + c) % 2)

        @block.scalar
        def _(act):
            def exp_tile(u, kt):
                act.wait_ge(st_made, KT * u + kt + 1)
                before = KT * (u - 1) + kt + 1
                if not isinstance(u, int) or before > 0:
                    act.wait_ge(pv_done, before)
                r = kt % 4
                dst = prob_a[:, r, kt * P:T] if kt < 4 else prob_b[:, r, r * P:CHUNK]
                act.activation(dst, ps_t[:, kt % 2, kt * P:T], ACT.Exp).then_inc(p_ready, 1)

            def keep_sums(u, half):
                act.wait_ge(pv_done, KT * (u + 1))
                if not isinstance(u, int) or u >= 2:
                    act.wait_ge(out_done, 2 * (u - 1))
                act.activation(sums[half][:], ps_o[:].rearrange("p c n -> p (c n)"), ACT.Copy).then_inc(sums_ready, 1)

            def step(i):
                for j in range(RING):
                    u = RING * i + j
                    for kt in range(KT):
                        exp_tile(u, kt)
                        if kt == 0 and not (isinstance(u, int) and u == 0):
                            keep_sums(u - 1, (j - 1) % 2)

            act.wait_ge(rows_made, 5 * RING + 3)
            step(0)
            with act.Fori(1, UNITS // RING) as i:
                step(i)
            keep_sums(UNITS - 1, (RING - 1) % 2)

        @block.vector
        def _(dve):
            def piece(half, k, n, bank):
                t, k0, keys = PIECES[k]
                col = t if k0 == 0 else KT + t - 4
                dve.wait_ge(slot_made, n + 1)
                dve.tensor_reduce(maxima[half][:, col:col + 1], ps_s[:, bank, 0:keys], AX.X, ALU.max).then_inc(slot_used, 1)

            def finish_maxima(i, j, n, bank):
                u, half = RING * i + j, j % 2
                dve.wait_ge(slot_used, n)
                dve.tensor_tensor(maxima[half][:, 4:KT], maxima[half][:, 4:KT], maxima[half][:, KT:KT + 4], ALU.max).then_inc(max_ready, 1)
                dve.wait_ge(slot_made, n + 1)
                dve.wait_ge(max_stored[j], 16 * i)
                dve.tensor_scalar(max_parts[j][:, HI, :], ps_s[0:KT, bank, 0:P], -1.0, None, ALU.mult).then_inc(part_hi, 1)
                dve.wait_ge(part_hi, u + 1)
                dve.scalar_tensor_tensor(out=max_parts[j][:, LO, :], in0=ps_s[0:KT, bank, 0:P], scalar=-1.0,
                                         in1=max_parts[j][:, HI, :], op0=ALU.mult, op1=ALU.subtract).then_inc(slot_used, 1)

            def output(i, j, c, n, bank):
                dve.wait_ge(slot_made, n + 1)
                dve.tensor_reduce(folded[:, c, :, 0:DC + 1],
                                  ps_s[:, bank, :].rearrange("p (q g w) -> p q w g", q=CT, g=4)[:, :, 0:DC + 1, :],
                                  AX.X, ALU.add).then_inc(slot_used, 1)
                dve.wait_ge(slot_used, n + 1)
                dve.reciprocal(rsum[:, c, :], folded[:, c, :, DC]).then_inc(rsum_ready, 1)
                dve.wait_ge(rsum_ready, 2 * (RING * i + j) + c + 1)
                dve.tensor_tensor(heads_out[:, bass.ds((i // 4) * KT + CT * c, CT), bass.ds((i % 4) * 4 * DC + j * DC, DC)],
                                  folded[:, c, :, 0:DC], rsum[:, c, :].unsqueeze(2).broadcast_to([P, CT, DC]),
                                  ALU.mult).then_inc(out_done, 1)

            def step(i):
                for j in range(RING):
                    n, bank = first_slot(i, j)
                    for e, (_, kind, which) in enumerate(uses(i, j)):
                        where = n + e, (bank + e) % 2
                        if kind == "piece":
                            piece(j % 2, which, *where)
                        elif kind == "output":
                            output(i if j else i - 1, (j - 1) % RING, which, *where)
                        else:
                            finish_maxima(i + (j + AHEAD) // RING, (j + AHEAD) % RING, *where)

            for u in range(AHEAD):
                n = MAXIMUM_SLOTS * u
                for k in range(len(PIECES)):
                    piece(u, k, n + k, (n + k) % 2)
                n += len(PIECES)
                finish_maxima(0, u, n, n % 2)
            step(0)
            with dve.Fori(1, UNITS // RING - 1) as i:
                step(i)
            step(UNITS // RING - 1)
            n = SLOTS * UNITS - 2
            for c in range(2):
                output(UNITS // RING - 1, RING - 1, c, n + c, (n + c) % 2)


WINDOWS = TILES
PER_BATCH = WINDOWS // B
PAIRS = HL // 2
TURNS = 5


def local_layers(nc, ctx, tensor, psum, sem, layer_in, layer_mid, w_qkv, w_o, w1, w2, ln_gb, b1, b2,
                 qk_scale, trig, ident, ident_bf):
    class Arena:

        def __init__(self, name, dt, words):
            self.whole, self.words, self.at = tensor(ctx, name, [P, words], dt), words, 0

        def take(self, *shape):
            n = 1
            for s in shape:
                n *= s
            part = self.whole[:, self.at:self.at + n]
            self.at += n
            assert self.at <= self.words
            if len(shape) == 1:
                return part
            names = "abcd"[:len(shape)]
            return part.rearrange(f"p ({' '.join(names)}) -> p {' '.join(names)}", **dict(zip(names, shape)))

    plain, rounded = Arena("plain", F32, 10240), Arena("rounded", F32R, 9728)
    wqkv_s = tensor(ctx, "wqkv_s", [P, 2, KE, 3 * INNER], F32R)
    wo_s = tensor(ctx, "wo_s", [P, 2, PAIRS, E], F32R)
    w1_s = tensor(ctx, "w1_s", [P, 2, KE, 2 * HIDP], F32R)
    w2_s = tensor(ctx, "w2_s", [P, 2, HT, E], F32R)
    w_raw = tensor(ctx, "lw_raw", [P, KE * 3 * INNER + HT * E])
    gb = tensor(ctx, "gb", [P, 2, KE])
    b1_t = tensor(ctx, "b1_t", [P, 2 * HT])
    b2_t = tensor(ctx, "b2_t", [P, E])
    scale_t = tensor(ctx, "scale_t", [P, 4, DL])
    trig_t = tensor(ctx, "trig_t", [P, PER_BATCH, 4, DL])
    rotary = tensor(ctx, "rotary", [P, PER_BATCH, 2, 2, DL])
    own_mask = tensor(ctx, "own_mask", [P, P], BF16)
    before_mask = tensor(ctx, "before_mask", [P, P], BF16)
    mask_even = tensor(ctx, "mask_even", [P, 4, 2, 2, P], BF16)
    mask_odd = tensor(ctx, "mask_odd", [P, 2, 2, P], BF16)
    minus_half = tensor(ctx, "l_minus_half", [P, 2 * HL])

    hin = [plain.take(E) for _ in range(2)]
    res = [plain.take(E) for _ in range(2)]
    mid = [plain.take(E) for _ in range(2)]
    square = plain.take(2 * HL, DL)
    straight = plain.take(2, HL, DL)
    crossed = plain.take(2, HL, DL)
    unit = plain.take(2 * HL, DL)
    prob = [plain.take(2, 2 * P) for _ in range(2)]
    prob_t = [plain.take(2, 2, P) for _ in range(2)]
    norm2, rnorm = plain.take(2 * HL), plain.take(2 * HL)
    minus_max, row_sum, row_inv = plain.take(HL), plain.take(HL), plain.take(HL)
    values = tensor(ctx, "l_values", [P, 2, HL, DL])
    ht = [rounded.take(2, KE, P) for _ in range(2)]
    halves_q = rounded.take(HL, 2, DL)
    halves_k = rounded.take(HL, 3, DL)
    keys = rounded.take(2, HL, 2, P)
    queries = rounded.take(HL, P)
    heads = rounded.take(2, PAIRS, P)
    plain.at = rounded.at = 0
    fin = [plain.take(CT, E) for _ in range(2)]
    fres = [plain.take(CT, E) for _ in range(2)]
    fout = [plain.take(CT, E) for _ in range(2)]
    affine = plain.take(KE, CHUNK)
    gate = [plain.take(CHUNK) for _ in range(2)]
    hidden = [plain.take(CHUNK) for _ in range(2)]
    stats, mean_var = plain.take(CT, 6), plain.take(CT, 2)
    var_eps, rstd = plain.take(CT), plain.take(CT)
    ft = rounded.take(2, KE, CHUNK)
    hid = rounded.take(2, HT, CHUNK)

    ps_h = psum(ctx, "l_ps_h", [P, CHUNK])
    ps_qk = psum(ctx, "l_ps_qk", [P, 2, CHUNK])
    ps_v = psum(ctx, "l_ps_v", [P, CHUNK])
    ps_ta = psum(ctx, "l_ps_ta", [P, CHUNK])
    ps_td = psum(ctx, "l_ps_td", [P, CHUNK])
    ps_s = psum(ctx, "l_ps_s", [P, 2, CHUNK])
    ps_ft = ps_qk
    ps_out = ps_s
    ps_ga = [(ps_h, ps_v), (ps_ta, ps_td)]

    def sems(names):
        return [sem("l_" + n) for n in names.split()]

    const_made, masks_made, weights_in, weights_split, trig_in, trig_scaled = sems(
        "const_made masks_made weights_in weights_split trig_in trig_scaled")
    layer_stored, f_counted = sems("layer_stored f_counted")
    h_turned, h_hi, h_lo, qk_made, v_made, v_kept = sems("h_turned h_hi h_lo qk_made v_made v_kept")
    sq_ready, crossed_ready, norm_sum, norm_ready, r_ready, added, u_ready, u_hi, u_lo = sems(
        "sq_ready crossed_ready norm_sum norm_ready r_ready added u_ready u_hi u_lo")
    ta_made, ta_used, td_made, td_used = sems("ta_made ta_used td_made td_used")
    s_made, max_ready, exp_ready, inv_ready, p_ready = sems("s_made max_ready exp_ready inv_ready p_ready")
    o_part, o_made, o_hi, o_lo, y_made, y_ready = sems("o_part o_made o_hi o_lo y_made y_ready")
    f_stats, f_aggr, f_var, f_rstd, f_norm, f_turned, f_affine, f_hi, f_lo = sems(
        "f_stats f_aggr f_var f_rstd f_norm f_turned f_affine f_hi f_lo")
    g_made, a_made, gate_ready, hid_ready, hid_hi, hid_lo, f_made, f_res, f_ready = sems(
        "g_made a_made gate_ready hid_ready hid_hi hid_lo f_made f_res f_ready")
    h_in, res_in, mid_out, f_in, fres_in, f_out = ([sem(f"l_{n}{j}") for j in range(2)]
                                                   for n in ("h_in", "res_in", "mid_out", "f_in", "fres_in", "f_out"))
    WI, CI = WINDOWS // 2, CHUNKS // 2
    QKV_IN, MLP_IN = 4 * 16, 4 * 16

    def is_first(i, j=0):
        return isinstance(i, int) and i == 0 and j == 0

    with nc.Block() as block:

        @block.gpsimd
        def _(pool):
            pool.memset(own_mask[:], 0.0).then_inc(const_made, 1)
            pool.memset(before_mask[:], 0.0).then_inc(const_made, 1)
            pool.memset(minus_half[:], -0.5).then_inc(const_made, 1)
            pool.wait_ge(const_made, 3)
            pool.affine_select(out=own_mask[:], in_=own_mask[:], compare_op=ALU.is_ge, fill=NEG, base=0,
                               pattern=[[-1, P]], channel_multiplier=1).then_inc(const_made, 1)
            pool.affine_select(out=before_mask[:], in_=before_mask[:], compare_op=ALU.is_ge, fill=NEG, base=0,
                               pattern=[[1, P]], channel_multiplier=-1).then_inc(const_made, 1)

            def window(l, i, j):
                t = WINDOWS * l + 2 * i + j
                pool.wait_ge(crossed_ready, t + 1)
                if not is_first(i, j):
                    pool.wait_ge(u_hi, t)
                    pool.wait_ge(u_lo, t)
                pool.tensor_tensor(unit.rearrange("p (s h) d -> p s h d", s=2), straight, crossed, ALU.add).then_inc(added, 1)
                pool.wait_ge(norm_ready, t + 1)
                pool.tensor_tensor(rnorm, norm2, minus_half[:], ALU.pow).then_inc(r_ready, 1)
                pool.wait_ge(added, t + 1)
                pool.wait_ge(r_ready, t + 1)
                pool.tensor_tensor(unit, unit, rnorm.unsqueeze(2).broadcast_to([P, 2 * HL, DL]), ALU.mult).then_inc(u_ready, 1)
                pool.wait_ge(u_ready, t + 1)
                pool.wait_ge(u_hi, t + 1)
                if not is_first(i, j):
                    pool.wait_ge(ta_made, TURNS * t - 2)
                    pool.wait_ge(td_made, TURNS * t - 2)
                for s, halves in ((0, halves_q), (1, halves_k)):
                    ins = pool.tensor_tensor(halves[:, :, LO, :], unit[:, s * HL:(s + 1) * HL, :], halves[:, :, HI, :], ALU.subtract)
                ins.then_inc(u_lo, 1)

            def inverse_deviation(l, i, j):
                t = CHUNKS * l + 2 * i + j
                pool.wait_ge(f_var, t + 1)
                pool.tensor_tensor(rstd, var_eps, minus_half[:, 0:CT], ALU.pow).then_inc(f_rstd, 1)

            def input_lo(l, i, j):
                t = CHUNKS * l + 2 * i + j
                for f in range(KE):
                    pool.wait_ge(f_hi, KE * t + f + 1)
                    pool.tensor_tensor(ft[:, LO, f, :], affine[:, f, :], ft[:, HI, f, :], ALU.subtract).then_inc(f_lo, 1)

            def chunk(l, i, j, last=False):
                t = CHUNKS * l + 2 * i + j
                if not last:
                    inverse_deviation(l, i + j, 1 - j)
                pool.wait_ge(fres_in[j], 16 * (CI * l + i + 1))
                pool.tensor_tensor(fres[j], fres[j], b2_t[:].unsqueeze(1).broadcast_to([P, CT, E]), ALU.add).then_inc(f_res, 1)
                for k in range(HT):
                    pool.wait_ge(hid_hi, HT * t + k + 1)
                    pool.tensor_tensor(hid[:, LO, k, :], hidden[k % 2], hid[:, HI, k, :], ALU.subtract).then_inc(hid_lo, 1)
                if not last:
                    input_lo(l, i + j, 1 - j)

            with pool.Fori(0, DEPTH) as l:
                for j in range(2):
                    window(l, 0, j)
                with pool.Fori(1, WI) as i:
                    for j in range(2):
                        window(l, i, j)
                inverse_deviation(l, 0, 0)
                input_lo(l, 0, 0)
                with pool.Fori(0, CI - 1) as i:
                    for j in range(2):
                        chunk(l, i, j)
                chunk(l, CI - 1, 0)
                chunk(l, CI - 1, 1, last=True)

        @block.sync
        def _(sp):
            sp.dma_start(trig_t[:], trig).then_inc(trig_in, 16)
            sp.wait_ge(trig_in, 16)

            def tokens(scratch, l, i, j, shift, columns):
                row = 1 - shift + P * (2 * (i % 4) + j)
                return scratch[l, i // 4, bass.ds(row, P), columns]

            def chunk_tokens(scratch, l, i, j, shift, columns):
                row = 1 - shift + CHUNK * j
                return scratch[l, i, row:row + CHUNK, columns].rearrange("(q p) e -> p q e", p=P)

            def load_h(l, i, j):
                sp.dma_start(hin[j][:, 0:P], tokens(layer_in, l, i, j, 0, slice(0, P))).then_inc(h_in[j], 16)
                sp.dma_start(hin[j][:, P:E], tokens(layer_in, l, i, j, 1, slice(P, E))).then_inc(h_in[j], 16)

            def load_res(l, i, j):
                sp.dma_start(res[j], tokens(layer_in, l, i, j, 0, slice(0, E))).then_inc(res_in[j], 16)

            def window(l, i, j, last):
                t = WINDOWS * l + 2 * i + j
                if not last:
                    sp.wait_ge(h_turned, t + 1)
                    load_h(l, i + 1, j)
                sp.wait_ge(y_ready, t + 1)
                sp.dma_start(tokens(layer_mid, l, i, j, 0, slice(0, E)), mid[j]).then_inc(mid_out[j], 16)
                if not last:
                    load_res(l, i + 1, j)

            def load_f(l, i, j):
                sp.dma_start(fin[j][:, :, 0:P], chunk_tokens(layer_mid, l, i, j, 0, slice(0, P))).then_inc(f_in[j], 16)
                sp.dma_start(fin[j][:, :, P:E], chunk_tokens(layer_mid, l, i, j, 1, slice(P, E))).then_inc(f_in[j], 16)

            def load_fres(l, i, j):
                sp.dma_start(fres[j], chunk_tokens(layer_mid, l, i, j, 0, slice(0, E))).then_inc(fres_in[j], 16)

            def chunk(l, i, j, last):
                t = CHUNKS * l + 2 * i + j
                if not last:
                    sp.wait_ge(f_turned, KE * (t + 1))
                    load_f(l, i + 1, j)
                sp.wait_ge(f_ready, 2 * (t + 1))
                sp.dma_start(chunk_tokens(layer_in, l + 1, i, j, 0, slice(0, E)), fout[j]).then_inc(f_out[j], 16)
                if not last:
                    load_fres(l, i + 1, j)

            with sp.Fori(0, DEPTH) as l:
                sp.dma_start(w_raw[:, 0:KE * 3 * INNER].rearrange("p (k n) -> p k n", k=KE),
                             w_qkv[l].rearrange("(k p) n -> p k n", p=P)).then_inc(weights_in, 16)
                sp.dma_start(w_raw[:, KE * 3 * INNER:KE * 3 * INNER + PAIRS * E].rearrange("p (k n) -> p k n", k=PAIRS),
                             w_o[l].rearrange("(k p) n -> p k n", p=P)).then_inc(weights_in, 16)
                sp.dma_start(scale_t[:], qk_scale[l]).then_inc(weights_in, 16)
                sp.dma_start(gb[:], ln_gb[l]).then_inc(weights_in, 16)
                for j in range(2):
                    load_h(l, 0, j)
                    load_res(l, 0, j)
                sp.wait_ge(weights_split, 8 * l + 4)
                sp.dma_start(w_raw[:, 0:KE * 2 * HIDP].rearrange("p (k n) -> p k n", k=KE),
                             w1[l].rearrange("(k p) n -> p k n", p=P)).then_inc(weights_in, 16)
                sp.dma_start(w_raw[:, KE * 2 * HIDP:KE * 2 * HIDP + HT * E].rearrange("p (k n) -> p k n", k=HT),
                             w2[l].rearrange("(k p) n -> p k n", p=P)).then_inc(weights_in, 16)
                sp.dma_start(b1_t[:], b1[l]).then_inc(weights_in, 16)
                sp.dma_start(b2_t[:], b2[l]).then_inc(weights_in, 16)
                with sp.Fori(0, WI - 1) as i:
                    for j in range(2):
                        window(l, i, j, False)
                for j in range(2):
                    window(l, WI - 1, j, True)
                for j in range(2):
                    sp.wait_ge(mid_out[j], 16 * WI * (l + 1))
                for j in range(2):
                    load_f(l, 0, j)
                    load_fres(l, 0, j)
                with sp.Fori(0, CI - 1) as i:
                    for j in range(2):
                        chunk(l, i, j, False)
                for j in range(2):
                    chunk(l, CI - 1, j, True)
                for j in range(2):
                    sp.wait_ge(f_out[j], 16 * CI * (l + 1))
                sp.sem_inc(layer_stored, 1)

        @block.tensor
        def _(pe):
            def turn_h(l, i, j):
                t = WINDOWS * l + 2 * i + j
                pe.wait_ge(h_in[j], 32 * (WI * l + i + 1))
                if not (isinstance(i, int) and i == 0):
                    pe.wait_ge(o_lo, t - 1)
                for f in range(KE):
                    mm = pe.transpose(ps_h[:, f * P:(f + 1) * P], hin[j][:, f * P:(f + 1) * P], ident[:])
                mm.then_inc(h_turned, 1)

            def project_qk(l, i, j):
                t = WINDOWS * l + 2 * i + j
                pe.wait_ge(h_lo, t + 1)
                if not is_first(i, j):
                    pe.wait_ge(crossed_ready, t)
                    pe.wait_ge(sq_ready, t)
                for s in range(2):
                    mm = products(pe, ps_qk[:, s, :], lambda part, f: ht[j][:, part, f, :],
                                  lambda part, f: wqkv_s[:, part, f, s * INNER:(s + 1) * INNER], KE)
                mm.then_inc(qk_made, 1)

            def turned_tile(t, n, even):
                pe.wait_ge(ta_used if even else td_used, TURNS * t + n)
                return ps_ta if even else ps_td, ta_made if even else td_made

            def stacks(l, i, j):
                t = WINDOWS * l + 2 * i + j
                pe.wait_ge(u_lo, t + 1)
                for n, (halves, part) in enumerate(((halves_k, HI), (halves_k, LO), (halves_q, HI))):
                    for even in (True, False):
                        out, made = turned_tile(t, n, even)
                        for q in range(4):
                            rows = halves[:, q + (0 if even else 4), part:part + 2, :].rearrange("p s d -> p (s d)")
                            mm = pe.transpose(out[:, q * P:(q + 1) * P], rows.bitcast(F32), ident[:])
                        mm.then_inc(made, 1)

            def project_v(l, i, j):
                t = WINDOWS * l + 2 * i + j
                if not is_first(i, j):
                    pe.wait_ge(y_ready, t)
                products(pe, ps_v[:], lambda part, f: ht[j][:, part, f, :],
                         lambda part, f: wqkv_s[:, part, f, 2 * INNER:3 * INNER], KE).then_inc(v_made, 1)

            def scores(l, i, j, p):
                t = WINDOWS * l + 2 * i + j
                if p == 0:
                    pe.wait_ge(ta_used, TURNS * t + 3)
                    pe.wait_ge(td_used, TURNS * t + 3)
                if not is_first(i, j) or p >= 2:
                    pe.wait_ge(exp_ready, PAIRS * t + p - 1)
                masks = (mask_even[:, i % 4] if j == 0 else mask_odd[:]).rearrange("p h s n -> p (h s n)")
                pe.matmul(ps_s[:, p % 2, :], ident_bf[:], masks, start=True, stop=False)
                for h2 in range(2):
                    for part in (HI, LO):
                        mm = pe.matmul(ps_s[:, p % 2, h2 * 2 * P:(h2 + 1) * 2 * P], queries[:, 2 * p + h2, :],
                                       keys[:, part, 2 * p + h2].rearrange("p s n -> p (s n)"), start=False, stop=h2 == 1 and part == LO)
                mm.then_inc(s_made, 1)

            def turn_prob(l, i, j, p):
                t = WINDOWS * l + 2 * i + j
                out, made = turned_tile(t, 3 + p // 2, p % 2 == 0)
                pe.wait_ge(p_ready, PAIRS * t + p + 1)
                for h2 in range(2):
                    for s in range(2):
                        mm = pe.transpose(out[:, (2 * h2 + s) * P:(2 * h2 + s + 1) * P], prob[p % 2][:, h2, s * P:(s + 1) * P], ident[:])
                mm.then_inc(made, 1)

            def weighted(l, i, j, p):
                t = WINDOWS * l + 2 * i + j
                if p == 0:
                    pe.wait_ge(v_kept, t + 1)
                pe.wait_ge(ta_used if p % 2 == 0 else td_used, TURNS * t + 4 + p // 2)
                for s in range(2):
                    for h2 in range(2):
                        mm = pe.matmul(ps_h[h2 * DL:(h2 + 1) * DL, p * P:(p + 1) * P], values[:, s, 2 * p + h2, :],
                                       prob_t[p % 2][:, h2, s, :], start=s == 0, stop=s == 1)
                if p < 2:
                    mm.then_inc(o_part, 1)
                if p == PAIRS - 1:
                    mm.then_inc(o_made, 1)

            def project_out(l, i, j):
                t = WINDOWS * l + 2 * i + j
                pe.wait_ge(o_lo, t + 1)
                products(pe, ps_v[:, 0:E], lambda part, f: heads[:, part, f, :], lambda part, f: wo_s[:, part, f, :],
                         PAIRS).then_inc(y_made, 1)

            def step(l, i, j, last=False):
                if not last:
                    turn_h(l, i + j, 1 - j)
                stacks(l, i, j)
                if not last:
                    project_qk(l, i + j, 1 - j)
                project_v(l, i, j)
                scores(l, i, j, 0)
                scores(l, i, j, 1)
                for p in range(PAIRS):
                    turn_prob(l, i, j, p)
                    weighted(l, i, j, p)
                    if p + 2 < PAIRS:
                        scores(l, i, j, p + 2)
                project_out(l, i, j)

            def turn_f(l, i, j):
                t = CHUNKS * l + 2 * i + j
                pe.wait_ge(f_norm, t + 1)
                if not is_first(i, j):
                    pe.wait_ge(f_affine, KE * t)
                for f in range(KE):
                    for q in range(CT):
                        mm = pe.transpose(ps_ft[:, f, q * P:(q + 1) * P], fin[j][:, q, f * P:(f + 1) * P], ident[:])
                    mm.then_inc(f_turned, 1)

            def hidden_tiles(l, i, j):
                t = CHUNKS * l + 2 * i + j
                pe.wait_ge(f_lo, KE * (t + 1))
                for k in range(HT):
                    if not is_first(i, j) or k >= 2:
                        pe.wait_ge(hid_ready, HT * t + k - 1)
                    for which, made in ((1, g_made), (0, a_made)):
                        c0 = which * HIDP + k * P
                        products(pe, ps_ga[k % 2][1 - which][:], lambda part, f: w1_s[:, part, f, c0:c0 + P],
                                 lambda part, f: ft[:, part, f, :], KE).then_inc(made, 1)

            def project_hidden(l, i, j):
                t = CHUNKS * l + 2 * i + j
                pe.wait_ge(hid_lo, HT * (t + 1))
                for q in range(CT):
                    if q % 2 == 0 and not is_first(i, j):
                        pe.wait_ge(f_ready, 2 * t - 1 + q // 2)
                    mm = products(pe, ps_out[:, q // 2, (q % 2) * E:(q % 2 + 1) * E],
                                  lambda part, f: hid[:, part, f, q * P:(q + 1) * P], lambda part, f: w2_s[:, part, f, :], HT)
                    if q % 2:
                        mm.then_inc(f_made, 1)

            def chunk(l, i, j, last=False):
                hidden_tiles(l, i, j)
                if not last:
                    turn_f(l, i + j, 1 - j)
                project_hidden(l, i, j)

            pe.wait_ge(masks_made, 5)
            with pe.Fori(0, DEPTH) as l:
                pe.wait_ge(weights_split, 8 * l + 4)
                turn_h(l, 0, 0)
                project_qk(l, 0, 0)
                for j in range(2):
                    step(l, 0, j)
                with pe.Fori(1, WI - 1) as i:
                    for j in range(2):
                        step(l, i, j)
                step(l, WI - 1, 0)
                step(l, WI - 1, 1, last=True)
                pe.wait_ge(weights_split, 8 * l + 8)
                turn_f(l, 0, 0)
                for j in range(2):
                    chunk(l, 0, j)
                with pe.Fori(1, CI - 1) as i:
                    for j in range(2):
                        chunk(l, i, j)
                chunk(l, CI - 1, 0)
                chunk(l, CI - 1, 1, last=True)

        @block.scalar
        def _(act):
            def project(l, i, j):
                t = WINDOWS * l + 2 * i + j
                act.wait_ge(h_turned, t + 1)
                if not (isinstance(i, int) and i == 0):
                    act.wait_ge(v_made, t - 1)
                act.activation(ht[j][:, HI].rearrange("p f n -> p (f n)"), ps_h[:, 0:E], ACT.Copy).then_inc(h_hi, 1)

            def squares(l, i, j):
                t = WINDOWS * l + 2 * i + j
                act.wait_ge(qk_made, t + 1)
                if not is_first(i, j):
                    act.wait_ge(norm_sum, t)
                act.activation(square.rearrange("p h d -> p (h d)"), ps_qk[:].rearrange("p s n -> p (s n)"), ACT.Square).then_inc(sq_ready, 1)

            def unit_hi(l, i, j):
                t = WINDOWS * l + 2 * i + j
                act.wait_ge(u_ready, t + 1)
                if not is_first(i, j):
                    act.wait_ge(ta_made, TURNS * t - 2)
                    act.wait_ge(td_made, TURNS * t - 2)
                act.activation(halves_q[:, :, HI, :], unit[:, 0:HL, :], ACT.Copy)
                act.activation(halves_k[:, :, 0:3:2, :], unit[:, HL:2 * HL, :].unsqueeze(2).broadcast_to([P, HL, 2, DL]),
                               ACT.Copy).then_inc(u_hi, 1)

            def stack(l, i, j, n):
                t = WINDOWS * l + 2 * i + j
                act.wait_ge(ta_made, TURNS * t + n + 1)
                if n == 0 and not is_first(i, j):
                    act.wait_ge(s_made, PAIRS * t)
                out = queries[:, 0:4, :] if n == 2 else keys[:, n, 0:4, j, :]
                act.activation(out, ps_ta[:].rearrange("p (h n) -> p h n", h=4), ACT.Copy).then_inc(ta_used, 1)

            def step(l, i, j, last=False):
                t = WINDOWS * l + 2 * i + j
                if not last:
                    project(l, i + j, 1 - j)
                for n in range(3):
                    stack(l, i, j, n)
                if not last:
                    squares(l, i + j, 1 - j)
                act.wait_ge(v_made, t + 1)
                if not is_first(i, j):
                    act.wait_ge(o_made, t)
                act.activation(values[:, j].rearrange("p h d -> p (h d)"), ps_v[:], ACT.Copy).then_inc(v_kept, 1)
                for p in range(PAIRS):
                    act.wait_ge(max_ready, PAIRS * t + p + 1)
                    if p >= 2:
                        act.wait_ge((ta_made, td_made)[p % 2], TURNS * t + 4)
                    elif not is_first(i, j):
                        act.wait_ge((ta_made, td_made)[p % 2], TURNS * t)
                    for h2 in range(2):
                        h = 2 * p + h2
                        ins = act.activation(prob[p % 2][:, h2, :], ps_s[:, p % 2, h2 * 2 * P:(h2 + 1) * 2 * P], ACT.Exp,
                                             bias=minus_max[:, h:h + 1], accum_out=row_sum[:, h:h + 1])
                    ins.then_inc(exp_ready, 1)
                    if p in (1, 3):
                        act.wait_ge(ta_made, TURNS * t + 4 + p // 2)
                        if p == 1 and not is_first(i, j):
                            act.wait_ge(o_made, t)
                        if p == 3:
                            act.wait_ge(o_part, 2 * t + 1)
                        act.activation(prob_t[0].rearrange("p h s n -> p (h s n)"), ps_ta[:], ACT.Copy).then_inc(ta_used, 1)
                    if p == 2 and not last:
                        unit_hi(l, i + j, 1 - j)
                act.wait_ge(o_made, t + 1)
                if not is_first(i, j):
                    act.wait_ge(y_made, t)
                act.activation(heads[:, HI].rearrange("p f n -> p (f n)"), ps_h[:], ACT.Copy).then_inc(o_hi, 1)

            def affine_tiles(l, i, j):
                t = CHUNKS * l + 2 * i + j
                for f in range(KE):
                    act.wait_ge(f_turned, KE * t + f + 1)
                    if not is_first(i, j):
                        act.wait_ge(f_lo, KE * t)
                    act.activation(affine[:, f, :], ps_ft[:, f, :], ACT.Identity, bias=gb[:, 1, f:f + 1],
                                   scale=gb[:, 0, f:f + 1]).then_inc(f_affine, 1)

            def hidden_hi(t, k, first):
                act.wait_ge(hid_ready, HT * t + k + 1)
                if k == 0 and not first:
                    act.wait_ge(f_made, 2 * t)
                act.activation(hid[:, HI, k, :], hidden[k % 2], ACT.Copy).then_inc(hid_hi, 1)

            def chunk(l, i, j, last=False):
                t = CHUNKS * l + 2 * i + j
                for k in range(HT):
                    act.wait_ge(g_made, HT * t + k + 1)
                    if not is_first(i, j) or k >= 2:
                        act.wait_ge(hid_ready, HT * t + k - 1)
                    act.activation(gate[k % 2], ps_ga[k % 2][0][:], ACT.Gelu, bias=b1_t[:, HT + k:HT + k + 1]).then_inc(gate_ready, 1)
                    if k:
                        hidden_hi(t, k - 1, is_first(i, j))
                hidden_hi(t, HT - 1, is_first(i, j))
                if not last:
                    affine_tiles(l, i + j, 1 - j)

            with act.Fori(0, DEPTH) as l:
                project(l, 0, 0)
                squares(l, 0, 0)
                unit_hi(l, 0, 0)
                for j in range(2):
                    step(l, 0, j)
                with act.Fori(1, WI - 1) as i:
                    for j in range(2):
                        step(l, i, j)
                step(l, WI - 1, 0)
                step(l, WI - 1, 1, last=True)
                affine_tiles(l, 0, 0)
                for j in range(2):
                    chunk(l, 0, j)
                with act.Fori(1, CI - 1) as i:
                    for j in range(2):
                        chunk(l, i, j)
                chunk(l, CI - 1, 0)
                chunk(l, CI - 1, 1, last=True)

        @block.vector
        def _(dve):
            def split_weights(l, base, parts):
                at = 0
                for n, (dst, k, cols) in enumerate(parts):
                    raw = w_raw[:, at:at + k * cols].rearrange("p (k n) -> p k n", k=k)
                    at += k * cols
                    dve.tensor_copy(dst[:, HI], raw).then_inc(weights_split, 1)
                    dve.wait_ge(weights_split, 8 * l + base + 2 * n + 1)
                    dve.tensor_tensor(dst[:, LO], raw, dst[:, HI], ALU.subtract).then_inc(weights_split, 1)

            def project(l, i, j):
                t = WINDOWS * l + 2 * i + j
                dve.wait_ge(h_hi, t + 1)
                dve.tensor_tensor(ht[j][:, LO].rearrange("p f n -> p (f n)"), ps_h[:, 0:E],
                                  ht[j][:, HI].rearrange("p f n -> p (f n)"), ALU.subtract).then_inc(h_lo, 1)

            def rotate(l, i, j):
                t = WINDOWS * l + 2 * i + j
                w = 2 * (i % 4) + j
                qk = ps_qk[:].rearrange("p s (h d) -> p s h d", h=HL)
                dve.wait_ge(sq_ready, t + 1)
                if not is_first(i, j):
                    dve.wait_ge(added, t)
                half = DL // 2
                cos = rotary[:, w, :, 0, :].unsqueeze(2).broadcast_to([P, 2, HL, DL])
                dve.tensor_tensor(straight, qk, cos, ALU.mult)
                for a in range(2):
                    mine, other = slice(a * half, (a + 1) * half), slice((1 - a) * half, (2 - a) * half)
                    sin = rotary[:, w, :, 1, mine].unsqueeze(2).broadcast_to([P, 2, HL, half])
                    ins = dve.tensor_tensor(crossed[:, :, :, mine], qk[:, :, :, other], sin, ALU.mult)
                ins.then_inc(crossed_ready, 1)
                if not is_first(i, j):
                    dve.wait_ge(r_ready, t)
                dve.tensor_reduce(norm2, square, AX.X, ALU.add).then_inc(norm_sum, 1)
                dve.wait_ge(norm_sum, t + 1)
                dve.tensor_scalar(norm2, norm2, 1e-24, None, ALU.max).then_inc(norm_ready, 1)

            def stack(l, i, j, n):
                t = WINDOWS * l + 2 * i + j
                dve.wait_ge(td_made, TURNS * t + n + 1)
                if n == 0 and not is_first(i, j):
                    dve.wait_ge(s_made, PAIRS * t)
                out = queries[:, 4:8, :] if n == 2 else keys[:, n, 4:8, j, :]
                dve.tensor_copy(out, ps_td[:].rearrange("p (h n) -> p h n", h=4)).then_inc(td_used, 1)

            def maxima(t, p):
                dve.wait_ge(s_made, PAIRS * t + p + 1)
                dve.tensor_reduce(minus_max[:, 2 * p:2 * p + 2], ps_s[:, p % 2, :].rearrange("p (h n) -> p h n", h=2),
                                  AX.X, ALU.max, negate=True).then_inc(max_ready, 1)

            def normalise(t, p):
                dve.wait_ge(exp_ready, PAIRS * t + p + 1)
                dve.reciprocal(row_inv[:, 2 * p:2 * p + 2], row_sum[:, 2 * p:2 * p + 2]).then_inc(inv_ready, 1)
                dve.wait_ge(inv_ready, PAIRS * t + p + 1)
                for h2 in range(2):
                    h = 2 * p + h2
                    ins = dve.tensor_scalar(prob[p % 2][:, h2, :], prob[p % 2][:, h2, :], row_inv[:, h:h + 1], None, ALU.mult)
                ins.then_inc(p_ready, 1)

            def turned_prob(t, p, skip):
                dve.wait_ge(td_made, TURNS * t + 4 + p // 2)
                if p == 1 and not skip:
                    dve.wait_ge(o_made, t)
                if p == 3:
                    dve.wait_ge(o_part, 2 * t + 2)
                dve.tensor_copy(prob_t[1].rearrange("p h s n -> p (h s n)"), ps_td[:]).then_inc(td_used, 1)

            def step(l, i, j, last=False):
                t = WINDOWS * l + 2 * i + j
                if not last:
                    project(l, i + j, 1 - j)
                for n in range(3):
                    stack(l, i, j, n)
                if not last:
                    rotate(l, i + j, 1 - j)
                maxima(t, 0)
                maxima(t, 1)
                normalise(t, 0)
                normalise(t, 1)
                maxima(t, 2)
                turned_prob(t, 1, is_first(i, j))
                maxima(t, 3)
                normalise(t, 2)
                normalise(t, 3)
                turned_prob(t, 3, is_first(i, j))
                dve.wait_ge(o_hi, t + 1)
                dve.tensor_tensor(heads[:, LO].rearrange("p f n -> p (f n)"), ps_h[:],
                                  heads[:, HI].rearrange("p f n -> p (f n)"), ALU.subtract).then_inc(o_lo, 1)
                dve.wait_ge(y_made, t + 1)
                dve.wait_ge(res_in[j], 16 * (WI * l + i + 1))
                if not (isinstance(i, int) and i == 0):
                    dve.wait_ge(mid_out[j], 16 * (WI * l + i))
                dve.tensor_tensor(mid[j], ps_v[:, 0:E], res[j], ALU.add).then_inc(y_ready, 1)

            def layer_norm(l, i, j):
                t = CHUNKS * l + 2 * i + j
                dve.wait_ge(f_in[j], 32 * (CI * l + i + 1))
                for q in range(CT):
                    dve.bn_stats(stats[:, q, :], fin[j][:, q, :]).then_inc(f_stats, 1)
                dve.wait_ge(f_stats, CT * (t + 1))
                dve.sem_inc(f_counted, 1)
                for q in range(CT):
                    dve.bn_aggr(mean_var[:, q, :], stats[:, q, :]).then_inc(f_aggr, 1)
                dve.wait_ge(f_aggr, CT * (t + 1))
                dve.tensor_scalar(var_eps, mean_var[:, :, 1], EPS, None, ALU.add).then_inc(f_var, 1)
                dve.wait_ge(f_rstd, t + 1)
                for q in range(CT):
                    ins = dve.tensor_scalar(fin[j][:, q, :], fin[j][:, q, :], mean_var[:, q, 0:1], rstd[:, q:q + 1],
                                            ALU.subtract, ALU.mult)
                ins.then_inc(f_norm, 1)

            def split_input(l, i, j):
                t = CHUNKS * l + 2 * i + j
                for f in range(KE):
                    dve.wait_ge(f_affine, KE * t + f + 1)
                    dve.tensor_copy(ft[:, HI, f, :], affine[:, f, :]).then_inc(f_hi, 1)

            def chunk(l, i, j, last=False):
                t = CHUNKS * l + 2 * i + j
                if not last:
                    layer_norm(l, i + j, 1 - j)
                for k in range(HT):
                    dve.wait_ge(a_made, HT * t + k + 1)
                    dve.wait_ge(gate_ready, HT * t + k + 1)
                    if not is_first(i, j) or k >= 2:
                        dve.wait_ge(hid_lo, HT * t + k - 1)
                    dve.scalar_tensor_tensor(out=hidden[k % 2], in0=ps_ga[k % 2][1][:], scalar=b1_t[:, k:k + 1],
                                             in1=gate[k % 2], op0=ALU.add, op1=ALU.mult).then_inc(hid_ready, 1)
                if not last:
                    split_input(l, i + j, 1 - j)
                dve.wait_ge(f_res, t + 1)
                if not (isinstance(i, int) and i == 0):
                    dve.wait_ge(f_out[j], 16 * (CI * l + i))
                for half in range(2):
                    dve.wait_ge(f_made, 2 * t + half + 1)
                    dve.tensor_tensor(fout[j][:, 2 * half:2 * half + 2, :], ps_out[:, half, :].rearrange("p (q e) -> p q e", q=2),
                                      fres[j][:, 2 * half:2 * half + 2, :], ALU.add).then_inc(f_ready, 1)

            dve.wait_ge(const_made, 5)
            both = lambda tile: tile[:].unsqueeze(1).broadcast_to([P, 2, P])
            dve.memset(mask_even[:, 0, :, 1, :], NEG).then_inc(masks_made, 1)
            for g in range(4):
                dve.tensor_copy(mask_even[:, g, :, 0, :], both(own_mask))
                if g:
                    dve.tensor_copy(mask_even[:, g, :, 1, :], both(before_mask))
            dve.tensor_copy(mask_odd[:, :, 0, :], both(before_mask)).then_inc(masks_made, 1)
            dve.tensor_copy(mask_odd[:, :, 1, :], both(own_mask)).then_inc(masks_made, 1)
            dve.memset(keys[:, :, :, 1, :].bitcast(F32), 0.0).then_inc(masks_made, 1)
            dve.memset(values[:, 1], 0.0).then_inc(masks_made, 1)
            dve.wait_ge(trig_in, 16)
            with dve.Fori(0, DEPTH) as l:
                dve.wait_ge(weights_in, (QKV_IN + MLP_IN) * l + QKV_IN)
                split_weights(l, 0, ((wqkv_s, KE, 3 * INNER), (wo_s, PAIRS, E)))
                dve.tensor_tensor(rotary[:].rearrange("p w s c d -> p w (s c) d"), trig_t[:],
                                  scale_t[:].unsqueeze(1).broadcast_to([P, PER_BATCH, 4, DL]), ALU.mult).then_inc(trig_scaled, 1)
                dve.wait_ge(trig_scaled, l + 1)
                project(l, 0, 0)
                rotate(l, 0, 0)
                for j in range(2):
                    step(l, 0, j)
                with dve.Fori(1, WI - 1) as i:
                    for j in range(2):
                        step(l, i, j)
                step(l, WI - 1, 0)
                step(l, WI - 1, 1, last=True)
                dve.wait_ge(weights_in, (QKV_IN + MLP_IN) * (l + 1))
                split_weights(l, 4, ((w1_s, KE, 2 * HIDP), (w2_s, HT, E)))
                layer_norm(l, 0, 0)
                split_input(l, 0, 0)
                for j in range(2):
                    chunk(l, 0, j)
                with dve.Fori(1, CI - 1) as i:
                    for j in range(2):
                        chunk(l, i, j)
                chunk(l, CI - 1, 0)
                chunk(l, CI - 1, 1, last=True)


def finish(nc, ctx, tensor, psum, sem, x, layer_in, attn_out, ident, wout_s, out):
    ain = [tensor(ctx, f"ain{j}", [P, CT, E]) for j in range(2)]
    xres = [tensor(ctx, f"xres{j}", [P, CT, E]) for j in range(2)]
    lres = [tensor(ctx, f"lres{j}", [P, CT, E]) for j in range(2)]
    at = [tensor(ctx, f"at{j}", [P, 2, KE, CHUNK], F32R) for j in range(2)]
    ps_at = psum(ctx, "ps_at", [P, KE, CHUNK])
    ps_y = psum(ctx, "ps_y", [P, 2, 2, E])
    a_in, r_in, stored = ([sem(f"o_{n}{j}") for j in range(2)] for n in ("a_in", "r_in", "stored"))
    turned, hi, lo, added, made, ready = (sem("o_" + n) for n in ("turned", "hi", "lo", "added", "made", "ready"))

    with nc.Block() as block:

        @block.sync
        def _(sp):
            def load(i, j):
                rows = slice(j * CHUNK, (j + 1) * CHUNK)
                sp.dma_start(ain[j][:], attn_out[bass.ds(2 * CT * i + CT * j, CT)].rearrange("q p e -> p q e")).then_inc(a_in[j], 16)
                sp.dma_start(xres[j][:], x[i, rows, :].rearrange("(q p) e -> p q e", p=P)).then_inc(r_in[j], 16)
                sp.dma_start(lres[j][:], layer_in[DEPTH, i, 1 + j * CHUNK:1 + (j + 1) * CHUNK, :]
                             .rearrange("(q p) e -> p q e", p=P)).then_inc(r_in[j], 16)

            def store(i, j):
                sp.wait_ge(ready, 2 * (2 * i + j + 1))
                sp.dma_start(out[i, j * CHUNK:(j + 1) * CHUNK, :].rearrange("(q p) e -> p q e", p=P), xres[j][:]).then_inc(stored[j], 16)

            for j in range(2):
                load(0, j)
            with sp.Fori(0, B - 1) as i:
                for j in range(2):
                    store(i, j)
                    sp.wait_ge(stored[j], 16 * (i + 1))
                    load(i + 1, j)
            for j in range(2):
                store(B - 1, j)
            for j in range(2):
                sp.wait_ge(stored[j], 16 * B)

        @block.gpsimd
        def _(pool):
            with pool.Fori(0, B) as i:
                for j in range(2):
                    pool.wait_ge(r_in[j], 32 * (i + 1))
                    pool.tensor_tensor(xres[j][:], xres[j][:], lres[j][:], ALU.add).then_inc(added, 1)

        @block.tensor
        def _(pe):
            with pe.Fori(0, B) as i:
                for j in range(2):
                    c = 2 * i + j
                    pe.wait_ge(a_in[j], 16 * (i + 1))
                    pe.wait_ge(lo, KE * c)
                    for f in range(KE):
                        for q in range(CT):
                            mm = pe.transpose(ps_at[:, f, q * P:(q + 1) * P], ain[j][:, q, f * P:(f + 1) * P], ident[:])
                        mm.then_inc(turned, 1)
                    pe.wait_ge(lo, KE * (c + 1))
                    pe.wait_ge(ready, 2 * c)
                    for q in range(CT):
                        mm = products(pe, ps_y[:, q // 2, q % 2, :], lambda part, f: at[j][:, part, f, q * P:(q + 1) * P],
                                      lambda part, f: wout_s[:, part, f, :], KE)
                        if q % 2:
                            mm.then_inc(made, 1)

        @block.scalar
        def _(act):
            with act.Fori(0, B) as i:
                for j in range(2):
                    c = 2 * i + j
                    for f in range(KE):
                        act.wait_ge(turned, KE * c + f + 1)
                        act.wait_ge(made, 4 * i)
                        act.activation(at[j][:, HI, f, :], ps_at[:, f, :], ACT.Copy).then_inc(hi, 1)

        @block.vector
        def _(dve):
            with dve.Fori(0, B) as i:
                for j in range(2):
                    c = 2 * i + j
                    for f in range(KE):
                        dve.wait_ge(hi, KE * c + f + 1)
                        dve.tensor_tensor(at[j][:, LO, f, :], ps_at[:, f, :], at[j][:, HI, f, :], ALU.subtract).then_inc(lo, 1)
                    dve.wait_ge(added, c + 1)
                    for half in range(2):
                        dve.wait_ge(made, 2 * c + half + 1)
                        dve.tensor_tensor(xres[j][:, 2 * half:2 * half + 2, :], ps_y[:, half], xres[j][:, 2 * half:2 * half + 2, :],
                                          ALU.add).then_inc(ready, 1)


def rotary_constants():
    import numpy as np
    half_idx = np.arange(0, DL, 2, dtype=np.float32)
    inv_freq = 1.0 / np.float32(10000.0) ** (half_idx / np.float32(DL))
    t = np.arange(T, dtype=np.float32)
    freqs = t[:, None] * inv_freq[None, :]
    freqs = np.concatenate([freqs, freqs], axis=-1)
    base = (half_idx + np.float32(0.4 * DL)) / np.float32(1.4 * DL)
    power = (t - T // 2) / np.float32(P // 2)
    scale = base[None, :] ** power[:, None]
    scale = np.concatenate([scale, scale], axis=-1)
    sign = np.where(np.arange(DL) < DL // 2, np.float32(-1), np.float32(1))
    cos, sin = np.cos(freqs), np.sin(freqs) * sign
    tables = np.stack([cos * scale * 8, sin * scale * 8, cos / scale, sin / scale], axis=1).astype(np.float32)
    return np.ascontiguousarray(tables.reshape(PER_BATCH, P, 4, DL).transpose(1, 0, 2, 3))


def kernel(L0_attn_query, L0_attn_key, L0_attn_value, L0_attn_in_proj_weight, L0_attn_out_proj_weight,
           L0_ffn_wqkv, L0_ffn_q_scale, L0_ffn_k_scale, L0_ffn_wo, L0_ffn_ln_g, L0_ffn_ln_b,
           L0_ffn_w1, L0_ffn_b1, L0_ffn_w2, L0_ffn_b2):
    import numpy as np
    import concourse.bacc as bacc
    from concourse.bass_utils import run_bass_kernel_spmd

    def padded(a, axis):
        widths = [(0, 0)] * a.ndim
        widths[axis] = (0, HIDP - HID)
        return np.pad(a, widths)

    def on_partitions(a, tiles):
        return a.reshape(DEPTH, tiles, P).transpose(0, 2, 1)

    def repeated(a):
        return np.broadcast_to(a[:, None], (DEPTH, P) + a.shape[1:])

    w1, b1 = np.asarray(L0_ffn_w1), np.asarray(L0_ffn_b1)
    qs, ks = np.asarray(L0_ffn_q_scale), np.asarray(L0_ffn_k_scale)
    swap = np.r_[DL // 2:DL, 0:DL // 2]
    arrays = {
        "x": np.asarray(L0_attn_query),
        "w_in": np.asarray(L0_attn_in_proj_weight).T,
        "w_out": np.asarray(L0_attn_out_proj_weight).T,
        "w_qkv": np.asarray(L0_ffn_wqkv),
        "w_o": np.asarray(L0_ffn_wo),
        "w1": np.concatenate([padded(w1[..., :HID], 2), padded(w1[..., HID:], 2)], axis=2),
        "w2": padded(np.asarray(L0_ffn_w2), 1),
        "ln_gb": np.stack([on_partitions(np.asarray(L0_ffn_ln_g), KE), on_partitions(np.asarray(L0_ffn_ln_b), KE)], axis=2),
        "b1": np.concatenate([on_partitions(padded(b1[:, :HID], 1), HT), on_partitions(padded(b1[:, HID:], 1), HT)], axis=2),
        "b2": repeated(np.asarray(L0_ffn_b2)),
        "qk_scale": repeated(np.stack([qs, qs[:, swap], ks, ks[:, swap]], axis=1)),
        "trig": rotary_constants(),
    }
    nc = bacc.Bacc("TRN2", target_bir_lowering=False, num_devices=1)
    aps = {}
    for name, a in arrays.items():
        arrays[name] = np.ascontiguousarray(a)
        aps[name] = nc.dram_tensor("in_" + name, a.shape, mybir.dt.from_np(a.dtype), kind="ExternalInput").ap()
    aps["out"] = nc.dram_tensor("out_0", (B, T, E), F32, kind="ExternalOutput").ap()
    build(nc, **aps)
    r = run_bass_kernel_spmd(nc, [{"in_" + name: a for name, a in arrays.items()}], core_ids=[0])
    return r.results[0]["out_0"]
```

```python
from contextlib import ExitStack

import concourse.bass as bass
from concourse import mybir

F32 = mybir.dt.float32
F32R = mybir.dt.float32r
BF16 = mybir.dt.bfloat16
ALU = mybir.AluOpType
ACT = mybir.ActivationFunctionType
AX = mybir.AxisListType

P = 128
B, T, E = 4, 1024, 256
TILES = B * T // P
CHUNK = 512
CT = CHUNK // P
CHUNKS = B * T // CHUNK
KE = E // P
EPS = 1e-5
NEG = -3e38

HC, DC = 16, 16
UNITS = B * HC
KT = T // P
STACK = 4 * DC
KROWS = 96
VW = 32

DEPTH, HL, DL = 2, 8, 64
INNER = HL * DL
HID = 682
HT = 6
HIDP = HT * P
HI, LO = 0, 1
PRODUCTS = ((HI, HI), (HI, LO), (LO, HI))


class Chain:

    def __init__(self, engine, sem, base=0):
        self.engine, self.sem, self.base, self.n = engine, sem, base, 0

    def add(self, instruction):
        instruction.then_inc(self.sem, 1)
        self.n += 1

    def wait(self):
        self.engine.wait_ge(self.sem, self.base + self.n)


def build(nc, x, w_in, w_out, w_qkv, w_o, w1, w2, ln_gb, b1, b2, qk_scale, trig, out):
    layer_in = nc.dram_tensor("layer_in", (DEPTH + 1, B, 1 + T, E), F32, kind="Internal").ap()
    layer_mid = nc.dram_tensor("layer_mid", (DEPTH, B, 1 + T, E), F32, kind="Internal").ap()
    q_stack = nc.dram_tensor("q_stack", (UNITS, STACK, T), F32, kind="Internal").ap()
    k_stack = nc.dram_tensor("k_stack", (UNITS, STACK, T), F32, kind="Internal").ap()
    neg_max = nc.dram_tensor("neg_max", (4, 2, T), F32, kind="Internal").ap()
    attn_out = nc.dram_tensor("attn_out", (TILES, P, E), F32, kind="Internal").ap()

    with ExitStack() as top:
        def tensor(ctx, name, shape, dt=F32):
            return ctx.enter_context(nc.sbuf_tensor(name, shape, dt))

        def psum(ctx, name, shape):
            return ctx.enter_context(nc.psum_tensor(name, shape, F32))

        def sem(name):
            return top.enter_context(nc.semaphore(name))

        ident = tensor(top, "ident", [P, P])
        ident_bf = tensor(top, "ident_bf", [P, P], BF16)
        wout_s = tensor(top, "wout_s", [P, 2, KE, E], F32R)

        with ExitStack() as ctx:
            values = tensor(ctx, "values", [P, UNITS, KT, DC])
            zeros = tensor(ctx, "zeros", [12, T])
            causal_qk = tensor(ctx, "causal_qk", [P, P], BF16)
            causal_kq = tensor(ctx, "causal_kq", [P, P], BF16)
            with ExitStack() as inner:
                win_s = tensor(inner, "win_s", [P, 2, KE, 3 * E], F32R)
                project(nc, inner, tensor, psum, sem, x, w_in, w_out, layer_in, layer_mid, q_stack, k_stack,
                        ident, ident_bf, causal_qk, causal_kq, zeros, win_s, wout_s, values)
            with ExitStack() as inner:
                attend(nc, inner, tensor, psum, sem, q_stack, k_stack, neg_max, attn_out,
                       ident, ident_bf, causal_qk, causal_kq, zeros, values)
        with ExitStack() as ctx:
            local_layers(nc, ctx, tensor, psum, sem, layer_in, layer_mid, w_qkv, w_o, w1, w2, ln_gb, b1, b2,
                         qk_scale, trig, ident, ident_bf)
        with ExitStack() as ctx:
            finish(nc, ctx, tensor, psum, sem, x, layer_in, attn_out, ident, wout_s, out)


def project(nc, ctx, tensor, psum, sem, x, w_in, w_out, layer_in, layer_mid, q_stack, k_stack,
            ident, ident_bf, causal_qk, causal_kq, zeros, win_s, wout_s, values):
    w_raw = tensor(ctx, "w_raw", [P, KE, 4 * E])
    xin = [tensor(ctx, f"xin{j}", [P, CT, E]) for j in range(2)]
    xn = [tensor(ctx, f"xn{j}", [P, CT, E]) for j in range(2)]
    stats = tensor(ctx, "stats", [P, CT, 6])
    mean_var = tensor(ctx, "mean_var", [P, CT, 2])
    var_eps = tensor(ctx, "var_eps", [P, CT])
    rstd = tensor(ctx, "rstd", [P, CT])
    minus_half = tensor(ctx, "minus_half", [P, CT])
    xt = [tensor(ctx, f"xt{j}", [P, 2, KE, CHUNK], F32R) for j in range(2)]
    qk = [tensor(ctx, f"qk{j}", [P, 2, 4, CHUNK], F32R) for j in range(2)]
    ps_xt = psum(ctx, "ps_xt", [P, KE, CHUNK])
    ps_qk = psum(ctx, "ps_qk", [P, 4, CHUNK])
    ps_v = psum(ctx, "ps_v", [P, 2, 2, E])

    const_made = sem("p_const_made")
    w_loaded = sem("p_w_loaded")
    zero_rows = sem("p_zero_rows")
    w_split = sem("p_w_split")
    x_loaded = [sem(f"p_x_loaded{j}") for j in range(2)]
    dve_own = sem("p_dve_own")
    counted = sem("p_counted")
    var_ready = sem("p_var_ready")
    rstd_ready = sem("p_rstd_ready")
    xn_ready = sem("p_xn_ready")
    xn_stored = [sem(f"p_xn_stored{j}") for j in range(2)]
    xt_made = sem("p_xt_made")
    xt_hi = sem("p_xt_hi")
    xt_lo = sem("p_xt_lo")
    qk_made = sem("p_qk_made")
    qk_hi = sem("p_qk_hi")
    qk_lo = sem("p_qk_lo")
    v_made = sem("p_v_made")
    v_kept = sem("p_v_kept")
    qk_stored = [sem(f"p_qk_stored{j}") for j in range(2)]
    DVE_LN = 2 * CT

    with nc.Block() as block:

        @block.gpsimd
        def _(pool):
            for t in (ident, ident_bf, causal_qk, causal_kq, zeros):
                pool.memset(t[:], 0.0).then_inc(const_made, 1)
            pool.memset(minus_half[:], -0.5).then_inc(const_made, 1)
            pool.wait_ge(const_made, 6)
            for t in (ident, ident_bf):
                pool.affine_select(out=t[:], in_=t[:], compare_op=ALU.not_equal, fill=1.0, base=0,
                                   pattern=[[-1, P]], channel_multiplier=1).then_inc(const_made, 1)
            pool.affine_select(out=causal_qk[:], in_=causal_qk[:], compare_op=ALU.is_ge, fill=NEG, base=0,
                               pattern=[[-1, P]], channel_multiplier=1).then_inc(const_made, 1)
            pool.affine_select(out=causal_kq[:], in_=causal_kq[:], compare_op=ALU.is_ge, fill=NEG, base=0,
                               pattern=[[1, P]], channel_multiplier=-1).then_inc(const_made, 1)
            with pool.Fori(0, CHUNKS) as c:
                pool.wait_ge(var_ready, c + 1)
                pool.tensor_tensor(rstd[:], var_eps[:], minus_half[:], ALU.pow).then_inc(rstd_ready, 1)

        @block.sync
        def _(sp):
            sp.dma_start(w_raw[:, :, 0:3 * E], w_in.rearrange("(k p) n -> p k n", p=P)).then_inc(w_loaded, 16)
            sp.dma_start(w_raw[:, :, 3 * E:4 * E], w_out.rearrange("(k p) n -> p k n", p=P)).then_inc(w_loaded, 16)
            sp.wait_ge(const_made, 6)
            sp.dma_start(layer_in[:, :, 0:1, :].rearrange("l b r e -> (l b r) e"), zeros[0:12, 0:E]).then_inc(zero_rows, 16)
            sp.dma_start(layer_mid[:, :, 0:1, :].rearrange("l b r e -> (l b r) e"), zeros[0:8, 0:E]).then_inc(zero_rows, 16)

            def load_x(i, j):
                b, half = i, j
                sp.dma_start(xin[j][:], x[b, half * CHUNK:(half + 1) * CHUNK, :]
                             .rearrange("(q p) e -> p q e", p=P)).then_inc(x_loaded[j], 16)

            def store_xn(i, j):
                sp.wait_ge(xn_ready, 2 * i + j + 1)
                sp.dma_start(layer_in[0, i, 1 + j * CHUNK:1 + (j + 1) * CHUNK, :]
                             .rearrange("(q p) e -> p q e", p=P), xn[j][:]).then_inc(xn_stored[j], 16)

            def store_qk(i, j):
                for m in range(4):
                    dst, h0 = (q_stack, k_stack)[m // 2], i * HC + m % 2 * (HC // 2)
                    for part in (HI, LO):
                        sp.wait_ge((qk_hi, qk_lo)[part], 4 * (2 * i + j) + m + 1)
                        places = (part, part + 2) if m < 2 else (2 * part, 2 * part + 1)
                        for r in places:
                            sp.dma_start(dst[bass.ds(h0, HC // 2), r * DC:(r + 1) * DC, j * CHUNK:(j + 1) * CHUNK],
                                         qk[j][:, part, m, :].bitcast(F32)).then_inc(qk_stored[j], 16)

            for j in range(2):
                load_x(0, j)
            with sp.Fori(0, B - 1) as i:
                for j in range(2):
                    store_xn(i, j)
                    load_x(i + 1, j)
                    store_qk(i, j)
            for j in range(2):
                store_xn(B - 1, j)
                store_qk(B - 1, j)
            sp.wait_ge(zero_rows, 32)
            for j in range(2):
                sp.wait_ge(xn_stored[j], 16 * B)
                sp.wait_ge(qk_stored[j], 16 * 16 * B)

        @block.vector
        def _(dve):
            dve.wait_ge(w_loaded, 32)
            dve.tensor_copy(win_s[:, HI], w_raw[:, :, 0:3 * E]).then_inc(w_split, 1)
            dve.tensor_copy(wout_s[:, HI], w_raw[:, :, 3 * E:4 * E]).then_inc(w_split, 1)
            dve.wait_ge(w_split, 2)
            dve.tensor_tensor(win_s[:, LO], w_raw[:, :, 0:3 * E], win_s[:, HI], ALU.subtract).then_inc(w_split, 1)
            dve.tensor_tensor(wout_s[:, LO], w_raw[:, :, 3 * E:4 * E], wout_s[:, HI], ALU.subtract).then_inc(w_split, 1)
            with dve.Fori(0, B) as i:
                for j in range(2):
                    c = 2 * i + j
                    own = Chain(dve, dve_own, c * DVE_LN)
                    dve.wait_ge(x_loaded[j], 16 * (i + 1))
                    for q in range(CT):
                        own.add(dve.bn_stats(stats[:, q, :], xin[j][:, q, :]))
                    own.wait()
                    dve.sem_inc(counted, 1)
                    for q in range(CT):
                        own.add(dve.bn_aggr(mean_var[:, q, :], stats[:, q, :]))
                    own.wait()
                    dve.tensor_scalar(var_eps[:], mean_var[:, :, 1], EPS, None, ALU.add).then_inc(var_ready, 1)
                    dve.wait_ge(rstd_ready, c + 1)
                    dve.wait_ge(xn_stored[j], 16 * i)
                    dve.wait_ge(xt_made, 2 * c)
                    for q in range(CT):
                        last = dve.tensor_scalar(xn[j][:, q, :], xin[j][:, q, :], mean_var[:, q, 0:1], rstd[:, q:q + 1],
                                                 ALU.subtract, ALU.mult)
                    last.then_inc(xn_ready, 1)
                    for f in range(KE):
                        dve.wait_ge(xt_hi, KE * c + f + 1)
                        dve.tensor_tensor(xt[j][:, LO, f, :], ps_xt[:, f, :], xt[j][:, HI, f, :], ALU.subtract).then_inc(xt_lo, 1)
                    for m in range(4):
                        dve.wait_ge(qk_hi, 4 * c + m + 1)
                        dve.wait_ge(qk_stored[j], 256 * i)
                        dve.scalar_tensor_tensor(out=qk[j][:, LO, m, :], in0=ps_qk[:, m, :], scalar=DC ** -0.5 if m < 2 else 1.0,
                                                 in1=qk[j][:, HI, m, :], op0=ALU.mult, op1=ALU.subtract).then_inc(qk_lo, 1)

        @block.scalar
        def _(act):
            with act.Fori(0, B) as i:
                for j in range(2):
                    c = 2 * i + j
                    for f in range(KE):
                        act.wait_ge(xt_made, KE * c + f + 1)
                        act.activation(xt[j][:, HI, f, :], ps_xt[:, f, :], ACT.Copy).then_inc(xt_hi, 1)
                    act.wait_ge(qk_stored[j], 256 * i)
                    for m in range(4):
                        act.wait_ge(qk_made, 4 * c + m + 1)
                        act.activation(qk[j][:, HI, m, :], ps_qk[:, m, :], ACT.Copy, scale=DC ** -0.5 if m < 2 else 1.0).then_inc(qk_hi, 1)
                    for v in range(2):
                        act.wait_ge(v_made, 2 * c + v + 1)
                        kt0 = CT * j + 2 * v
                        act.activation(values[:, bass.ds(i * HC, HC), kt0:kt0 + 2, :].rearrange("p h t d -> p t h d"),
                                       ps_v[:, v].rearrange("p t (h d) -> p t h d", h=HC), ACT.Copy).then_inc(v_kept, 1)

        @block.tensor
        def _(pe):
            pe.wait_ge(const_made, 10)
            pe.wait_ge(w_split, 4)
            with pe.Fori(0, B) as i:
                for j in range(2):
                    c = 2 * i + j
                    pe.wait_ge(xn_ready, c + 1)
                    pe.wait_ge(xt_lo, KE * c)
                    for f in range(KE):
                        for q in range(CT):
                            mm = pe.transpose(ps_xt[:, f, q * P:(q + 1) * P], xn[j][:, q, f * P:(f + 1) * P], ident[:])
                        mm.then_inc(xt_made, 1)
                    pe.wait_ge(xt_lo, KE * c + KE)
                    pe.wait_ge(qk_lo, 4 * c)
                    for m in range(4):
                        products(pe, ps_qk[:, m, :], lambda part, f: win_s[:, part, f, m * P:(m + 1) * P],
                                 lambda part, f: xt[j][:, part, f, :], KE).then_inc(qk_made, 1)
                    pe.wait_ge(v_kept, 2 * c)
                    for q in range(CT):
                        mm = products(pe, ps_v[:, q // 2, q % 2, :], lambda part, f: xt[j][:, part, f, q * P:(q + 1) * P],
                                      lambda part, f: win_s[:, part, f, 2 * E:3 * E], KE)
                        if q % 2:
                            mm.then_inc(v_made, 1)


def products(pe, out, stationary, moving, tiles):
    steps = [(f, a, b) for f in range(tiles) for a, b in PRODUCTS]
    for n, (f, a, b) in enumerate(steps):
        mm = pe.matmul(out, stationary(a, f), moving(b, f), start=n == 0, stop=n == len(steps) - 1)
    return mm


PIECES = [(t, k0, min(CHUNK, (t + 1) * P - k0)) for t in range(KT) for k0 in range(0, (t + 1) * P, CHUNK)]
PIECES_AT = (3, 2, 2, 2, 2, 1, 0, 0)
AHEAD = 2
RING = 4
MAXIMUM_SLOTS = len(PIECES) + 1
SLOTS = MAXIMUM_SLOTS + 2


def first_slot(i, j):
    n = AHEAD * MAXIMUM_SLOTS - 2 + SLOTS * j
    if isinstance(i, int) and i == 0 and j == 0:
        n += 2
    if isinstance(i, int) and i == UNITS // RING - 1 and j > RING - AHEAD:
        n -= MAXIMUM_SLOTS * (j - (RING - AHEAD))
    return SLOTS * RING * i + n, n % 2


def uses(i, j):
    ahead = not (isinstance(i, int) and i == UNITS // RING - 1 and j >= RING - AHEAD)
    outputs = not (isinstance(i, int) and i == 0 and j == 0)
    listed, k = [], 0
    for kt in range(KT):
        if ahead:
            listed += [(kt, "piece", k + n) for n in range(PIECES_AT[kt])]
            k += PIECES_AT[kt]
        if outputs and kt == 1:
            listed += [(kt, "output", c) for c in range(2)]
    if ahead:
        listed.append((KT, "maxima", 0))
    return listed


def attend(nc, ctx, tensor, psum, sem, q_stack, k_stack, neg_max, attn_out,
           ident, ident_bf, causal_qk, causal_kq, zeros, values):
    qs = [tensor(ctx, f"qs{j}", [KROWS, T], F32R) for j in range(RING)]
    ks = [tensor(ctx, f"ks{j}", [KROWS, T], F32R) for j in range(RING)]
    vs = [tensor(ctx, f"vs{j}", [P, KT, VW]) for j in range(RING)]
    prob_a = tensor(ctx, "prob_a", [P, 4, T])
    prob_b = tensor(ctx, "prob_b", [P, 4, CHUNK])
    maxima = [tensor(ctx, f"maxima{j}", [P, KT + 4]) for j in range(2)]
    max_parts = [tensor(ctx, f"max_parts{j}", [KT, 2, P], F32R) for j in range(RING)]
    sums = [tensor(ctx, f"sums{j}", [P, T]) for j in range(2)]
    folded = tensor(ctx, "folded", [P, 2, CT, VW])
    rsum = tensor(ctx, "rsum", [P, 2, CT])
    heads_out = tensor(ctx, "heads_out", [P, TILES, E])
    ps_s = psum(ctx, "ps_s", [P, 2, CHUNK])
    ps_t = psum(ctx, "ps_t", [P, 2, T])
    ps_o = psum(ctx, "ps_o", [P, 2, CHUNK])

    rows_made = sem("a_rows_made")
    loaded = [sem(f"a_loaded{j}") for j in range(RING)]
    v_ready = sem("a_v_ready")
    slot_made = sem("a_slot_made")
    slot_used = sem("a_slot_used")
    part_hi = sem("a_part_hi")
    rsum_ready = sem("a_rsum_ready")
    max_ready = sem("a_max_ready")
    max_stored = [sem(f"a_max_stored{j}") for j in range(RING)]
    max_loaded = [sem(f"a_max_loaded{j}") for j in range(RING)]
    st_made = sem("a_st_made")
    p_ready = sem("a_p_ready")
    pv_done = sem("a_pv_done")
    sums_ready = sem("a_sums_ready")
    out_done = sem("a_out_done")
    attn_stored = sem("a_attn_stored")
    LOADS = 48

    with nc.Block() as block:

        @block.gpsimd
        def _(pool):
            constants = [(t[j][64:KROWS, :].bitcast(F32), 0.0) for j in range(RING) for t in (qs, ks)]
            constants += [(vs[j][:, :, DC:VW], 0.0) for j in range(RING)]
            constants += [(prob_a[:, r, 0:r * P], 0.0) for r in range(1, 4)]
            constants += [(ks[j][64:66, :].bitcast(F32), 1.0) for j in range(RING)]
            constants += [(vs[j][:, :, DC:DC + 1], 1.0) for j in range(RING)]
            for n, (rows, value) in enumerate(constants):
                pool.memset(rows, value).then_inc(rows_made, 1)
                pool.wait_ge(rows_made, n + 1)

            def values_of(u, j):
                pool.tensor_copy(vs[j][:, :, 0:DC], values[:, u]).then_inc(v_ready, 1)

            for j in range(RING):
                values_of(j, j)
            with pool.Fori(1, UNITS // RING) as i:
                for j in range(RING):
                    u = RING * i + j
                    pool.wait_ge(pv_done, KT * (u - RING + 1))
                    values_of(u, j)

        @block.sync
        def _(sp):
            sp.wait_ge(rows_made, 5 * RING + 3)

            def load(i, j):
                u = RING * i + j
                sp.dma_start(qs[j][0:STACK, :].bitcast(F32), q_stack[u]).then_inc(loaded[j], 16)
                sp.dma_start(ks[j][0:STACK, :].bitcast(F32), k_stack[u]).then_inc(loaded[j], 16)
                sp.dma_start(qs[j][64:66, :].bitcast(F32), zeros[0:2, :]).then_inc(loaded[j], 16)

            def maximum_rows(i, j, n):
                sp.wait_ge(slot_used, n + 1)
                sp.dma_start(neg_max[j].rearrange("s (t n) -> t s n", t=KT),
                             max_parts[j][:].bitcast(F32)).then_inc(max_stored[j], 16)
                sp.wait_ge(max_stored[j], 16 * (i + 1))
                sp.dma_start(qs[j][64:66, :].bitcast(F32), neg_max[j]).then_inc(max_loaded[j], 16)

            def step(i, last=False):
                for j in range(RING):
                    if not (last and j >= RING - AHEAD):
                        maximum_rows(i + (j + AHEAD) // RING, (j + AHEAD) % RING, first_slot(i, j)[0] + len(uses(i, j)) - 1)
                    if not last:
                        sp.wait_ge(st_made, KT * (RING * i + j + 1))
                        load(i + 1, j)

            for j in range(RING):
                load(0, j)
            for j in range(AHEAD):
                maximum_rows(0, j, MAXIMUM_SLOTS * (j + 1) - 1)
            step(0)
            with sp.Fori(1, UNITS // RING - 1) as i:
                step(i)
            step(UNITS // RING - 1, last=True)
            sp.wait_ge(out_done, 2 * UNITS)
            sp.dma_start(attn_out.rearrange("t p e -> p t e"), heads_out[:]).then_inc(attn_stored, 16)
            sp.wait_ge(attn_stored, 16)

        @block.tensor
        def _(pe):
            def free_bank(n):
                if not isinstance(n, int) or n >= 2:
                    pe.wait_ge(slot_used, n - 1)

            def piece(j, k, n, bank):
                t, k0, keys = PIECES[k]
                free_bank(n)
                diagonal = k0 + keys == (t + 1) * P
                mm = pe.matmul(ps_s[:, bank, 0:keys], qs[j][:, t * P:(t + 1) * P], ks[j][:, k0:k0 + keys],
                               start=True, stop=not diagonal)
                if diagonal:
                    mm = pe.matmul(ps_s[:, bank, keys - P:keys], ident_bf[:], causal_qk[:], start=False, stop=True)
                mm.then_inc(slot_made, 1)

            def turn_maxima(u, half, n, bank):
                pe.wait_ge(max_ready, u + 1)
                free_bank(n)
                pe.transpose(ps_s[0:KT, bank, 0:P], maxima[half][:, 0:KT], ident[:]).then_inc(slot_made, 1)

            def turn_output(u, half, c, n, bank):
                pe.wait_ge(sums_ready, u + 1)
                free_bank(n)
                for q in range(CT):
                    mm = pe.transpose(ps_s[:, bank, q * P:(q + 1) * P], sums[half][:, (CT * c + q) * P:(CT * c + q + 1) * P], ident[:])
                mm.then_inc(slot_made, 1)

            def scores_t(i, j, kt):
                n = KT * (RING * i + j) + kt
                if kt == 0:
                    pe.wait_ge(max_loaded[j], 16 * (i + 1))
                if not isinstance(n, int) or n >= 2:
                    pe.wait_ge(p_ready, n - 1)
                q0, half = kt * P, kt % 2
                for a in range(q0 // CHUNK, T // CHUNK):
                    lo, hi = max(q0, a * CHUNK), (a + 1) * CHUNK
                    diagonal = lo == q0
                    mm = pe.matmul(ps_t[:, half, lo:hi], ks[j][:, q0:q0 + P], qs[j][:, lo:hi], start=True, stop=not diagonal)
                    if diagonal:
                        mm = pe.matmul(ps_t[:, half, q0:q0 + P], ident_bf[:], causal_kq[:], start=False, stop=True)
                mm.then_inc(st_made, 1)

            def weighted(i, j, kt):
                u, r = RING * i + j, kt % 4
                g = (r + 2) % 4
                pe.wait_ge(p_ready, KT * u + kt + 1)
                if kt == 0:
                    pe.wait_ge(v_ready, u + 1)
                    pe.wait_ge(sums_ready, u)
                if kt < 4:
                    pe.matmul(ps_o[r * VW:(r + 1) * VW, 0, :], vs[j][:, kt, :], prob_a[:, r, 0:CHUNK], start=True, stop=True)
                    mm = pe.matmul(ps_o[g * VW:(g + 1) * VW, 1, :], vs[j][:, kt, :], prob_a[:, r, CHUNK:T], start=True, stop=False)
                else:
                    mm = pe.matmul(ps_o[g * VW:(g + 1) * VW, 1, r * P:CHUNK], vs[j][:, kt, :], prob_b[:, r, r * P:CHUNK],
                                   start=False, stop=True)
                mm.then_inc(pv_done, 1)

            def step(i):
                for j in range(RING):
                    u, listed = RING * i + j, uses(i, j)
                    n, bank = first_slot(i, j)
                    ja = (j + AHEAD) % RING
                    if any(kind == "piece" for _, kind, _ in listed):
                        pe.wait_ge(loaded[ja], LOADS * (i + (j + AHEAD) // RING + 1))
                    for kt in range(KT + 1):
                        if kt < KT:
                            scores_t(i, j, kt)
                        elif listed and listed[-1][1] == "maxima":
                            weighted(i, j, KT - 1)
                        for e, (at, kind, which) in enumerate(listed):
                            if at != kt:
                                continue
                            where = n + e, (bank + e) % 2
                            if kind == "piece":
                                piece(ja, which, *where)
                            elif kind == "output":
                                turn_output(u - 1, (j - 1) % 2, which, *where)
                            else:
                                turn_maxima(u + AHEAD, j % 2, *where)
                        if 1 <= kt < KT:
                            weighted(i, j, kt - 1)
                    if not (listed and listed[-1][1] == "maxima"):
                        weighted(i, j, KT - 1)

            pe.wait_ge(rows_made, 5 * RING + 3)
            for u in range(AHEAD):
                n = MAXIMUM_SLOTS * u
                pe.wait_ge(loaded[u], LOADS)
                for k in range(len(PIECES)):
                    piece(u, k, n + k, (n + k) % 2)
                n += len(PIECES)
                turn_maxima(u, u % 2, n, n % 2)
            step(0)
            with pe.Fori(1, UNITS // RING - 1) as i:
                step(i)
            step(UNITS // RING - 1)
            n = SLOTS * UNITS - 2
            for c in range(2):
                turn_output(UNITS - 1, (RING - 1) % 2, c, n + c, (n + c) % 2)

        @block.scalar
        def _(act):
            def exp_tile(u, kt):
                act.wait_ge(st_made, KT * u + kt + 1)
                before = KT * (u - 1) + kt + 1
                if not isinstance(u, int) or before > 0:
                    act.wait_ge(pv_done, before)
                r = kt % 4
                dst = prob_a[:, r, kt * P:T] if kt < 4 else prob_b[:, r, r * P:CHUNK]
                act.activation(dst, ps_t[:, kt % 2, kt * P:T], ACT.Exp).then_inc(p_ready, 1)

            def keep_sums(u, half):
                act.wait_ge(pv_done, KT * (u + 1))
                if not isinstance(u, int) or u >= 2:
                    act.wait_ge(out_done, 2 * (u - 1))
                act.activation(sums[half][:], ps_o[:].rearrange("p c n -> p (c n)"), ACT.Copy).then_inc(sums_ready, 1)

            def step(i):
                for j in range(RING):
                    u = RING * i + j
                    for kt in range(KT):
                        exp_tile(u, kt)
                        if kt == 0 and not (isinstance(u, int) and u == 0):
                            keep_sums(u - 1, (j - 1) % 2)

            act.wait_ge(rows_made, 5 * RING + 3)
            step(0)
            with act.Fori(1, UNITS // RING) as i:
                step(i)
            keep_sums(UNITS - 1, (RING - 1) % 2)

        @block.vector
        def _(dve):
            def piece(half, k, n, bank):
                t, k0, keys = PIECES[k]
                col = t if k0 == 0 else KT + t - 4
                dve.wait_ge(slot_made, n + 1)
                dve.tensor_reduce(maxima[half][:, col:col + 1], ps_s[:, bank, 0:keys], AX.X, ALU.max).then_inc(slot_used, 1)

            def finish_maxima(i, j, n, bank):
                u, half = RING * i + j, j % 2
                dve.wait_ge(slot_used, n)
                dve.tensor_tensor(maxima[half][:, 4:KT], maxima[half][:, 4:KT], maxima[half][:, KT:KT + 4], ALU.max).then_inc(max_ready, 1)
                dve.wait_ge(slot_made, n + 1)
                dve.wait_ge(max_stored[j], 16 * i)
                dve.tensor_scalar(max_parts[j][:, HI, :], ps_s[0:KT, bank, 0:P], -1.0, None, ALU.mult).then_inc(part_hi, 1)
                dve.wait_ge(part_hi, u + 1)
                dve.scalar_tensor_tensor(out=max_parts[j][:, LO, :], in0=ps_s[0:KT, bank, 0:P], scalar=-1.0,
                                         in1=max_parts[j][:, HI, :], op0=ALU.mult, op1=ALU.subtract).then_inc(slot_used, 1)

            def output(i, j, c, n, bank):
                dve.wait_ge(slot_made, n + 1)
                dve.tensor_reduce(folded[:, c, :, 0:DC + 1],
                                  ps_s[:, bank, :].rearrange("p (q g w) -> p q w g", q=CT, g=4)[:, :, 0:DC + 1, :],
                                  AX.X, ALU.add).then_inc(slot_used, 1)
                dve.wait_ge(slot_used, n + 1)
                dve.reciprocal(rsum[:, c, :], folded[:, c, :, DC]).then_inc(rsum_ready, 1)
                dve.wait_ge(rsum_ready, 2 * (RING * i + j) + c + 1)
                dve.tensor_tensor(heads_out[:, bass.ds((i // 4) * KT + CT * c, CT), bass.ds((i % 4) * 4 * DC + j * DC, DC)],
                                  folded[:, c, :, 0:DC], rsum[:, c, :].unsqueeze(2).broadcast_to([P, CT, DC]),
                                  ALU.mult).then_inc(out_done, 1)

            def step(i):
                for j in range(RING):
                    n, bank = first_slot(i, j)
                    for e, (_, kind, which) in enumerate(uses(i, j)):
                        where = n + e, (bank + e) % 2
                        if kind == "piece":
                            piece(j % 2, which, *where)
                        elif kind == "output":
                            output(i if j else i - 1, (j - 1) % RING, which, *where)
                        else:
                            finish_maxima(i + (j + AHEAD) // RING, (j + AHEAD) % RING, *where)

            for u in range(AHEAD):
                n = MAXIMUM_SLOTS * u
                for k in range(len(PIECES)):
                    piece(u, k, n + k, (n + k) % 2)
                n += len(PIECES)
                finish_maxima(0, u, n, n % 2)
            step(0)
            with dve.Fori(1, UNITS // RING - 1) as i:
                step(i)
            step(UNITS // RING - 1)
            n = SLOTS * UNITS - 2
            for c in range(2):
                output(UNITS // RING - 1, RING - 1, c, n + c, (n + c) % 2)


WINDOWS = TILES
PER_BATCH = WINDOWS // B
PAIRS = HL // 2
TURNS = 5


def local_layers(nc, ctx, tensor, psum, sem, layer_in, layer_mid, w_qkv, w_o, w1, w2, ln_gb, b1, b2,
                 qk_scale, trig, ident, ident_bf):
    class Arena:

        def __init__(self, name, dt, words):
            self.whole, self.words, self.at = tensor(ctx, name, [P, words], dt), words, 0

        def take(self, *shape):
            n = 1
            for s in shape:
                n *= s
            part = self.whole[:, self.at:self.at + n]
            self.at += n
            assert self.at <= self.words
            if len(shape) == 1:
                return part
            names = "abcd"[:len(shape)]
            return part.rearrange(f"p ({' '.join(names)}) -> p {' '.join(names)}", **dict(zip(names, shape)))

    plain, rounded = Arena("plain", F32, 10240), Arena("rounded", F32R, 9728)
    wqkv_s = tensor(ctx, "wqkv_s", [P, 2, KE, 3 * INNER], F32R)
    wo_s = tensor(ctx, "wo_s", [P, 2, PAIRS, E], F32R)
    w1_s = tensor(ctx, "w1_s", [P, 2, KE, 2 * HIDP], F32R)
    w2_s = tensor(ctx, "w2_s", [P, 2, HT, E], F32R)
    w_raw = tensor(ctx, "lw_raw", [P, KE * 3 * INNER + HT * E])
    gb = tensor(ctx, "gb", [P, 2, KE])
    b1_t = tensor(ctx, "b1_t", [P, 2 * HT])
    b2_t = tensor(ctx, "b2_t", [P, E])
    scale_t = tensor(ctx, "scale_t", [P, 4, DL])
    trig_t = tensor(ctx, "trig_t", [P, PER_BATCH, 4, DL])
    rotary = tensor(ctx, "rotary", [P, PER_BATCH, 2, 2, DL])
    own_mask = tensor(ctx, "own_mask", [P, P], BF16)
    before_mask = tensor(ctx, "before_mask", [P, P], BF16)
    mask_even = tensor(ctx, "mask_even", [P, 4, 2, 2, P], BF16)
    mask_odd = tensor(ctx, "mask_odd", [P, 2, 2, P], BF16)
    minus_half = tensor(ctx, "l_minus_half", [P, 2 * HL])

    hin = [plain.take(E) for _ in range(2)]
    res = [plain.take(E) for _ in range(2)]
    mid = [plain.take(E) for _ in range(2)]
    square = plain.take(2 * HL, DL)
    straight = plain.take(2, HL, DL)
    crossed = plain.take(2, HL, DL)
    unit = plain.take(2 * HL, DL)
    prob = [plain.take(2, 2 * P) for _ in range(2)]
    prob_t = [plain.take(2, 2, P) for _ in range(2)]
    norm2, rnorm = plain.take(2 * HL), plain.take(2 * HL)
    minus_max, row_sum, row_inv = plain.take(HL), plain.take(HL), plain.take(HL)
    values = tensor(ctx, "l_values", [P, 2, HL, DL])
    ht = [rounded.take(2, KE, P) for _ in range(2)]
    halves_q = rounded.take(HL, 2, DL)
    halves_k = rounded.take(HL, 3, DL)
    keys = rounded.take(2, HL, 2, P)
    queries = rounded.take(HL, P)
    heads = rounded.take(2, PAIRS, P)
    plain.at = rounded.at = 0
    fin = [plain.take(CT, E) for _ in range(2)]
    fres = [plain.take(CT, E) for _ in range(2)]
    fout = [plain.take(CT, E) for _ in range(2)]
    affine = plain.take(KE, CHUNK)
    gate = [plain.take(CHUNK) for _ in range(2)]
    hidden = [plain.take(CHUNK) for _ in range(2)]
    stats, mean_var = plain.take(CT, 6), plain.take(CT, 2)
    var_eps, rstd = plain.take(CT), plain.take(CT)
    ft = rounded.take(2, KE, CHUNK)
    hid = rounded.take(2, HT, CHUNK)

    ps_h = psum(ctx, "l_ps_h", [P, CHUNK])
    ps_qk = psum(ctx, "l_ps_qk", [P, 2, CHUNK])
    ps_v = psum(ctx, "l_ps_v", [P, CHUNK])
    ps_ta = psum(ctx, "l_ps_ta", [P, CHUNK])
    ps_td = psum(ctx, "l_ps_td", [P, CHUNK])
    ps_s = psum(ctx, "l_ps_s", [P, 2, CHUNK])
    ps_ft = ps_qk
    ps_out = ps_s
    ps_ga = [(ps_h, ps_v), (ps_ta, ps_td)]

    def sems(names):
        return [sem("l_" + n) for n in names.split()]

    const_made, masks_made, weights_in, weights_split, trig_in, trig_scaled = sems(
        "const_made masks_made weights_in weights_split trig_in trig_scaled")
    layer_stored, f_counted = sems("layer_stored f_counted")
    h_turned, h_hi, h_lo, qk_made, v_made, v_kept = sems("h_turned h_hi h_lo qk_made v_made v_kept")
    sq_ready, crossed_ready, norm_sum, norm_ready, r_ready, added, u_ready, u_hi, u_lo = sems(
        "sq_ready crossed_ready norm_sum norm_ready r_ready added u_ready u_hi u_lo")
    ta_made, ta_used, td_made, td_used = sems("ta_made ta_used td_made td_used")
    s_made, max_ready, exp_ready, inv_ready, p_ready = sems("s_made max_ready exp_ready inv_ready p_ready")
    o_part, o_made, o_hi, o_lo, y_made, y_ready = sems("o_part o_made o_hi o_lo y_made y_ready")
    f_stats, f_aggr, f_var, f_rstd, f_norm, f_turned, f_affine, f_hi, f_lo = sems(
        "f_stats f_aggr f_var f_rstd f_norm f_turned f_affine f_hi f_lo")
    g_made, a_made, gate_ready, hid_ready, hid_hi, hid_lo, f_made, f_res, f_ready = sems(
        "g_made a_made gate_ready hid_ready hid_hi hid_lo f_made f_res f_ready")
    h_in, res_in, mid_out, f_in, fres_in, f_out = ([sem(f"l_{n}{j}") for j in range(2)]
                                                   for n in ("h_in", "res_in", "mid_out", "f_in", "fres_in", "f_out"))
    WI, CI = WINDOWS // 2, CHUNKS // 2
    QKV_IN, MLP_IN = 4 * 16, 4 * 16

    def is_first(i, j=0):
        return isinstance(i, int) and i == 0 and j == 0

    def side(tile, s):
        return tile[:, s * HL:(s + 1) * HL]

    def is_window(i, j, *which):
        return isinstance(i, int) and 2 * i + j in which

    def away(i, j, n):
        return i + (j + n) // 2, (j + n) % 2

    with nc.Block() as block:

        @block.gpsimd
        def _(pool):
            pool.memset(own_mask[:], 0.0).then_inc(const_made, 1)
            pool.memset(before_mask[:], 0.0).then_inc(const_made, 1)
            pool.memset(minus_half[:], -0.5).then_inc(const_made, 1)
            pool.wait_ge(const_made, 3)
            pool.affine_select(out=own_mask[:], in_=own_mask[:], compare_op=ALU.is_ge, fill=NEG, base=0,
                               pattern=[[-1, P]], channel_multiplier=1).then_inc(const_made, 1)
            pool.affine_select(out=before_mask[:], in_=before_mask[:], compare_op=ALU.is_ge, fill=NEG, base=0,
                               pattern=[[1, P]], channel_multiplier=-1).then_inc(const_made, 1)

            def norm_inverse(l, i, j, s):
                n = 2 * (WINDOWS * l + 2 * i + j) + 1 - s
                pool.wait_ge(norm_ready, n + 1)
                pool.tensor_tensor(side(rnorm, s), side(norm2, s), side(minus_half, s), ALU.pow).then_inc(r_ready, 1)

            def unit_vectors(l, i, j, s):
                n = 2 * (WINDOWS * l + 2 * i + j) + 1 - s
                pool.wait_ge(crossed_ready, n + 1)
                if not is_first(i, j):
                    pool.wait_ge(u_hi, n - 1)
                    pool.wait_ge(u_lo, n - 1)
                pool.tensor_tensor(side(unit, s), straight[:, s], crossed[:, s], ALU.add).then_inc(added, 1)
                pool.wait_ge(r_ready, n + 1)
                pool.wait_ge(added, n + 1)
                pool.tensor_tensor(side(unit, s), side(unit, s), side(rnorm, s).unsqueeze(2).broadcast_to([P, HL, DL]),
                                   ALU.mult).then_inc(u_ready, 1)

            def unit_lo(l, i, j, s):
                t = WINDOWS * l + 2 * i + j
                pool.wait_ge(u_ready, 2 * t + 2 - s)
                pool.wait_ge(u_hi, 2 * t + 2 - s)
                if not is_first(i, j):
                    pool.wait_ge(ta_made, TURNS * t - 2 - s)
                    pool.wait_ge(td_made, TURNS * t - 2 - s)
                halves = halves_k if s else halves_q
                pool.tensor_tensor(halves[:, :, LO, :], side(unit, s), halves[:, :, HI, :], ALU.subtract).then_inc(u_lo, 1)

            def window(l, i, j):
                norm_inverse(l, i, j, 1)
                unit_vectors(l, i, j, 1)
                norm_inverse(l, i, j, 0)
                unit_lo(l, i, j, 1)
                unit_vectors(l, i, j, 0)
                unit_lo(l, i, j, 0)

            def inverse_deviation(l, i, j):
                t = CHUNKS * l + 2 * i + j
                pool.wait_ge(f_var, t + 1)
                pool.tensor_tensor(rstd, var_eps, minus_half[:, 0:CT], ALU.pow).then_inc(f_rstd, 1)

            def input_lo(l, i, j):
                t = CHUNKS * l + 2 * i + j
                for f in range(KE):
                    pool.wait_ge(f_hi, KE * t + f + 1)
                    pool.tensor_tensor(ft[:, LO, f, :], affine[:, f, :], ft[:, HI, f, :], ALU.subtract).then_inc(f_lo, 1)

            def chunk(l, i, j, last=False):
                t = CHUNKS * l + 2 * i + j
                if not last:
                    inverse_deviation(l, i + j, 1 - j)
                pool.wait_ge(fres_in[j], 16 * (CI * l + i + 1))
                pool.tensor_tensor(fres[j], fres[j], b2_t[:].unsqueeze(1).broadcast_to([P, CT, E]), ALU.add).then_inc(f_res, 1)
                for k in range(HT):
                    pool.wait_ge(hid_hi, HT * t + k + 1)
                    pool.tensor_tensor(hid[:, LO, k, :], hidden[k % 2], hid[:, HI, k, :], ALU.subtract).then_inc(hid_lo, 1)
                if not last:
                    input_lo(l, i + j, 1 - j)

            with pool.Fori(0, DEPTH) as l:
                for j in range(2):
                    window(l, 0, j)
                with pool.Fori(1, WI) as i:
                    for j in range(2):
                        window(l, i, j)
                inverse_deviation(l, 0, 0)
                input_lo(l, 0, 0)
                with pool.Fori(0, CI - 1) as i:
                    for j in range(2):
                        chunk(l, i, j)
                chunk(l, CI - 1, 0)
                chunk(l, CI - 1, 1, last=True)

        @block.sync
        def _(sp):
            sp.dma_start(trig_t[:], trig).then_inc(trig_in, 16)
            sp.wait_ge(trig_in, 16)

            def tokens(scratch, l, i, j, shift, columns):
                row = 1 - shift + P * (2 * (i % 4) + j)
                return scratch[l, i // 4, bass.ds(row, P), columns]

            def chunk_tokens(scratch, l, i, j, shift, columns):
                row = 1 - shift + CHUNK * j
                return scratch[l, i, row:row + CHUNK, columns].rearrange("(q p) e -> p q e", p=P)

            def load_h(l, i, j):
                sp.dma_start(hin[j][:, 0:P], tokens(layer_in, l, i, j, 0, slice(0, P))).then_inc(h_in[j], 16)
                sp.dma_start(hin[j][:, P:E], tokens(layer_in, l, i, j, 1, slice(P, E))).then_inc(h_in[j], 16)

            def load_res(l, i, j):
                sp.dma_start(res[j], tokens(layer_in, l, i, j, 0, slice(0, E))).then_inc(res_in[j], 16)

            def window(l, i, j, load_next=True, load_residual=True):
                t = WINDOWS * l + 2 * i + j
                if load_next:
                    sp.wait_ge(h_turned, t + 3)
                    load_h(l, i + 2, j)
                sp.wait_ge(y_ready, t + 1)
                sp.dma_start(tokens(layer_mid, l, i, j, 0, slice(0, E)), mid[j]).then_inc(mid_out[j], 16)
                if load_residual:
                    load_res(l, i + 1, j)

            def load_f(l, i, j):
                sp.dma_start(fin[j][:, :, 0:P], chunk_tokens(layer_mid, l, i, j, 0, slice(0, P))).then_inc(f_in[j], 16)
                sp.dma_start(fin[j][:, :, P:E], chunk_tokens(layer_mid, l, i, j, 1, slice(P, E))).then_inc(f_in[j], 16)

            def load_fres(l, i, j):
                sp.dma_start(fres[j], chunk_tokens(layer_mid, l, i, j, 0, slice(0, E))).then_inc(fres_in[j], 16)

            def chunk(l, i, j, last):
                t = CHUNKS * l + 2 * i + j
                if not last:
                    sp.wait_ge(f_turned, KE * (t + 1))
                    load_f(l, i + 1, j)
                sp.wait_ge(f_ready, 2 * (t + 1))
                sp.dma_start(chunk_tokens(layer_in, l + 1, i, j, 0, slice(0, E)), fout[j]).then_inc(f_out[j], 16)
                if not last:
                    load_fres(l, i + 1, j)

            with sp.Fori(0, DEPTH) as l:
                sp.dma_start(w_raw[:, 0:KE * 3 * INNER].rearrange("p (k n) -> p k n", k=KE),
                             w_qkv[l].rearrange("(k p) n -> p k n", p=P)).then_inc(weights_in, 16)
                sp.dma_start(w_raw[:, KE * 3 * INNER:KE * 3 * INNER + PAIRS * E].rearrange("p (k n) -> p k n", k=PAIRS),
                             w_o[l].rearrange("(k p) n -> p k n", p=P)).then_inc(weights_in, 16)
                sp.dma_start(scale_t[:], qk_scale[l]).then_inc(weights_in, 16)
                sp.dma_start(gb[:], ln_gb[l]).then_inc(weights_in, 16)
                for j in range(2):
                    load_h(l, 0, j)
                    load_res(l, 0, j)
                sp.wait_ge(weights_split, 8 * l + 4)
                sp.dma_start(w_raw[:, 0:KE * 2 * HIDP].rearrange("p (k n) -> p k n", k=KE),
                             w1[l].rearrange("(k p) n -> p k n", p=P)).then_inc(weights_in, 16)
                sp.dma_start(w_raw[:, KE * 2 * HIDP:KE * 2 * HIDP + HT * E].rearrange("p (k n) -> p k n", k=HT),
                             w2[l].rearrange("(k p) n -> p k n", p=P)).then_inc(weights_in, 16)
                sp.dma_start(b1_t[:], b1[l]).then_inc(weights_in, 16)
                sp.dma_start(b2_t[:], b2[l]).then_inc(weights_in, 16)
                for j in range(2):
                    sp.wait_ge(h_turned, WINDOWS * l + j + 1)
                    load_h(l, 1, j)
                with sp.Fori(0, WI - 2) as i:
                    for j in range(2):
                        window(l, i, j)
                for j in range(2):
                    window(l, WI - 2, j, load_next=False)
                for j in range(2):
                    window(l, WI - 1, j, load_next=False, load_residual=False)
                for j in range(2):
                    sp.wait_ge(mid_out[j], 16 * WI * (l + 1))
                for j in range(2):
                    load_f(l, 0, j)
                    load_fres(l, 0, j)
                with sp.Fori(0, CI - 1) as i:
                    for j in range(2):
                        chunk(l, i, j, False)
                for j in range(2):
                    chunk(l, CI - 1, j, True)
                for j in range(2):
                    sp.wait_ge(f_out[j], 16 * CI * (l + 1))
                sp.sem_inc(layer_stored, 1)

        @block.tensor
        def _(pe):
            def turn_h(l, i, j):
                t = WINDOWS * l + 2 * i + j
                pe.wait_ge(h_in[j], 32 * (WI * l + i + 1))
                if is_window(i, j, 1, 2):
                    pe.wait_ge(h_lo, t)
                elif not is_first(i, j):
                    pe.wait_ge(o_lo, t - 2)
                for f in range(KE):
                    mm = pe.transpose(ps_h[:, f * P:(f + 1) * P], hin[j][:, f * P:(f + 1) * P], ident[:])
                mm.then_inc(h_turned, 1)

            def project_side(l, i, j, s):
                t = WINDOWS * l + 2 * i + j
                if s == 1:
                    pe.wait_ge(h_lo, t + 1)
                if not is_first(i, j):
                    pe.wait_ge(crossed_ready, 2 * t - s)
                    pe.wait_ge(sq_ready, 2 * t - s)
                products(pe, ps_qk[:, s, :], lambda part, f: ht[j][:, part, f, :],
                         lambda part, f: wqkv_s[:, part, f, s * INNER:(s + 1) * INNER], KE).then_inc(qk_made, 1)

            def turned_tile(t, n, even, first=False):
                if not (first and n == 0):
                    pe.wait_ge(ta_used if even else td_used, TURNS * t + n)
                return ps_ta if even else ps_td, ta_made if even else td_made

            def stacks(l, i, j, n):
                t = WINDOWS * l + 2 * i + j
                if n != 1:
                    pe.wait_ge(u_lo, 2 * t + 1 + n // 2)
                halves, part = ((halves_k, HI), (halves_k, LO), (halves_q, HI))[n]
                for even in (True, False):
                    out, made = turned_tile(t, n, even, is_first(i, j))
                    for q in range(4):
                        rows = halves[:, q + (0 if even else 4), part:part + 2, :].rearrange("p s d -> p (s d)")
                        mm = pe.transpose(out[:, q * P:(q + 1) * P], rows.bitcast(F32), ident[:])
                    mm.then_inc(made, 1)

            def project_v(l, i, j):
                t = WINDOWS * l + 2 * i + j
                if is_window(i, j, 1):
                    pe.wait_ge(v_kept, t)
                elif not is_first(i, j):
                    pe.wait_ge(y_ready, t - 1)
                products(pe, ps_v[:], lambda part, f: ht[j][:, part, f, :],
                         lambda part, f: wqkv_s[:, part, f, 2 * INNER:3 * INNER], KE).then_inc(v_made, 1)

            def scores(l, i, j, p):
                t = WINDOWS * l + 2 * i + j
                if p == 0:
                    pe.wait_ge(ta_used, TURNS * t + 3)
                    pe.wait_ge(td_used, TURNS * t + 3)
                if not is_first(i, j) or p >= 2:
                    pe.wait_ge(exp_ready, PAIRS * t + p - 1)
                masks = (mask_even[:, i % 4] if j == 0 else mask_odd[:]).rearrange("p h s n -> p (h s n)")
                pe.matmul(ps_s[:, p % 2, :], ident_bf[:], masks, start=True, stop=False)
                for h2 in range(2):
                    for part in (HI, LO):
                        mm = pe.matmul(ps_s[:, p % 2, h2 * 2 * P:(h2 + 1) * 2 * P], queries[:, 2 * p + h2, :],
                                       keys[:, part, 2 * p + h2].rearrange("p s n -> p (s n)"), start=False, stop=h2 == 1 and part == LO)
                mm.then_inc(s_made, 1)

            def turn_prob(l, i, j, p):
                t = WINDOWS * l + 2 * i + j
                out, made = turned_tile(t, 3 + p // 2, p % 2 == 0)
                pe.wait_ge(p_ready, PAIRS * t + p + 1)
                for h2 in range(2):
                    for s in range(2):
                        mm = pe.transpose(out[:, (2 * h2 + s) * P:(2 * h2 + s + 1) * P], prob[p % 2][:, h2, s * P:(s + 1) * P], ident[:])
                mm.then_inc(made, 1)

            def weighted(l, i, j, p):
                t = WINDOWS * l + 2 * i + j
                if p == 0:
                    pe.wait_ge(v_kept, t + 1)
                    if not is_window(i, j, WINDOWS - 2, WINDOWS - 1):
                        pe.wait_ge(h_lo, t + 3)
                pe.wait_ge(ta_used if p % 2 == 0 else td_used, TURNS * t + 4 + p // 2)
                for s in range(2):
                    for h2 in range(2):
                        mm = pe.matmul(ps_h[h2 * DL:(h2 + 1) * DL, p * P:(p + 1) * P], values[:, s, 2 * p + h2, :],
                                       prob_t[p % 2][:, h2, s, :], start=s == 0, stop=s == 1)
                if p < 2:
                    mm.then_inc(o_part, 1)
                if p == PAIRS - 1:
                    mm.then_inc(o_made, 1)

            def project_out(l, i, j):
                t = WINDOWS * l + 2 * i + j
                pe.wait_ge(o_lo, t + 1)
                if is_window(i, j, WINDOWS - 1):
                    pe.wait_ge(y_ready, t)
                else:
                    pe.wait_ge(v_kept, t + 2)
                products(pe, ps_v[:, 0:E], lambda part, f: heads[:, part, f, :], lambda part, f: wo_s[:, part, f, :],
                         PAIRS).then_inc(y_made, 1)

            def step(l, i, j, before=True, next1=True, next2=True):
                stacks(l, i, j, 0)
                if before:
                    weighted(l, *away(i, j, -1), PAIRS - 1)
                stacks(l, i, j, 1)
                stacks(l, i, j, 2)
                if next2:
                    turn_h(l, *away(i, j, 2))
                if before:
                    project_out(l, *away(i, j, -1))
                scores(l, i, j, 0)
                scores(l, i, j, 1)
                if next1:
                    project_v(l, *away(i, j, 1))
                scores(l, i, j, 2)
                turn_prob(l, i, j, 0)
                scores(l, i, j, 3)
                turn_prob(l, i, j, 1)
                weighted(l, i, j, 0)
                if next2:
                    project_side(l, *away(i, j, 2), 1)
                turn_prob(l, i, j, 2)
                weighted(l, i, j, 1)
                if next2:
                    project_side(l, *away(i, j, 2), 0)
                turn_prob(l, i, j, 3)
                weighted(l, i, j, 2)

            def turn_f(l, i, j):
                t = CHUNKS * l + 2 * i + j
                pe.wait_ge(f_norm, t + 1)
                if not is_first(i, j):
                    pe.wait_ge(f_affine, KE * t)
                for f in range(KE):
                    for q in range(CT):
                        mm = pe.transpose(ps_ft[:, f, q * P:(q + 1) * P], fin[j][:, q, f * P:(f + 1) * P], ident[:])
                    mm.then_inc(f_turned, 1)

            def hidden_tiles(l, i, j):
                t = CHUNKS * l + 2 * i + j
                pe.wait_ge(f_lo, KE * (t + 1))
                for k in range(HT):
                    if not is_first(i, j) or k >= 2:
                        pe.wait_ge(hid_ready, HT * t + k - 1)
                    for which, made in ((1, g_made), (0, a_made)):
                        c0 = which * HIDP + k * P
                        products(pe, ps_ga[k % 2][1 - which][:], lambda part, f: w1_s[:, part, f, c0:c0 + P],
                                 lambda part, f: ft[:, part, f, :], KE).then_inc(made, 1)

            def project_hidden(l, i, j):
                t = CHUNKS * l + 2 * i + j
                pe.wait_ge(hid_lo, HT * (t + 1))
                for q in range(CT):
                    if q % 2 == 0 and not is_first(i, j):
                        pe.wait_ge(f_ready, 2 * t - 1 + q // 2)
                    mm = products(pe, ps_out[:, q // 2, (q % 2) * E:(q % 2 + 1) * E],
                                  lambda part, f: hid[:, part, f, q * P:(q + 1) * P], lambda part, f: w2_s[:, part, f, :], HT)
                    if q % 2:
                        mm.then_inc(f_made, 1)

            def chunk(l, i, j, last=False):
                hidden_tiles(l, i, j)
                if not last:
                    turn_f(l, i + j, 1 - j)
                project_hidden(l, i, j)

            pe.wait_ge(masks_made, 5)
            with pe.Fori(0, DEPTH) as l:
                pe.wait_ge(weights_split, 8 * l + 4)
                turn_h(l, 0, 0)
                for s in (1, 0):
                    project_side(l, 0, 0, s)
                turn_h(l, 0, 1)
                project_v(l, 0, 0)
                for s in (1, 0):
                    project_side(l, 0, 1, s)
                step(l, 0, 0, before=False)
                step(l, 0, 1)
                with pe.Fori(1, WI - 1) as i:
                    for j in range(2):
                        step(l, i, j)
                step(l, WI - 1, 0, next2=False)
                step(l, WI - 1, 1, next1=False, next2=False)
                weighted(l, WI - 1, 1, PAIRS - 1)
                project_out(l, WI - 1, 1)
                pe.wait_ge(weights_split, 8 * l + 8)
                turn_f(l, 0, 0)
                for j in range(2):
                    chunk(l, 0, j)
                with pe.Fori(1, CI - 1) as i:
                    for j in range(2):
                        chunk(l, i, j)
                chunk(l, CI - 1, 0)
                chunk(l, CI - 1, 1, last=True)

        @block.scalar
        def _(act):
            def project(l, i, j):
                t = WINDOWS * l + 2 * i + j
                act.wait_ge(h_turned, t + 1)
                if not (isinstance(i, int) and i == 0):
                    act.wait_ge(v_made, t - 1)
                act.activation(ht[j][:, HI].rearrange("p f n -> p (f n)"), ps_h[:, 0:E], ACT.Copy).then_inc(h_hi, 1)

            def squares(l, i, j, s):
                n = 2 * (WINDOWS * l + 2 * i + j) + 1 - s
                act.wait_ge(qk_made, n + 1)
                if not is_first(i, j):
                    act.wait_ge(norm_sum, n - 1)
                act.activation(side(square, s).rearrange("p h d -> p (h d)"), ps_qk[:, s, :], ACT.Square).then_inc(sq_ready, 1)

            def unit_hi(l, i, j, s):
                t = WINDOWS * l + 2 * i + j
                act.wait_ge(u_ready, 2 * t + 2 - s)
                if not is_first(i, j):
                    act.wait_ge(ta_made, TURNS * t - 2 - s)
                    act.wait_ge(td_made, TURNS * t - 2 - s)
                if s == 0:
                    act.activation(halves_q[:, :, HI, :], unit[:, 0:HL, :], ACT.Copy).then_inc(u_hi, 1)
                else:
                    act.activation(halves_k[:, :, 0:3:2, :], unit[:, HL:2 * HL, :].unsqueeze(2).broadcast_to([P, HL, 2, DL]),
                                   ACT.Copy).then_inc(u_hi, 1)

            def stack(l, i, j, n):
                t = WINDOWS * l + 2 * i + j
                act.wait_ge(ta_made, TURNS * t + n + 1)
                if n == 0 and not is_first(i, j):
                    act.wait_ge(s_made, PAIRS * t)
                out = queries[:, 0:4, :] if n == 2 else keys[:, n, 0:4, j, :]
                act.activation(out, ps_ta[:].rearrange("p (h n) -> p h n", h=4), ACT.Copy).then_inc(ta_used, 1)

            def keep_values(l, i, j):
                t = WINDOWS * l + 2 * i + j
                act.wait_ge(v_made, t + 1)
                if not is_first(i, j):
                    act.wait_ge(o_made, t)
                act.activation(values[:, j].rearrange("p h d -> p (h d)"), ps_v[:], ACT.Copy).then_inc(v_kept, 1)

            def exponentials(l, i, j, p):
                t = WINDOWS * l + 2 * i + j
                act.wait_ge(max_ready, PAIRS * t + p + 1)
                if p >= 2:
                    act.wait_ge((ta_made, td_made)[p % 2], TURNS * t + 4)
                elif not is_first(i, j):
                    act.wait_ge((ta_made, td_made)[p % 2], TURNS * t)
                for h2 in range(2):
                    h = 2 * p + h2
                    ins = act.activation(prob[p % 2][:, h2, :], ps_s[:, p % 2, h2 * 2 * P:(h2 + 1) * 2 * P], ACT.Exp,
                                         bias=minus_max[:, h:h + 1], accum_out=row_sum[:, h:h + 1])
                ins.then_inc(exp_ready, 1)

            def turned_prob(l, i, j, p):
                t = WINDOWS * l + 2 * i + j
                act.wait_ge(ta_made, TURNS * t + 4 + p // 2)
                if p == 0 and not is_first(i, j):
                    act.wait_ge(o_made, t)
                if p == 2:
                    act.wait_ge(o_part, 2 * t + 1)
                act.activation(prob_t[0].rearrange("p h s n -> p (h s n)"), ps_ta[:], ACT.Copy).then_inc(ta_used, 1)

            def outputs_hi(l, i, j):
                t = WINDOWS * l + 2 * i + j
                act.wait_ge(o_made, t + 1)
                if not is_first(i, j):
                    act.wait_ge(y_made, t)
                act.activation(heads[:, HI].rearrange("p f n -> p (f n)"), ps_h[:], ACT.Copy).then_inc(o_hi, 1)

            def step(l, i, j, before=True, next1=True, next2=True):
                stack(l, i, j, 0)
                if before:
                    outputs_hi(l, *away(i, j, -1))
                stack(l, i, j, 1)
                keep_values(l, i, j)
                stack(l, i, j, 2)
                if next2:
                    project(l, *away(i, j, 2))
                if next1:
                    unit_hi(l, *away(i, j, 1), 1)
                exponentials(l, i, j, 0)
                exponentials(l, i, j, 1)
                turned_prob(l, i, j, 0)
                exponentials(l, i, j, 2)
                exponentials(l, i, j, 3)
                if next2:
                    squares(l, *away(i, j, 2), 1)
                turned_prob(l, i, j, 2)
                if next1:
                    unit_hi(l, *away(i, j, 1), 0)
                if next2:
                    squares(l, *away(i, j, 2), 0)

            def affine_tiles(l, i, j):
                t = CHUNKS * l + 2 * i + j
                for f in range(KE):
                    act.wait_ge(f_turned, KE * t + f + 1)
                    if not is_first(i, j):
                        act.wait_ge(f_lo, KE * t)
                    act.activation(affine[:, f, :], ps_ft[:, f, :], ACT.Identity, bias=gb[:, 1, f:f + 1],
                                   scale=gb[:, 0, f:f + 1]).then_inc(f_affine, 1)

            def hidden_hi(t, k, first):
                act.wait_ge(hid_ready, HT * t + k + 1)
                if k == 0 and not first:
                    act.wait_ge(f_made, 2 * t)
                act.activation(hid[:, HI, k, :], hidden[k % 2], ACT.Copy).then_inc(hid_hi, 1)

            def chunk(l, i, j, last=False):
                t = CHUNKS * l + 2 * i + j
                for k in range(HT):
                    act.wait_ge(g_made, HT * t + k + 1)
                    if not is_first(i, j) or k >= 2:
                        act.wait_ge(hid_ready, HT * t + k - 1)
                    act.activation(gate[k % 2], ps_ga[k % 2][0][:], ACT.Gelu, bias=b1_t[:, HT + k:HT + k + 1]).then_inc(gate_ready, 1)
                    if k:
                        hidden_hi(t, k - 1, is_first(i, j))
                hidden_hi(t, HT - 1, is_first(i, j))
                if not last:
                    affine_tiles(l, i + j, 1 - j)

            with act.Fori(0, DEPTH) as l:
                project(l, 0, 0)
                for s in (1, 0):
                    squares(l, 0, 0, s)
                project(l, 0, 1)
                for s in (1, 0):
                    unit_hi(l, 0, 0, s)
                for s in (1, 0):
                    squares(l, 0, 1, s)
                step(l, 0, 0, before=False)
                step(l, 0, 1)
                with act.Fori(1, WI - 1) as i:
                    for j in range(2):
                        step(l, i, j)
                step(l, WI - 1, 0, next2=False)
                step(l, WI - 1, 1, next1=False, next2=False)
                outputs_hi(l, WI - 1, 1)
                affine_tiles(l, 0, 0)
                for j in range(2):
                    chunk(l, 0, j)
                with act.Fori(1, CI - 1) as i:
                    for j in range(2):
                        chunk(l, i, j)
                chunk(l, CI - 1, 0)
                chunk(l, CI - 1, 1, last=True)

        @block.vector
        def _(dve):
            def split_weights(l, base, parts):
                at = 0
                for n, (dst, k, cols) in enumerate(parts):
                    raw = w_raw[:, at:at + k * cols].rearrange("p (k n) -> p k n", k=k)
                    at += k * cols
                    dve.tensor_copy(dst[:, HI], raw).then_inc(weights_split, 1)
                    dve.wait_ge(weights_split, 8 * l + base + 2 * n + 1)
                    dve.tensor_tensor(dst[:, LO], raw, dst[:, HI], ALU.subtract).then_inc(weights_split, 1)

            def project(l, i, j):
                t = WINDOWS * l + 2 * i + j
                dve.wait_ge(h_hi, t + 1)
                dve.tensor_tensor(ht[j][:, LO].rearrange("p f n -> p (f n)"), ps_h[:, 0:E],
                                  ht[j][:, HI].rearrange("p f n -> p (f n)"), ALU.subtract).then_inc(h_lo, 1)

            def norms(l, i, j, s):
                n = 2 * (WINDOWS * l + 2 * i + j) + 1 - s
                dve.wait_ge(sq_ready, n + 1)
                if not is_first(i, j):
                    dve.wait_ge(r_ready, n - 1)
                dve.tensor_reduce(side(norm2, s), side(square, s), AX.X, ALU.add).then_inc(norm_sum, 1)
                dve.wait_ge(norm_sum, n + 1)
                dve.tensor_scalar(side(norm2, s), side(norm2, s), 1e-24, None, ALU.max).then_inc(norm_ready, 1)

            def rotate(l, i, j, s):
                n = 2 * (WINDOWS * l + 2 * i + j) + 1 - s
                w = 2 * (i % 4) + j
                qk = ps_qk[:].rearrange("p s (h d) -> p s h d", h=HL)
                dve.wait_ge(sq_ready, n + 1)
                if not is_first(i, j):
                    dve.wait_ge(added, n - 1)
                half = DL // 2
                cos = rotary[:, w, s, 0, :].unsqueeze(1).broadcast_to([P, HL, DL])
                dve.tensor_tensor(straight[:, s], qk[:, s], cos, ALU.mult)
                for a in range(2):
                    mine, other = slice(a * half, (a + 1) * half), slice((1 - a) * half, (2 - a) * half)
                    sin = rotary[:, w, s, 1, mine].unsqueeze(1).broadcast_to([P, HL, half])
                    ins = dve.tensor_tensor(crossed[:, s, :, mine], qk[:, s, :, other], sin, ALU.mult)
                ins.then_inc(crossed_ready, 1)

            def stack(l, i, j, n):
                t = WINDOWS * l + 2 * i + j
                dve.wait_ge(td_made, TURNS * t + n + 1)
                if n == 0 and not is_first(i, j):
                    dve.wait_ge(s_made, PAIRS * t)
                out = queries[:, 4:8, :] if n == 2 else keys[:, n, 4:8, j, :]
                dve.tensor_copy(out, ps_td[:].rearrange("p (h n) -> p h n", h=4)).then_inc(td_used, 1)

            def maxima(t, p):
                dve.wait_ge(s_made, PAIRS * t + p + 1)
                dve.tensor_reduce(minus_max[:, 2 * p:2 * p + 2], ps_s[:, p % 2, :].rearrange("p (h n) -> p h n", h=2),
                                  AX.X, ALU.max, negate=True).then_inc(max_ready, 1)

            def normalise(t, p):
                dve.wait_ge(exp_ready, PAIRS * t + p + 1)
                dve.reciprocal(row_inv[:, 2 * p:2 * p + 2], row_sum[:, 2 * p:2 * p + 2]).then_inc(inv_ready, 1)
                dve.wait_ge(inv_ready, PAIRS * t + p + 1)
                for h2 in range(2):
                    h = 2 * p + h2
                    ins = dve.tensor_scalar(prob[p % 2][:, h2, :], prob[p % 2][:, h2, :], row_inv[:, h:h + 1], None, ALU.mult)
                ins.then_inc(p_ready, 1)

            def turned_prob(t, p, skip):
                dve.wait_ge(td_made, TURNS * t + 4 + p // 2)
                if p == 1 and not skip:
                    dve.wait_ge(o_made, t)
                if p == 3:
                    dve.wait_ge(o_part, 2 * t + 2)
                dve.tensor_copy(prob_t[1].rearrange("p h s n -> p (h s n)"), ps_td[:]).then_inc(td_used, 1)

            def outputs_lo(l, i, j):
                t = WINDOWS * l + 2 * i + j
                dve.wait_ge(o_hi, t + 1)
                dve.tensor_tensor(heads[:, LO].rearrange("p f n -> p (f n)"), ps_h[:],
                                  heads[:, HI].rearrange("p f n -> p (f n)"), ALU.subtract).then_inc(o_lo, 1)

            def add_residual(l, i, j):
                t = WINDOWS * l + 2 * i + j
                dve.wait_ge(y_made, t + 1)
                dve.wait_ge(res_in[j], 16 * (WI * l + i + 1))
                if not is_window(i, j, 0, 1):
                    dve.wait_ge(mid_out[j], 16 * (WI * l + i))
                dve.tensor_tensor(mid[j], ps_v[:, 0:E], res[j], ALU.add).then_inc(y_ready, 1)

            def step(l, i, j, before=True, next1=True, next2=True):
                t = WINDOWS * l + 2 * i + j
                stack(l, i, j, 0)
                if next1:
                    norms(l, *away(i, j, 1), 0)
                stack(l, i, j, 1)
                if before:
                    outputs_lo(l, *away(i, j, -1))
                stack(l, i, j, 2)
                if next2:
                    project(l, *away(i, j, 2))
                if before:
                    add_residual(l, *away(i, j, -1))
                maxima(t, 0)
                maxima(t, 1)
                normalise(t, 0)
                normalise(t, 1)
                maxima(t, 2)
                turned_prob(t, 1, is_first(i, j))
                maxima(t, 3)
                normalise(t, 2)
                if next1:
                    rotate(l, *away(i, j, 1), 0)
                normalise(t, 3)
                if next2:
                    rotate(l, *away(i, j, 2), 1)
                    norms(l, *away(i, j, 2), 1)
                turned_prob(t, 3, is_first(i, j))

            def layer_norm(l, i, j):
                t = CHUNKS * l + 2 * i + j
                dve.wait_ge(f_in[j], 32 * (CI * l + i + 1))
                for q in range(CT):
                    dve.bn_stats(stats[:, q, :], fin[j][:, q, :]).then_inc(f_stats, 1)
                dve.wait_ge(f_stats, CT * (t + 1))
                dve.sem_inc(f_counted, 1)
                for q in range(CT):
                    dve.bn_aggr(mean_var[:, q, :], stats[:, q, :]).then_inc(f_aggr, 1)
                dve.wait_ge(f_aggr, CT * (t + 1))
                dve.tensor_scalar(var_eps, mean_var[:, :, 1], EPS, None, ALU.add).then_inc(f_var, 1)
                dve.wait_ge(f_rstd, t + 1)
                for q in range(CT):
                    ins = dve.tensor_scalar(fin[j][:, q, :], fin[j][:, q, :], mean_var[:, q, 0:1], rstd[:, q:q + 1],
                                            ALU.subtract, ALU.mult)
                ins.then_inc(f_norm, 1)

            def split_input(l, i, j):
                t = CHUNKS * l + 2 * i + j
                for f in range(KE):
                    dve.wait_ge(f_affine, KE * t + f + 1)
                    dve.tensor_copy(ft[:, HI, f, :], affine[:, f, :]).then_inc(f_hi, 1)

            def chunk(l, i, j, last=False):
                t = CHUNKS * l + 2 * i + j
                if not last:
                    layer_norm(l, i + j, 1 - j)
                for k in range(HT):
                    dve.wait_ge(a_made, HT * t + k + 1)
                    dve.wait_ge(gate_ready, HT * t + k + 1)
                    if not is_first(i, j) or k >= 2:
                        dve.wait_ge(hid_lo, HT * t + k - 1)
                    dve.scalar_tensor_tensor(out=hidden[k % 2], in0=ps_ga[k % 2][1][:], scalar=b1_t[:, k:k + 1],
                                             in1=gate[k % 2], op0=ALU.add, op1=ALU.mult).then_inc(hid_ready, 1)
                if not last:
                    split_input(l, i + j, 1 - j)
                dve.wait_ge(f_res, t + 1)
                if not (isinstance(i, int) and i == 0):
                    dve.wait_ge(f_out[j], 16 * (CI * l + i))
                for half in range(2):
                    dve.wait_ge(f_made, 2 * t + half + 1)
                    dve.tensor_tensor(fout[j][:, 2 * half:2 * half + 2, :], ps_out[:, half, :].rearrange("p (q e) -> p q e", q=2),
                                      fres[j][:, 2 * half:2 * half + 2, :], ALU.add).then_inc(f_ready, 1)

            dve.wait_ge(const_made, 5)
            both = lambda tile: tile[:].unsqueeze(1).broadcast_to([P, 2, P])
            dve.memset(mask_even[:, 0, :, 1, :], NEG).then_inc(masks_made, 1)
            for g in range(4):
                dve.tensor_copy(mask_even[:, g, :, 0, :], both(own_mask))
                if g:
                    dve.tensor_copy(mask_even[:, g, :, 1, :], both(before_mask))
            dve.tensor_copy(mask_odd[:, :, 0, :], both(before_mask)).then_inc(masks_made, 1)
            dve.tensor_copy(mask_odd[:, :, 1, :], both(own_mask)).then_inc(masks_made, 1)
            dve.memset(keys[:, :, :, 1, :].bitcast(F32), 0.0).then_inc(masks_made, 1)
            dve.memset(values[:, 1], 0.0).then_inc(masks_made, 1)
            dve.wait_ge(trig_in, 16)
            with dve.Fori(0, DEPTH) as l:
                dve.wait_ge(weights_in, (QKV_IN + MLP_IN) * l + QKV_IN)
                split_weights(l, 0, ((wqkv_s, KE, 3 * INNER), (wo_s, PAIRS, E)))
                dve.tensor_tensor(rotary[:].rearrange("p w s c d -> p w (s c) d"), trig_t[:],
                                  scale_t[:].unsqueeze(1).broadcast_to([P, PER_BATCH, 4, DL]), ALU.mult).then_inc(trig_scaled, 1)
                dve.wait_ge(trig_scaled, l + 1)
                project(l, 0, 0)
                for s in (1, 0):
                    rotate(l, 0, 0, s)
                    norms(l, 0, 0, s)
                project(l, 0, 1)
                rotate(l, 0, 1, 1)
                norms(l, 0, 1, 1)
                step(l, 0, 0, before=False)
                for m in range(1, 4):
                    step(l, m // 2, m % 2)
                with dve.Fori(2, WI - 1) as i:
                    for j in range(2):
                        step(l, i, j)
                step(l, WI - 1, 0, next2=False)
                step(l, WI - 1, 1, next1=False, next2=False)
                outputs_lo(l, WI - 1, 1)
                add_residual(l, WI - 1, 1)
                dve.wait_ge(weights_in, (QKV_IN + MLP_IN) * (l + 1))
                split_weights(l, 4, ((w1_s, KE, 2 * HIDP), (w2_s, HT, E)))
                layer_norm(l, 0, 0)
                split_input(l, 0, 0)
                for j in range(2):
                    chunk(l, 0, j)
                with dve.Fori(1, CI - 1) as i:
                    for j in range(2):
                        chunk(l, i, j)
                chunk(l, CI - 1, 0)
                chunk(l, CI - 1, 1, last=True)


def finish(nc, ctx, tensor, psum, sem, x, layer_in, attn_out, ident, wout_s, out):
    ain = [tensor(ctx, f"ain{j}", [P, CT, E]) for j in range(2)]
    xres = [tensor(ctx, f"xres{j}", [P, CT, E]) for j in range(2)]
    lres = [tensor(ctx, f"lres{j}", [P, CT, E]) for j in range(2)]
    at = [tensor(ctx, f"at{j}", [P, 2, KE, CHUNK], F32R) for j in range(2)]
    ps_at = psum(ctx, "ps_at", [P, KE, CHUNK])
    ps_y = psum(ctx, "ps_y", [P, 2, 2, E])
    a_in, r_in, stored = ([sem(f"o_{n}{j}") for j in range(2)] for n in ("a_in", "r_in", "stored"))
    turned, hi, lo, added, made, ready = (sem("o_" + n) for n in ("turned", "hi", "lo", "added", "made", "ready"))

    with nc.Block() as block:

        @block.sync
        def _(sp):
            def load(i, j):
                rows = slice(j * CHUNK, (j + 1) * CHUNK)
                sp.dma_start(ain[j][:], attn_out[bass.ds(2 * CT * i + CT * j, CT)].rearrange("q p e -> p q e")).then_inc(a_in[j], 16)
                sp.dma_start(xres[j][:], x[i, rows, :].rearrange("(q p) e -> p q e", p=P)).then_inc(r_in[j], 16)
                sp.dma_start(lres[j][:], layer_in[DEPTH, i, 1 + j * CHUNK:1 + (j + 1) * CHUNK, :]
                             .rearrange("(q p) e -> p q e", p=P)).then_inc(r_in[j], 16)

            def store(i, j):
                sp.wait_ge(ready, 2 * (2 * i + j + 1))
                sp.dma_start(out[i, j * CHUNK:(j + 1) * CHUNK, :].rearrange("(q p) e -> p q e", p=P), xres[j][:]).then_inc(stored[j], 16)

            for j in range(2):
                load(0, j)
            with sp.Fori(0, B - 1) as i:
                for j in range(2):
                    store(i, j)
                    sp.wait_ge(stored[j], 16 * (i + 1))
                    load(i + 1, j)
            for j in range(2):
                store(B - 1, j)
            for j in range(2):
                sp.wait_ge(stored[j], 16 * B)

        @block.gpsimd
        def _(pool):
            with pool.Fori(0, B) as i:
                for j in range(2):
                    pool.wait_ge(r_in[j], 32 * (i + 1))
                    pool.tensor_tensor(xres[j][:], xres[j][:], lres[j][:], ALU.add).then_inc(added, 1)

        @block.tensor
        def _(pe):
            with pe.Fori(0, B) as i:
                for j in range(2):
                    c = 2 * i + j
                    pe.wait_ge(a_in[j], 16 * (i + 1))
                    pe.wait_ge(lo, KE * c)
                    for f in range(KE):
                        for q in range(CT):
                            mm = pe.transpose(ps_at[:, f, q * P:(q + 1) * P], ain[j][:, q, f * P:(f + 1) * P], ident[:])
                        mm.then_inc(turned, 1)
                    pe.wait_ge(lo, KE * (c + 1))
                    pe.wait_ge(ready, 2 * c)
                    for q in range(CT):
                        mm = products(pe, ps_y[:, q // 2, q % 2, :], lambda part, f: at[j][:, part, f, q * P:(q + 1) * P],
                                      lambda part, f: wout_s[:, part, f, :], KE)
                        if q % 2:
                            mm.then_inc(made, 1)

        @block.scalar
        def _(act):
            with act.Fori(0, B) as i:
                for j in range(2):
                    c = 2 * i + j
                    for f in range(KE):
                        act.wait_ge(turned, KE * c + f + 1)
                        act.wait_ge(made, 4 * i)
                        act.activation(at[j][:, HI, f, :], ps_at[:, f, :], ACT.Copy).then_inc(hi, 1)

        @block.vector
        def _(dve):
            with dve.Fori(0, B) as i:
                for j in range(2):
                    c = 2 * i + j
                    for f in range(KE):
                        dve.wait_ge(hi, KE * c + f + 1)
                        dve.tensor_tensor(at[j][:, LO, f, :], ps_at[:, f, :], at[j][:, HI, f, :], ALU.subtract).then_inc(lo, 1)
                    dve.wait_ge(added, c + 1)
                    for half in range(2):
                        dve.wait_ge(made, 2 * c + half + 1)
                        dve.tensor_tensor(xres[j][:, 2 * half:2 * half + 2, :], ps_y[:, half], xres[j][:, 2 * half:2 * half + 2, :],
                                          ALU.add).then_inc(ready, 1)


def rotary_constants():
    import numpy as np
    half_idx = np.arange(0, DL, 2, dtype=np.float32)
    inv_freq = 1.0 / np.float32(10000.0) ** (half_idx / np.float32(DL))
    t = np.arange(T, dtype=np.float32)
    freqs = t[:, None] * inv_freq[None, :]
    freqs = np.concatenate([freqs, freqs], axis=-1)
    base = (half_idx + np.float32(0.4 * DL)) / np.float32(1.4 * DL)
    power = (t - T // 2) / np.float32(P // 2)
    scale = base[None, :] ** power[:, None]
    scale = np.concatenate([scale, scale], axis=-1)
    sign = np.where(np.arange(DL) < DL // 2, np.float32(-1), np.float32(1))
    cos, sin = np.cos(freqs), np.sin(freqs) * sign
    tables = np.stack([cos * scale * 8, sin * scale * 8, cos / scale, sin / scale], axis=1).astype(np.float32)
    return np.ascontiguousarray(tables.reshape(PER_BATCH, P, 4, DL).transpose(1, 0, 2, 3))


def kernel(L0_attn_query, L0_attn_key, L0_attn_value, L0_attn_in_proj_weight, L0_attn_out_proj_weight,
           L0_ffn_wqkv, L0_ffn_q_scale, L0_ffn_k_scale, L0_ffn_wo, L0_ffn_ln_g, L0_ffn_ln_b,
           L0_ffn_w1, L0_ffn_b1, L0_ffn_w2, L0_ffn_b2):
    import numpy as np
    import concourse.bacc as bacc
    from concourse.bass_utils import run_bass_kernel_spmd

    def padded(a, axis):
        widths = [(0, 0)] * a.ndim
        widths[axis] = (0, HIDP - HID)
        return np.pad(a, widths)

    def on_partitions(a, tiles):
        return a.reshape(DEPTH, tiles, P).transpose(0, 2, 1)

    def repeated(a):
        return np.broadcast_to(a[:, None], (DEPTH, P) + a.shape[1:])

    w1, b1 = np.asarray(L0_ffn_w1), np.asarray(L0_ffn_b1)
    qs, ks = np.asarray(L0_ffn_q_scale), np.asarray(L0_ffn_k_scale)
    swap = np.r_[DL // 2:DL, 0:DL // 2]
    arrays = {
        "x": np.asarray(L0_attn_query),
        "w_in": np.asarray(L0_attn_in_proj_weight).T,
        "w_out": np.asarray(L0_attn_out_proj_weight).T,
        "w_qkv": np.asarray(L0_ffn_wqkv),
        "w_o": np.asarray(L0_ffn_wo),
        "w1": np.concatenate([padded(w1[..., :HID], 2), padded(w1[..., HID:], 2)], axis=2),
        "w2": padded(np.asarray(L0_ffn_w2), 1),
        "ln_gb": np.stack([on_partitions(np.asarray(L0_ffn_ln_g), KE), on_partitions(np.asarray(L0_ffn_ln_b), KE)], axis=2),
        "b1": np.concatenate([on_partitions(padded(b1[:, :HID], 1), HT), on_partitions(padded(b1[:, HID:], 1), HT)], axis=2),
        "b2": repeated(np.asarray(L0_ffn_b2)),
        "qk_scale": repeated(np.stack([qs, qs[:, swap], ks, ks[:, swap]], axis=1)),
        "trig": rotary_constants(),
    }
    nc = bacc.Bacc("TRN2", target_bir_lowering=False, num_devices=1)
    aps = {}
    for name, a in arrays.items():
        arrays[name] = np.ascontiguousarray(a)
        aps[name] = nc.dram_tensor("in_" + name, a.shape, mybir.dt.from_np(a.dtype), kind="ExternalInput").ap()
    aps["out"] = nc.dram_tensor("out_0", (B, T, E), F32, kind="ExternalOutput").ap()
    build(nc, **aps)
    r = run_bass_kernel_spmd(nc, [{"in_" + name: a for name, a in arrays.items()}], core_ids=[0])
    return r.results[0]["out_0"]
```

```python
from contextlib import ExitStack

import concourse.bass as bass
from concourse import mybir

F32 = mybir.dt.float32
F32R = mybir.dt.float32r
BF16 = mybir.dt.bfloat16
ALU = mybir.AluOpType
ACT = mybir.ActivationFunctionType
AX = mybir.AxisListType

P = 128
B, T, E = 4, 1024, 256
TILES = B * T // P
CHUNK = 512
CT = CHUNK // P
CHUNKS = B * T // CHUNK
KE = E // P
EPS = 1e-5
NEG = -3e38

HC, DC = 16, 16
UNITS = B * HC
KT = T // P
STACK = 4 * DC
KROWS = 96
VW = 32

DEPTH, HL, DL = 2, 8, 64
INNER = HL * DL
HID = 682
HT = 6
HIDP = HT * P
HI, LO = 0, 1
PRODUCTS = ((HI, HI), (HI, LO), (LO, HI))


class Chain:

    def __init__(self, engine, sem, base=0):
        self.engine, self.sem, self.base, self.n = engine, sem, base, 0

    def add(self, instruction):
        instruction.then_inc(self.sem, 1)
        self.n += 1

    def wait(self):
        self.engine.wait_ge(self.sem, self.base + self.n)


def build(nc, x, w_in, w_out, w_qkv, w_o, w1, w2, ln_gb, b1, b2, qk_scale, trig, out):
    layer_in = nc.dram_tensor("layer_in", (DEPTH + 1, B, 1 + T, E), F32, kind="Internal").ap()
    layer_mid = nc.dram_tensor("layer_mid", (DEPTH, B, 1 + T, E), F32, kind="Internal").ap()
    q_parts = nc.dram_tensor("q_parts", (UNITS, 2 * DC, T), F32, kind="Internal").ap()
    k_parts = nc.dram_tensor("k_parts", (UNITS, 2 * DC, T), F32, kind="Internal").ap()
    neg_max = nc.dram_tensor("neg_max", (4, 2, T), F32, kind="Internal").ap()
    attn_out = nc.dram_tensor("attn_out", (TILES, P, E), F32, kind="Internal").ap()

    with ExitStack() as top:
        def tensor(ctx, name, shape, dt=F32):
            return ctx.enter_context(nc.sbuf_tensor(name, shape, dt))

        def psum(ctx, name, shape):
            return ctx.enter_context(nc.psum_tensor(name, shape, F32))

        def sem(name):
            return top.enter_context(nc.semaphore(name))

        ident = tensor(top, "ident", [P, P])
        ident_bf = tensor(top, "ident_bf", [P, P], BF16)
        wout_s = tensor(top, "wout_s", [P, 2, KE, E], F32R)
        w_raw = tensor(top, "lw_raw", [P, KE * 3 * INNER + HT * E])
        weights_in = sem("l_weights_in")

        with ExitStack() as ctx:
            values = tensor(ctx, "values", [P, UNITS, KT, DC])
            zeros = tensor(ctx, "zeros", [12, T])
            causal_qk = tensor(ctx, "causal_qk", [P, P], BF16)
            causal_kq = tensor(ctx, "causal_kq", [P, P], BF16)
            with ExitStack() as inner:
                win_s = tensor(inner, "win_s", [P, 2, KE, 3 * E], F32R)
                project(nc, inner, tensor, psum, sem, x, w_in, w_out, layer_in, layer_mid, q_parts, k_parts,
                        ident, ident_bf, causal_qk, causal_kq, zeros, win_s, wout_s, values)
            with ExitStack() as inner:
                attend(nc, inner, tensor, psum, sem, w_qkv, w_o, w_raw, weights_in, q_parts, k_parts, neg_max, attn_out,
                       ident, ident_bf, causal_qk, causal_kq, zeros, values)
        with ExitStack() as ctx:
            local_layers(nc, ctx, tensor, psum, sem, w_raw, weights_in, layer_in, layer_mid, w_qkv, w_o, w1, w2, ln_gb, b1, b2,
                         qk_scale, trig, ident, ident_bf)
        with ExitStack() as ctx:
            finish(nc, ctx, tensor, psum, sem, x, layer_in, attn_out, ident, wout_s, out)


def is_zero(n):
    return isinstance(n, int) and n == 0


def project(nc, ctx, tensor, psum, sem, x, w_in, w_out, layer_in, layer_mid, q_parts, k_parts,
            ident, ident_bf, causal_qk, causal_kq, zeros, win_s, wout_s, values):
    w_raw = tensor(ctx, "w_raw", [P, KE, 4 * E])
    xin = [tensor(ctx, f"xin{j}", [P, CT, E]) for j in range(2)]
    xn = [tensor(ctx, f"xn{j}", [P, CT, E]) for j in range(2)]
    stats = tensor(ctx, "stats", [P, CT, 6])
    mean_var = tensor(ctx, "mean_var", [P, CT, 2])
    var_eps = tensor(ctx, "var_eps", [P, CT])
    rstd = tensor(ctx, "rstd", [P, CT])
    minus_half = tensor(ctx, "minus_half", [P, CT])
    xt = [tensor(ctx, f"xt{j}", [P, 2, KE, CHUNK], F32R) for j in range(2)]
    qk = [tensor(ctx, f"qk{j}", [P, 2, 4, CHUNK], F32R) for j in range(2)]
    ps_xt = psum(ctx, "ps_xt", [P, KE, CHUNK])
    ps_qk = psum(ctx, "ps_qk", [P, 4, CHUNK])
    ps_v = psum(ctx, "ps_v", [P, 2, 2, E])

    const_made = sem("p_const_made")
    w_loaded = sem("p_w_loaded")
    zero_rows = sem("p_zero_rows")
    w_split = sem("p_w_split")
    x_loaded = [sem(f"p_x_loaded{j}") for j in range(2)]
    dve_own = sem("p_dve_own")
    counted = sem("p_counted")
    var_ready = sem("p_var_ready")
    rstd_ready = sem("p_rstd_ready")
    xn_ready = sem("p_xn_ready")
    xn_stored = [sem(f"p_xn_stored{j}") for j in range(2)]
    xt_made = sem("p_xt_made")
    xt_hi = sem("p_xt_hi")
    xt_lo = sem("p_xt_lo")
    qk_made = sem("p_qk_made")
    qk_hi = sem("p_qk_hi")
    qk_lo = sem("p_qk_lo")
    v_made = sem("p_v_made")
    v_kept = sem("p_v_kept")
    qk_stored = [sem(f"p_qk_stored{j}") for j in range(2)]
    DVE_LN = 2 * CT

    with nc.Block() as block:

        @block.gpsimd
        def _(pool):
            for t in (ident, ident_bf, causal_qk, causal_kq, zeros):
                pool.memset(t[:], 0.0).then_inc(const_made, 1)
            pool.memset(minus_half[:], -0.5).then_inc(const_made, 1)
            pool.wait_ge(const_made, 6)
            for t in (ident, ident_bf):
                pool.affine_select(out=t[:], in_=t[:], compare_op=ALU.not_equal, fill=1.0, base=0,
                                   pattern=[[-1, P]], channel_multiplier=1).then_inc(const_made, 1)
            pool.affine_select(out=causal_qk[:], in_=causal_qk[:], compare_op=ALU.is_ge, fill=NEG, base=0,
                               pattern=[[-1, P]], channel_multiplier=1).then_inc(const_made, 1)
            pool.affine_select(out=causal_kq[:], in_=causal_kq[:], compare_op=ALU.is_ge, fill=NEG, base=0,
                               pattern=[[1, P]], channel_multiplier=-1).then_inc(const_made, 1)
            with pool.Fori(0, CHUNKS) as c:
                pool.wait_ge(var_ready, c + 1)
                pool.tensor_tensor(rstd[:], var_eps[:], minus_half[:], ALU.pow).then_inc(rstd_ready, 1)

        @block.sync
        def _(sp):
            sp.dma_start(w_raw[:, :, 0:3 * E], w_in.rearrange("(k p) n -> p k n", p=P)).then_inc(w_loaded, 16)
            sp.dma_start(w_raw[:, :, 3 * E:4 * E], w_out.rearrange("(k p) n -> p k n", p=P)).then_inc(w_loaded, 16)
            sp.wait_ge(const_made, 6)
            sp.dma_start(layer_in[:, :, 0:1, :].rearrange("l b r e -> (l b r) e"), zeros[0:12, 0:E]).then_inc(zero_rows, 16)
            sp.dma_start(layer_mid[:, :, 0:1, :].rearrange("l b r e -> (l b r) e"), zeros[0:8, 0:E]).then_inc(zero_rows, 16)

            def load_x(i, j):
                b, half = i, j
                sp.dma_start(xin[j][:], x[b, half * CHUNK:(half + 1) * CHUNK, :]
                             .rearrange("(q p) e -> p q e", p=P)).then_inc(x_loaded[j], 16)

            def store_xn(i, j):
                sp.wait_ge(xn_ready, 2 * i + j + 1)
                sp.dma_start(layer_in[0, i, 1 + j * CHUNK:1 + (j + 1) * CHUNK, :]
                             .rearrange("(q p) e -> p q e", p=P), xn[j][:]).then_inc(xn_stored[j], 16)

            def store_qk(i, j):
                for m in range(4):
                    dst, h0 = (q_parts, k_parts)[m // 2], i * HC + m % 2 * (HC // 2)
                    for part in (HI, LO):
                        sp.wait_ge((qk_hi, qk_lo)[part], 4 * (2 * i + j) + m + 1)
                        sp.dma_start(dst[bass.ds(h0, HC // 2), part * DC:(part + 1) * DC, j * CHUNK:(j + 1) * CHUNK],
                                     qk[j][:, part, m, :].bitcast(F32)).then_inc(qk_stored[j], 16)

            for j in range(2):
                load_x(0, j)
            with sp.Fori(0, B - 1) as i:
                for j in range(2):
                    store_xn(i, j)
                    load_x(i + 1, j)
                    store_qk(i, j)
            for j in range(2):
                store_xn(B - 1, j)
                store_qk(B - 1, j)
            sp.wait_ge(zero_rows, 32)
            for j in range(2):
                sp.wait_ge(xn_stored[j], 16 * B)
                sp.wait_ge(qk_stored[j], 8 * 16 * B)

        @block.vector
        def _(dve):
            dve.wait_ge(w_loaded, 32)
            dve.tensor_copy(win_s[:, HI], w_raw[:, :, 0:3 * E]).then_inc(w_split, 1)
            dve.tensor_copy(wout_s[:, HI], w_raw[:, :, 3 * E:4 * E]).then_inc(w_split, 1)
            dve.wait_ge(w_split, 2)
            dve.tensor_tensor(win_s[:, LO], w_raw[:, :, 0:3 * E], win_s[:, HI], ALU.subtract).then_inc(w_split, 1)
            dve.tensor_tensor(wout_s[:, LO], w_raw[:, :, 3 * E:4 * E], wout_s[:, HI], ALU.subtract).then_inc(w_split, 1)

            def normalise(i, j):
                c = 2 * i + j
                own = Chain(dve, dve_own, c * DVE_LN)
                dve.wait_ge(x_loaded[j], 16 * (i + 1))
                for q in range(CT):
                    own.add(dve.bn_stats(stats[:, q, :], xin[j][:, q, :]))
                own.wait()
                dve.sem_inc(counted, 1)
                for q in range(CT):
                    own.add(dve.bn_aggr(mean_var[:, q, :], stats[:, q, :]))
                own.wait()
                dve.tensor_scalar(var_eps[:], mean_var[:, :, 1], EPS, None, ALU.add).then_inc(var_ready, 1)
                dve.wait_ge(rstd_ready, c + 1)
                if not is_zero(i):
                    dve.wait_ge(xn_stored[j], 16 * i)
                if not is_zero(c):
                    dve.wait_ge(xt_made, 2 * c)
                for q in range(CT):
                    last = dve.tensor_scalar(xn[j][:, q, :], xin[j][:, q, :], mean_var[:, q, 0:1], rstd[:, q:q + 1],
                                             ALU.subtract, ALU.mult)
                last.then_inc(xn_ready, 1)

            def split_x(i, j):
                c = 2 * i + j
                for f in range(KE):
                    dve.wait_ge(xt_hi, KE * c + f + 1)
                    dve.tensor_tensor(xt[j][:, LO, f, :], ps_xt[:, f, :], xt[j][:, HI, f, :], ALU.subtract).then_inc(xt_lo, 1)

            def split_qk(i, j):
                c = 2 * i + j
                for m in range(4):
                    dve.wait_ge(qk_hi, 4 * c + m + 1)
                    if not is_zero(i):
                        dve.wait_ge(qk_stored[j], 128 * i)
                    dve.scalar_tensor_tensor(out=qk[j][:, LO, m, :], in0=ps_qk[:, m, :], scalar=DC ** -0.5 if m < 2 else 1.0,
                                             in1=qk[j][:, HI, m, :], op0=ALU.mult, op1=ALU.subtract).then_inc(qk_lo, 1)

            def step(i, j, last=False):
                split_x(i, j)
                if not last:
                    normalise(i + j, 1 - j)
                split_qk(i, j)

            normalise(0, 0)
            for j in range(2):
                step(0, j)
            with dve.Fori(1, B - 1) as i:
                for j in range(2):
                    step(i, j)
            step(B - 1, 0)
            step(B - 1, 1, last=True)

        @block.scalar
        def _(act):
            def x_hi(i, j):
                c = 2 * i + j
                for f in range(KE):
                    act.wait_ge(xt_made, KE * c + f + 1)
                    act.activation(xt[j][:, HI, f, :], ps_xt[:, f, :], ACT.Copy).then_inc(xt_hi, 1)

            def parts_hi(i, j):
                c = 2 * i + j
                if not is_zero(i):
                    act.wait_ge(qk_stored[j], 128 * i)
                for m in range(4):
                    act.wait_ge(qk_made, 4 * c + m + 1)
                    act.activation(qk[j][:, HI, m, :], ps_qk[:, m, :], ACT.Copy, scale=DC ** -0.5 if m < 2 else 1.0).then_inc(qk_hi, 1)

            def keep_values(i, j):
                c = 2 * i + j
                for v in range(2):
                    act.wait_ge(v_made, 2 * c + v + 1)
                    kt0 = CT * j + 2 * v
                    act.activation(values[:, bass.ds(i * HC, HC), kt0:kt0 + 2, :].rearrange("p h t d -> p t h d"),
                                   ps_v[:, v].rearrange("p t (h d) -> p t h d", h=HC), ACT.Copy).then_inc(v_kept, 1)

            def step(i, j, last=False):
                parts_hi(i, j)
                if not last:
                    x_hi(i + j, 1 - j)
                keep_values(i, j)

            x_hi(0, 0)
            for j in range(2):
                step(0, j)
            with act.Fori(1, B - 1) as i:
                for j in range(2):
                    step(i, j)
            step(B - 1, 0)
            step(B - 1, 1, last=True)

        @block.tensor
        def _(pe):
            pe.wait_ge(const_made, 10)
            pe.wait_ge(w_split, 4)

            def turn_x(i, j):
                c = 2 * i + j
                pe.wait_ge(xn_ready, c + 1)
                if not is_zero(c):
                    pe.wait_ge(xt_lo, KE * c)
                for f in range(KE):
                    for q in range(CT):
                        mm = pe.transpose(ps_xt[:, f, q * P:(q + 1) * P], xn[j][:, q, f * P:(f + 1) * P], ident[:])
                    mm.then_inc(xt_made, 1)

            def project_qk(i, j):
                c = 2 * i + j
                pe.wait_ge(xt_lo, KE * c + KE)
                if not is_zero(c):
                    pe.wait_ge(qk_lo, 4 * c)
                for m in range(4):
                    products(pe, ps_qk[:, m, :], lambda part, f: win_s[:, part, f, m * P:(m + 1) * P],
                             lambda part, f: xt[j][:, part, f, :], KE).then_inc(qk_made, 1)

            def project_v(i, j):
                c = 2 * i + j
                if not is_zero(c):
                    pe.wait_ge(v_kept, 2 * c)
                for q in range(CT):
                    mm = products(pe, ps_v[:, q // 2, q % 2, :], lambda part, f: xt[j][:, part, f, q * P:(q + 1) * P],
                                  lambda part, f: win_s[:, part, f, 2 * E:3 * E], KE)
                    if q % 2:
                        mm.then_inc(v_made, 1)

            def step(i, j, last=False):
                project_qk(i, j)
                if not last:
                    turn_x(i + j, 1 - j)
                project_v(i, j)

            turn_x(0, 0)
            for j in range(2):
                step(0, j)
            with pe.Fori(1, B - 1) as i:
                for j in range(2):
                    step(i, j)
            step(B - 1, 0)
            step(B - 1, 1, last=True)


def products(pe, out, stationary, moving, tiles):
    steps = [(f, a, b) for f in range(tiles) for a, b in PRODUCTS]
    for n, (f, a, b) in enumerate(steps):
        mm = pe.matmul(out, stationary(a, f), moving(b, f), start=n == 0, stop=n == len(steps) - 1)
    return mm


PIECES = [(t, k0, min(CHUNK, (t + 1) * P - k0)) for t in range(KT) for k0 in range(0, (t + 1) * P, CHUNK)]
PIECES_AT = (3, 2, 3, 2, 1, 1, 0, 0)
AHEAD = 2
RING = 4
MAXIMUM_SLOTS = len(PIECES) + 1
SLOTS = MAXIMUM_SLOTS + 2


def first_slot(i, j):
    n = AHEAD * MAXIMUM_SLOTS - 2 + SLOTS * j
    if isinstance(i, int) and i == 0 and j == 0:
        n += 2
    if isinstance(i, int) and i == UNITS // RING - 1 and j > RING - AHEAD:
        n -= MAXIMUM_SLOTS * (j - (RING - AHEAD))
    return SLOTS * RING * i + n, n % 2


def uses(i, j):
    ahead = not (isinstance(i, int) and i == UNITS // RING - 1 and j >= RING - AHEAD)
    outputs = not (isinstance(i, int) and i == 0 and j == 0)
    listed, k = [], 0
    for kt in range(KT):
        if ahead:
            listed += [(kt, "piece", k + n) for n in range(PIECES_AT[kt])]
            k += PIECES_AT[kt]
    if outputs:
        listed += [(KT - 1, "output", c) for c in range(2)]
    if ahead:
        listed.append((KT - 1, "maxima", 0))
    return listed


def load_qkv_weights(sp, l, w_qkv, w_o, w_raw, weights_in):
    qkv = KE * 3 * INNER
    sp.dma_start(w_raw[:, 0:qkv].rearrange("p (k n) -> p k n", k=KE),
                 w_qkv[l].rearrange("(k p) n -> p k n", p=P)).then_inc(weights_in, 16)
    sp.dma_start(w_raw[:, qkv:qkv + PAIRS * E].rearrange("p (k n) -> p k n", k=PAIRS),
                 w_o[l].rearrange("(k p) n -> p k n", p=P)).then_inc(weights_in, 16)


def attend(nc, ctx, tensor, psum, sem, w_qkv, w_o, w_raw, weights_in, q_parts, k_parts, neg_max, attn_out,
           ident, ident_bf, causal_qk, causal_kq, zeros, values):
    qs = [tensor(ctx, f"qs{j}", [KROWS, T], F32R) for j in range(RING)]
    ks = [tensor(ctx, f"ks{j}", [KROWS, T], F32R) for j in range(RING)]
    vs = [tensor(ctx, f"vs{j}", [P, KT, VW]) for j in range(RING)]
    prob_a = tensor(ctx, "prob_a", [P, 4, T])
    prob_b = tensor(ctx, "prob_b", [P, 4, CHUNK])
    maxima = [tensor(ctx, f"maxima{j}", [P, KT + 4]) for j in range(2)]
    max_parts = [tensor(ctx, f"max_parts{j}", [KT, 2, P], F32R) for j in range(RING)]
    sums = [tensor(ctx, f"sums{j}", [P, T]) for j in range(2)]
    folded = tensor(ctx, "folded", [P, 2, CT, VW])
    rsum = tensor(ctx, "rsum", [P, KT])
    minus_one = tensor(ctx, "minus_one", [P, KT])
    minus_max = [tensor(ctx, f"minus_max{j}", [KT, P]) for j in range(2)]
    heads_out = tensor(ctx, "heads_out", [P, TILES, E])
    ps_s = psum(ctx, "ps_s", [P, 2, CHUNK])
    ps_t = psum(ctx, "ps_t", [P, 2, T])
    ps_o = psum(ctx, "ps_o", [P, 2, CHUNK])

    rows_made = sem("a_rows_made")
    loaded = [sem(f"a_loaded{j}") for j in range(RING)]
    v_ready = sem("a_v_ready")
    slot_made = sem("a_slot_made")
    slot_used = sem("a_slot_used")
    part_hi = sem("a_part_hi")
    parts_ready = sem("a_parts_ready")
    minus_ready = sem("a_minus_ready")
    max_ready = sem("a_max_ready")
    max_stored = [sem(f"a_max_stored{j}") for j in range(RING)]
    max_loaded = [sem(f"a_max_loaded{j}") for j in range(RING)]
    st_made = sem("a_st_made")
    p_ready = sem("a_p_ready")
    pv_done = sem("a_pv_done")
    sums_ready = sem("a_sums_ready")
    rsum_ready = sem("a_rsum_ready")
    fold_done = sem("a_fold_done")
    out_done = sem("a_out_done")
    attn_stored = sem("a_attn_stored")
    one_made = sem("a_one_made")
    LOADS = 6 * 16
    CONSTANTS = 5 * RING + 3

    with nc.Block() as block:

        @block.gpsimd
        def _(pool):
            pool.memset(minus_one[:], -1.0).then_inc(one_made, 1)
            pool.wait_ge(one_made, 1)

            def values_of(u, j):
                pool.tensor_copy(vs[j][:, :, 0:DC], values[:, u]).then_inc(v_ready, 1)

            def split_maxima(i, j):
                u = RING * i + j
                pool.wait_ge(minus_ready, u + 1)
                if not (isinstance(i, int) and i == 0):
                    pool.wait_ge(max_stored[j], 16 * i)
                pool.tensor_tensor(max_parts[j][:, HI, :], minus_max[j % 2][:], zeros[0:KT, 0:P], ALU.add).then_inc(part_hi, 1)
                pool.wait_ge(part_hi, u + 1)
                pool.tensor_tensor(max_parts[j][:, LO, :], minus_max[j % 2][:], max_parts[j][:, HI, :], ALU.subtract).then_inc(parts_ready, 1)

            def output(i, j):
                pool.wait_ge(fold_done, RING * i + j + 1)
                pool.tensor_tensor(rsum[:], folded[:, :, :, DC].rearrange("p c q -> p (c q)"), minus_one[:], ALU.pow).then_inc(rsum_ready, 1)
                pool.wait_ge(rsum_ready, RING * i + j + 1)
                pool.tensor_tensor(heads_out[:, bass.ds((i // 4) * KT, KT), bass.ds((i % 4) * 4 * DC + j * DC, DC)],
                                   folded[:, :, :, 0:DC].rearrange("p c q d -> p (c q) d"),
                                   rsum[:].unsqueeze(2).broadcast_to([P, KT, DC]), ALU.mult).then_inc(out_done, 1)

            def step(i, last=False):
                for j in range(RING):
                    if not (isinstance(i, int) and i == 0):
                        pool.wait_ge(pv_done, KT * (RING * (i - 1) + j + 1))
                        values_of(RING * i + j, j)
                    if not (isinstance(i, int) and i == 0 and j == 0):
                        output(i if j else i - 1, (j - 1) % RING)
                    if not (last and j >= RING - AHEAD):
                        split_maxima(i + (j + AHEAD) // RING, (j + AHEAD) % RING)

            for j in range(RING):
                values_of(j, j)
            for j in range(AHEAD):
                split_maxima(0, j)
            step(0)
            with pool.Fori(1, UNITS // RING - 1) as i:
                step(i)
            step(UNITS // RING - 1, last=True)
            output(UNITS // RING - 1, RING - 1)

        @block.sync
        def _(sp):
            sp.wait_ge(rows_made, CONSTANTS)

            def load(i, j):
                u = RING * i + j
                for r in (0, 2):
                    sp.dma_start(qs[j][r * DC:(r + 2) * DC, :].bitcast(F32), q_parts[u]).then_inc(loaded[j], 16)
                sp.dma_start(ks[j][0:2 * DC, :].bitcast(F32), k_parts[u]).then_inc(loaded[j], 16)
                for r, part in ((2, LO), (3, HI)):
                    sp.dma_start(ks[j][r * DC:(r + 1) * DC, :].bitcast(F32),
                                 k_parts[u, part * DC:(part + 1) * DC, :]).then_inc(loaded[j], 16)
                sp.dma_start(qs[j][64:66, :].bitcast(F32), zeros[0:2, :]).then_inc(loaded[j], 16)

            def maximum_rows(i, j):
                sp.wait_ge(parts_ready, RING * i + j + 1)
                sp.dma_start(neg_max[j].rearrange("s (t n) -> t s n", t=KT),
                             max_parts[j][:].bitcast(F32)).then_inc(max_stored[j], 16)
                sp.wait_ge(max_stored[j], 16 * (i + 1))
                sp.dma_start(qs[j][64:66, :].bitcast(F32), neg_max[j]).then_inc(max_loaded[j], 16)

            def step(i, last=False):
                for j in range(RING):
                    if not (last and j >= RING - AHEAD):
                        maximum_rows(i + (j + AHEAD) // RING, (j + AHEAD) % RING)
                    if not last:
                        sp.wait_ge(st_made, KT * (RING * i + j + 1))
                        load(i + 1, j)

            for j in range(RING):
                load(0, j)
            for j in range(AHEAD):
                maximum_rows(0, j)

            def store_batch(b):
                sp.wait_ge(out_done, HC * (b + 1))
                sp.dma_start(attn_out[bass.ds(KT * b, KT)].rearrange("t p e -> p t e"),
                             heads_out[:, bass.ds(KT * b, KT), :]).then_inc(attn_stored, 16)

            turns = HC // RING
            load_qkv_weights(sp, 0, w_qkv, w_o, w_raw, weights_in)
            step(0)
            with sp.Fori(1, turns) as i:
                step(i)
            store_batch(0)
            with sp.Fori(1, B - 1) as b:
                with sp.Fori(0, turns) as r:
                    step(turns * b + r)
                store_batch(b)
            with sp.Fori(turns * (B - 1), turns * B - 1) as i:
                step(i)
            step(turns * B - 1, last=True)
            store_batch(B - 1)
            sp.wait_ge(attn_stored, 16 * B)

        @block.tensor
        def _(pe):
            def free_bank(n):
                if not isinstance(n, int) or n >= 2:
                    pe.wait_ge(slot_used, n - 1)

            def piece(j, k, n, bank):
                t, k0, keys = PIECES[k]
                free_bank(n)
                diagonal = k0 + keys == (t + 1) * P
                mm = pe.matmul(ps_s[:, bank, 0:keys], qs[j][:, t * P:(t + 1) * P], ks[j][:, k0:k0 + keys],
                               start=True, stop=not diagonal)
                if diagonal:
                    mm = pe.matmul(ps_s[:, bank, keys - P:keys], ident_bf[:], causal_qk[:], start=False, stop=True)
                mm.then_inc(slot_made, 1)

            def turn_maxima(u, half, n, bank):
                pe.wait_ge(max_ready, u + 1)
                free_bank(n)
                pe.transpose(ps_s[0:KT, bank, 0:P], maxima[half][:, 0:KT], ident[:]).then_inc(slot_made, 1)

            def turn_output(u, half, c, n, bank):
                pe.wait_ge(sums_ready, u + 1)
                free_bank(n)
                for q in range(CT):
                    mm = pe.transpose(ps_s[:, bank, q * P:(q + 1) * P], sums[half][:, (CT * c + q) * P:(CT * c + q + 1) * P], ident[:])
                mm.then_inc(slot_made, 1)

            def scores_t(i, j, kt):
                n = KT * (RING * i + j) + kt
                if kt == 0:
                    pe.wait_ge(max_loaded[j], 16 * (i + 1))
                if not isinstance(n, int) or n >= 2:
                    pe.wait_ge(p_ready, n - 1)
                q0, half = kt * P, kt % 2
                for a in range(q0 // CHUNK, T // CHUNK):
                    lo, hi = max(q0, a * CHUNK), (a + 1) * CHUNK
                    diagonal = lo == q0
                    mm = pe.matmul(ps_t[:, half, lo:hi], ks[j][:, q0:q0 + P], qs[j][:, lo:hi], start=True, stop=not diagonal)
                    if diagonal:
                        mm = pe.matmul(ps_t[:, half, q0:q0 + P], ident_bf[:], causal_kq[:], start=False, stop=True)
                mm.then_inc(st_made, 1)

            def weighted(i, j, kt):
                u, r = RING * i + j, kt % 4
                g = (r + 2) % 4
                pe.wait_ge(p_ready, KT * u + kt + 1)
                if kt == 0:
                    pe.wait_ge(v_ready, u + 1)
                    if not (isinstance(u, int) and u == 0):
                        pe.wait_ge(sums_ready, u)
                if kt < 4:
                    pe.matmul(ps_o[r * VW:(r + 1) * VW, 0, :], vs[j][:, kt, :], prob_a[:, r, 0:CHUNK], start=True, stop=True)
                    mm = pe.matmul(ps_o[g * VW:(g + 1) * VW, 1, :], vs[j][:, kt, :], prob_a[:, r, CHUNK:T], start=True, stop=False)
                else:
                    mm = pe.matmul(ps_o[g * VW:(g + 1) * VW, 1, r * P:CHUNK], vs[j][:, kt, :], prob_b[:, r, r * P:CHUNK],
                                   start=False, stop=True)
                mm.then_inc(pv_done, 1)

            def weighted_with(i, j, kt):
                if kt == 1 and not (isinstance(i, int) and i == 0 and j == 0):
                    for before in range(4, KT):
                        weighted(i if j else i - 1, (j - 1) % RING, before)
                if kt in (3, 5):
                    weighted(i, j, kt - 3)
                    weighted(i, j, kt - 2)

            def step(i):
                for j in range(RING):
                    u, listed = RING * i + j, uses(i, j)
                    n, bank = first_slot(i, j)
                    ja = (j + AHEAD) % RING
                    if any(kind == "piece" for _, kind, _ in listed):
                        pe.wait_ge(loaded[ja], LOADS * (i + (j + AHEAD) // RING + 1))
                    for kt in range(KT):
                        scores_t(i, j, kt)
                        uses_now = [(e, kind, which) for e, (at, kind, which) in enumerate(listed) if at == kt]
                        for number, (e, kind, which) in enumerate(uses_now):
                            where = n + e, (bank + e) % 2
                            if kind == "piece":
                                piece(ja, which, *where)
                            elif kind == "output":
                                turn_output(u - 1, (j - 1) % 2, which, *where)
                            else:
                                turn_maxima(u + AHEAD, j % 2, *where)
                            if number == 0:
                                weighted_with(i, j, kt)
                        if not uses_now:
                            weighted_with(i, j, kt)

            pe.wait_ge(rows_made, CONSTANTS)
            for u in range(AHEAD):
                n = MAXIMUM_SLOTS * u
                pe.wait_ge(loaded[u], LOADS)
                for k in range(len(PIECES)):
                    piece(u, k, n + k, (n + k) % 2)
                n += len(PIECES)
                turn_maxima(u, u % 2, n, n % 2)
            step(0)
            with pe.Fori(1, UNITS // RING - 1) as i:
                step(i)
            step(UNITS // RING - 1)
            for kt in range(4, KT):
                weighted(UNITS // RING - 1, RING - 1, kt)
            n = SLOTS * UNITS - 2
            for c in range(2):
                turn_output(UNITS - 1, (RING - 1) % 2, c, n + c, (n + c) % 2)

        @block.scalar
        def _(act):
            def exp_tile(u, kt):
                act.wait_ge(st_made, KT * u + kt + 1)
                before = KT * (u - 1) + kt + 1
                if not isinstance(u, int) or before > 0:
                    act.wait_ge(pv_done, before)
                r = kt % 4
                dst = prob_a[:, r, kt * P:T] if kt < 4 else prob_b[:, r, r * P:CHUNK]
                act.activation(dst, ps_t[:, kt % 2, kt * P:T], ACT.Exp).then_inc(p_ready, 1)

            def keep_sums(u, half):
                act.wait_ge(pv_done, KT * (u + 1))
                if not isinstance(u, int) or u >= 2:
                    act.wait_ge(out_done, u - 1)
                act.activation(sums[half][:], ps_o[:].rearrange("p c n -> p (c n)"), ACT.Copy).then_inc(sums_ready, 1)

            def step(i):
                for j in range(RING):
                    u = RING * i + j
                    for kt in range(KT):
                        exp_tile(u, kt)
                        if kt == 2 and not (isinstance(u, int) and u == 0):
                            keep_sums(u - 1, (j - 1) % 2)

            act.wait_ge(rows_made, CONSTANTS)
            step(0)
            with act.Fori(1, UNITS // RING) as i:
                step(i)
            keep_sums(UNITS - 1, (RING - 1) % 2)

        @block.vector
        def _(dve):
            constants = [(t[j][64:KROWS, :].bitcast(F32), 0.0) for j in range(RING) for t in (qs, ks)]
            constants += [(vs[j][:, :, DC:VW], 0.0) for j in range(RING)]
            constants += [(prob_a[:, r, 0:r * P], 0.0) for r in range(1, 4)]
            zeroed = len(constants)
            constants += [(ks[j][64:66, :].bitcast(F32), 1.0) for j in range(RING)]
            constants += [(vs[j][:, :, DC:DC + 1], 1.0) for j in range(RING)]
            for n, (rows, value) in enumerate(constants):
                if n == zeroed:
                    dve.wait_ge(rows_made, zeroed)
                dve.memset(rows, value).then_inc(rows_made, 1)
            assert len(constants) == CONSTANTS

            def piece(half, k, n, bank):
                t, k0, keys = PIECES[k]
                col = t if k0 == 0 else KT + t - 4
                dve.wait_ge(slot_made, n + 1)
                dve.tensor_reduce(maxima[half][:, col:col + 1], ps_s[:, bank, 0:keys], AX.X, ALU.max).then_inc(slot_used, 1)
                if k == len(PIECES) - 1:
                    dve.wait_ge(slot_used, n + 1)
                    dve.tensor_tensor(maxima[half][:, 4:KT], maxima[half][:, 4:KT], maxima[half][:, KT:KT + 4], ALU.max).then_inc(max_ready, 1)

            def finish_maxima(i, j, n, bank):
                u = RING * i + j
                dve.wait_ge(slot_made, n + 1)
                if not (isinstance(i, int) and i == 0 and j < 2):
                    dve.wait_ge(parts_ready, u - 1)
                dve.tensor_scalar(minus_max[j % 2][:], ps_s[0:KT, bank, 0:P], -1.0, None, ALU.mult).then_inc(slot_used, 1)
                dve.wait_ge(slot_used, n + 1)
                dve.sem_inc(minus_ready, 1)

            def output(i, j, c, n, bank):
                dve.wait_ge(slot_made, n + 1)
                if c == 0 and not (isinstance(i, int) and i == 0 and j == 0):
                    dve.wait_ge(out_done, RING * i + j)
                dve.tensor_reduce(folded[:, c, :, 0:DC + 1],
                                  ps_s[:, bank, :].rearrange("p (q g w) -> p q w g", q=CT, g=4)[:, :, 0:DC + 1, :],
                                  AX.X, ALU.add).then_inc(slot_used, 1)
                if c == 1:
                    dve.wait_ge(slot_used, n + 1)
                    dve.sem_inc(fold_done, 1)

            def step(i):
                for j in range(RING):
                    n, bank = first_slot(i, j)
                    for e, (_, kind, which) in enumerate(uses(i, j)):
                        where = n + e, (bank + e) % 2
                        if kind == "piece":
                            piece(j % 2, which, *where)
                        elif kind == "output":
                            output(i if j else i - 1, (j - 1) % RING, which, *where)
                        else:
                            finish_maxima(i + (j + AHEAD) // RING, (j + AHEAD) % RING, *where)

            for u in range(AHEAD):
                n = MAXIMUM_SLOTS * u
                for k in range(len(PIECES)):
                    piece(u, k, n + k, (n + k) % 2)
                n += len(PIECES)
                finish_maxima(0, u, n, n % 2)
            step(0)
            with dve.Fori(1, UNITS // RING - 1) as i:
                step(i)
            step(UNITS // RING - 1)
            n = SLOTS * UNITS - 2
            for c in range(2):
                output(UNITS // RING - 1, RING - 1, c, n + c, (n + c) % 2)


WINDOWS = TILES
PER_BATCH = WINDOWS // B
PAIRS = HL // 2
TURNS = 5


def local_layers(nc, ctx, tensor, psum, sem, w_raw, weights_in, layer_in, layer_mid, w_qkv, w_o, w1, w2, ln_gb, b1, b2,
                 qk_scale, trig, ident, ident_bf):
    class Arena:

        def __init__(self, name, dt, words):
            self.whole, self.words, self.at = tensor(ctx, name, [P, words], dt), words, 0

        def take(self, *shape):
            n = 1
            for s in shape:
                n *= s
            part = self.whole[:, self.at:self.at + n]
            self.at += n
            assert self.at <= self.words
            if len(shape) == 1:
                return part
            names = "abcd"[:len(shape)]
            return part.rearrange(f"p ({' '.join(names)}) -> p {' '.join(names)}", **dict(zip(names, shape)))

    plain, rounded = Arena("plain", F32, 10240), Arena("rounded", F32R, 9728)
    wqkv_s = tensor(ctx, "wqkv_s", [P, 2, KE, 3 * INNER], F32R)
    wo_s = tensor(ctx, "wo_s", [P, 2, PAIRS, E], F32R)
    w1_s = tensor(ctx, "w1_s", [P, 2, KE, 2 * HIDP], F32R)
    w2_s = tensor(ctx, "w2_s", [P, 2, HT, E], F32R)
    gb = tensor(ctx, "gb", [P, 2, KE])
    b1_t = tensor(ctx, "b1_t", [P, 2 * HT])
    b2_t = tensor(ctx, "b2_t", [P, E])
    scale_t = tensor(ctx, "scale_t", [P, 4, DL])
    trig_t = tensor(ctx, "trig_t", [P, PER_BATCH, 4, DL])
    rotary = tensor(ctx, "rotary", [P, PER_BATCH, 2, 2, DL])
    own_mask = tensor(ctx, "own_mask", [P, P], BF16)
    before_mask = tensor(ctx, "before_mask", [P, P], BF16)
    mask_even = tensor(ctx, "mask_even", [P, 4, 2, 2, P], BF16)
    mask_odd = tensor(ctx, "mask_odd", [P, 2, 2, P], BF16)
    minus_half = tensor(ctx, "l_minus_half", [P, 2 * HL])

    hin = [plain.take(E) for _ in range(2)]
    res = [plain.take(E) for _ in range(2)]
    mid = [plain.take(E) for _ in range(2)]
    square = plain.take(2 * HL, DL)
    straight = plain.take(2, HL, DL)
    crossed = plain.take(2, HL, DL)
    unit = plain.take(2 * HL, DL)
    prob = [plain.take(2, 2 * P) for _ in range(2)]
    prob_t = [plain.take(2, 2, P) for _ in range(2)]
    norm2, rnorm = plain.take(2 * HL), plain.take(2 * HL)
    minus_max, row_sum, row_inv = plain.take(HL), plain.take(HL), plain.take(HL)
    values = tensor(ctx, "l_values", [P, 2, HL, DL])
    ht = [rounded.take(2, KE, P) for _ in range(2)]
    halves_q = rounded.take(HL, 2, DL)
    halves_k = rounded.take(HL, 3, DL)
    keys = rounded.take(2, HL, 2, P)
    queries = rounded.take(HL, P)
    heads = rounded.take(2, PAIRS, P)
    plain.at = rounded.at = 0
    fin = [plain.take(CT, E) for _ in range(2)]
    fres = [plain.take(CT, E) for _ in range(2)]
    fout = [plain.take(CT, E) for _ in range(2)]
    affine = plain.take(KE, CHUNK)
    gate = [plain.take(CHUNK) for _ in range(2)]
    hidden = [plain.take(CHUNK) for _ in range(2)]
    stats, mean_var = plain.take(CT, 6), plain.take(CT, 2)
    var_eps, rstd = plain.take(CT), plain.take(CT)
    ft = rounded.take(2, KE, CHUNK)
    hid = rounded.take(2, HT, CHUNK)

    ps_h = psum(ctx, "l_ps_h", [P, CHUNK])
    ps_qk = psum(ctx, "l_ps_qk", [P, 2, CHUNK])
    ps_v = psum(ctx, "l_ps_v", [P, CHUNK])
    ps_ta = psum(ctx, "l_ps_ta", [P, CHUNK])
    ps_td = psum(ctx, "l_ps_td", [P, CHUNK])
    ps_s = psum(ctx, "l_ps_s", [P, 2, CHUNK])
    ps_ft = ps_qk
    ps_out = ps_s
    ps_ga = [(ps_h, ps_v), (ps_ta, ps_td)]

    def sems(names):
        return [sem("l_" + n) for n in names.split()]

    const_made, masks_made, weights_hi, weights_split, trig_in, trig_scaled = sems(
        "const_made masks_made weights_hi weights_split trig_in trig_scaled")
    layer_stored, f_counted = sems("layer_stored f_counted")
    h_turned, h_hi, h_lo, qk_made, v_made, v_kept = sems("h_turned h_hi h_lo qk_made v_made v_kept")
    sq_ready, crossed_ready, norm_sum, norm_ready, r_ready, added, u_ready, u_hi, u_lo = sems(
        "sq_ready crossed_ready norm_sum norm_ready r_ready added u_ready u_hi u_lo")
    ta_made, ta_used, td_made, td_used = sems("ta_made ta_used td_made td_used")
    s_made, max_ready, exp_ready, inv_ready, p_ready = sems("s_made max_ready exp_ready inv_ready p_ready")
    o_part, o_made, o_hi, o_lo, y_made, y_ready = sems("o_part o_made o_hi o_lo y_made y_ready")
    f_stats, f_aggr, f_var, f_rstd, f_norm, f_turned, f_affine, f_hi, f_lo = sems(
        "f_stats f_aggr f_var f_rstd f_norm f_turned f_affine f_hi f_lo")
    g_made, a_made, gate_ready, hid_ready, hid_hi, hid_lo, f_made, f_res, f_ready = sems(
        "g_made a_made gate_ready hid_ready hid_hi hid_lo f_made f_res f_ready")
    h_in, res_in, mid_out, f_in, fres_in, f_out = ([sem(f"l_{n}{j}") for j in range(2)]
                                                   for n in ("h_in", "res_in", "mid_out", "f_in", "fres_in", "f_out"))
    WI, CI = WINDOWS // 2, CHUNKS // 2
    QKV_IN, MLP_IN = 4 * 16, 4 * 16

    def is_first(i, j=0):
        return isinstance(i, int) and i == 0 and j == 0

    def side(tile, s):
        return tile[:, s * HL:(s + 1) * HL]

    def is_window(i, j, *which):
        return isinstance(i, int) and 2 * i + j in which

    def away(i, j, n):
        return i + (j + n) // 2, (j + n) % 2

    with nc.Block() as block:

        @block.gpsimd
        def _(pool):
            pool.memset(own_mask[:], 0.0).then_inc(const_made, 1)
            pool.memset(before_mask[:], 0.0).then_inc(const_made, 1)
            pool.memset(minus_half[:], -0.5).then_inc(const_made, 1)
            pool.wait_ge(const_made, 3)
            pool.affine_select(out=own_mask[:], in_=own_mask[:], compare_op=ALU.is_ge, fill=NEG, base=0,
                               pattern=[[-1, P]], channel_multiplier=1).then_inc(const_made, 1)
            pool.affine_select(out=before_mask[:], in_=before_mask[:], compare_op=ALU.is_ge, fill=NEG, base=0,
                               pattern=[[1, P]], channel_multiplier=-1).then_inc(const_made, 1)

            def norm_inverse(l, i, j, s):
                n = 2 * (WINDOWS * l + 2 * i + j) + 1 - s
                pool.wait_ge(norm_ready, n + 1)
                pool.tensor_tensor(side(rnorm, s), side(norm2, s), side(minus_half, s), ALU.pow).then_inc(r_ready, 1)

            def unit_vectors(l, i, j, s):
                n = 2 * (WINDOWS * l + 2 * i + j) + 1 - s
                pool.wait_ge(crossed_ready, n + 1)
                if not is_first(i, j):
                    pool.wait_ge(u_hi, n - 1)
                    pool.wait_ge(u_lo, n - 1)
                pool.tensor_tensor(side(unit, s), straight[:, s], crossed[:, s], ALU.add).then_inc(added, 1)
                pool.wait_ge(r_ready, n + 1)
                pool.wait_ge(added, n + 1)
                pool.tensor_tensor(side(unit, s), side(unit, s), side(rnorm, s).unsqueeze(2).broadcast_to([P, HL, DL]),
                                   ALU.mult).then_inc(u_ready, 1)

            def unit_lo(l, i, j, s):
                t = WINDOWS * l + 2 * i + j
                pool.wait_ge(u_ready, 2 * t + 2 - s)
                pool.wait_ge(u_hi, 2 * t + 2 - s)
                if not is_first(i, j):
                    pool.wait_ge(ta_made, TURNS * t - 2 - s)
                    pool.wait_ge(td_made, TURNS * t - 2 - s)
                halves = halves_k if s else halves_q
                pool.tensor_tensor(halves[:, :, LO, :], side(unit, s), halves[:, :, HI, :], ALU.subtract).then_inc(u_lo, 1)

            def window(l, i, j):
                norm_inverse(l, i, j, 1)
                unit_vectors(l, i, j, 1)
                norm_inverse(l, i, j, 0)
                unit_lo(l, i, j, 1)
                unit_vectors(l, i, j, 0)
                unit_lo(l, i, j, 0)

            def inverse_deviation(l, i, j):
                t = CHUNKS * l + 2 * i + j
                pool.wait_ge(f_var, t + 1)
                pool.tensor_tensor(rstd, var_eps, minus_half[:, 0:CT], ALU.pow).then_inc(f_rstd, 1)

            def input_lo(l, i, j):
                t = CHUNKS * l + 2 * i + j
                for f in range(KE):
                    pool.wait_ge(f_hi, KE * t + f + 1)
                    pool.tensor_tensor(ft[:, LO, f, :], affine[:, f, :], ft[:, HI, f, :], ALU.subtract).then_inc(f_lo, 1)

            def chunk(l, i, j, last=False):
                t = CHUNKS * l + 2 * i + j
                if not last:
                    inverse_deviation(l, i + j, 1 - j)
                pool.wait_ge(fres_in[j], 16 * (CI * l + i + 1))
                pool.tensor_tensor(fres[j], fres[j], b2_t[:].unsqueeze(1).broadcast_to([P, CT, E]), ALU.add).then_inc(f_res, 1)
                for k in range(HT):
                    pool.wait_ge(hid_hi, HT * t + k + 1)
                    pool.tensor_tensor(hid[:, LO, k, :], hidden[k % 2], hid[:, HI, k, :], ALU.subtract).then_inc(hid_lo, 1)
                if not last:
                    input_lo(l, i + j, 1 - j)

            with pool.Fori(0, DEPTH) as l:
                for j in range(2):
                    window(l, 0, j)
                with pool.Fori(1, WI) as i:
                    for j in range(2):
                        window(l, i, j)
                inverse_deviation(l, 0, 0)
                input_lo(l, 0, 0)
                with pool.Fori(0, CI - 1) as i:
                    for j in range(2):
                        chunk(l, i, j)
                chunk(l, CI - 1, 0)
                chunk(l, CI - 1, 1, last=True)

        @block.sync
        def _(sp):
            sp.dma_start(trig_t[:], trig).then_inc(trig_in, 16)
            sp.wait_ge(trig_in, 16)

            def tokens(scratch, l, i, j, shift, columns):
                row = 1 - shift + P * (2 * (i % 4) + j)
                return scratch[l, i // 4, bass.ds(row, P), columns]

            def chunk_tokens(scratch, l, i, j, shift, columns):
                row = 1 - shift + CHUNK * j
                return scratch[l, i, row:row + CHUNK, columns].rearrange("(q p) e -> p q e", p=P)

            def load_h(l, i, j):
                sp.dma_start(hin[j][:, 0:P], tokens(layer_in, l, i, j, 0, slice(0, P))).then_inc(h_in[j], 16)
                sp.dma_start(hin[j][:, P:E], tokens(layer_in, l, i, j, 1, slice(P, E))).then_inc(h_in[j], 16)

            def load_res(l, i, j):
                sp.dma_start(res[j], tokens(layer_in, l, i, j, 0, slice(0, E))).then_inc(res_in[j], 16)

            def window(l, i, j, load_next=True, load_residual=True):
                t = WINDOWS * l + 2 * i + j
                if load_next:
                    sp.wait_ge(h_turned, t + 3)
                    load_h(l, i + 2, j)
                sp.wait_ge(y_ready, t + 1)
                sp.dma_start(tokens(layer_mid, l, i, j, 0, slice(0, E)), mid[j]).then_inc(mid_out[j], 16)
                if load_residual:
                    load_res(l, i + 1, j)

            def load_f(l, i, j):
                sp.dma_start(fin[j][:, :, 0:P], chunk_tokens(layer_mid, l, i, j, 0, slice(0, P))).then_inc(f_in[j], 16)
                sp.dma_start(fin[j][:, :, P:E], chunk_tokens(layer_mid, l, i, j, 1, slice(P, E))).then_inc(f_in[j], 16)

            def load_fres(l, i, j):
                sp.dma_start(fres[j], chunk_tokens(layer_mid, l, i, j, 0, slice(0, E))).then_inc(fres_in[j], 16)

            def chunk(l, i, j, last):
                t = CHUNKS * l + 2 * i + j
                if not last:
                    sp.wait_ge(f_turned, KE * (t + 1))
                    load_f(l, i + 1, j)
                sp.wait_ge(f_ready, 2 * (t + 1))
                sp.dma_start(chunk_tokens(layer_in, l + 1, i, j, 0, slice(0, E)), fout[j]).then_inc(f_out[j], 16)
                if not last:
                    load_fres(l, i + 1, j)

            def layer(l, last=False):
                sp.dma_start(scale_t[:], qk_scale[l]).then_inc(weights_in, 16)
                sp.dma_start(gb[:], ln_gb[l]).then_inc(weights_in, 16)
                for j in range(2):
                    load_h(l, 0, j)
                    load_res(l, 0, j)
                sp.wait_ge(weights_split, 4 * l + 2)
                sp.dma_start(w_raw[:, 0:KE * 2 * HIDP].rearrange("p (k n) -> p k n", k=KE),
                             w1[l].rearrange("(k p) n -> p k n", p=P)).then_inc(weights_in, 16)
                sp.dma_start(w_raw[:, KE * 2 * HIDP:KE * 2 * HIDP + HT * E].rearrange("p (k n) -> p k n", k=HT),
                             w2[l].rearrange("(k p) n -> p k n", p=P)).then_inc(weights_in, 16)
                sp.dma_start(b1_t[:], b1[l]).then_inc(weights_in, 16)
                sp.dma_start(b2_t[:], b2[l]).then_inc(weights_in, 16)
                for j in range(2):
                    sp.wait_ge(h_turned, WINDOWS * l + j + 1)
                    load_h(l, 1, j)
                with sp.Fori(0, WI - 2) as i:
                    for j in range(2):
                        window(l, i, j)
                for j in range(2):
                    window(l, WI - 2, j, load_next=False)
                for j in range(2):
                    window(l, WI - 1, j, load_next=False, load_residual=False)
                for j in range(2):
                    sp.wait_ge(mid_out[j], 16 * WI * (l + 1))
                for j in range(2):
                    load_f(l, 0, j)
                    load_fres(l, 0, j)
                if not last:
                    sp.wait_ge(weights_split, 4 * l + 4)
                    load_qkv_weights(sp, l + 1, w_qkv, w_o, w_raw, weights_in)
                with sp.Fori(0, CI - 1) as i:
                    for j in range(2):
                        chunk(l, i, j, False)
                for j in range(2):
                    chunk(l, CI - 1, j, True)
                for j in range(2):
                    sp.wait_ge(f_out[j], 16 * CI * (l + 1))
                sp.sem_inc(layer_stored, 1)

            with sp.Fori(0, DEPTH - 1) as l:
                layer(l)
            layer(DEPTH - 1, last=True)

        @block.tensor
        def _(pe):
            def turn_h(l, i, j):
                t = WINDOWS * l + 2 * i + j
                pe.wait_ge(h_in[j], 32 * (WI * l + i + 1))
                if is_window(i, j, 1, 2):
                    pe.wait_ge(h_lo, t)
                elif not is_first(i, j):
                    pe.wait_ge(o_lo, t - 2)
                for f in range(KE):
                    mm = pe.transpose(ps_h[:, f * P:(f + 1) * P], hin[j][:, f * P:(f + 1) * P], ident[:])
                mm.then_inc(h_turned, 1)

            def project_side(l, i, j, s):
                t = WINDOWS * l + 2 * i + j
                if s == 1:
                    pe.wait_ge(h_lo, t + 1)
                if not is_first(i, j):
                    pe.wait_ge(crossed_ready, 2 * t - s)
                    pe.wait_ge(sq_ready, 2 * t - s)
                products(pe, ps_qk[:, s, :], lambda part, f: ht[j][:, part, f, :],
                         lambda part, f: wqkv_s[:, part, f, s * INNER:(s + 1) * INNER], KE).then_inc(qk_made, 1)

            def turned_tile(t, n, even, first=False):
                if not (first and n == 0):
                    pe.wait_ge(ta_used if even else td_used, TURNS * t + n)
                return ps_ta if even else ps_td, ta_made if even else td_made

            def stacks(l, i, j, n):
                t = WINDOWS * l + 2 * i + j
                if n != 1:
                    pe.wait_ge(u_lo, 2 * t + 1 + n // 2)
                halves, part = ((halves_k, HI), (halves_k, LO), (halves_q, HI))[n]
                for even in (True, False):
                    out, made = turned_tile(t, n, even, is_first(i, j))
                    for q in range(4):
                        rows = halves[:, q + (0 if even else 4), part:part + 2, :].rearrange("p s d -> p (s d)")
                        mm = pe.transpose(out[:, q * P:(q + 1) * P], rows.bitcast(F32), ident[:])
                    mm.then_inc(made, 1)

            def project_v(l, i, j):
                t = WINDOWS * l + 2 * i + j
                if is_window(i, j, 1):
                    pe.wait_ge(v_kept, t)
                elif not is_first(i, j):
                    pe.wait_ge(y_ready, t - 1)
                products(pe, ps_v[:], lambda part, f: ht[j][:, part, f, :],
                         lambda part, f: wqkv_s[:, part, f, 2 * INNER:3 * INNER], KE).then_inc(v_made, 1)

            def scores(l, i, j, p):
                t = WINDOWS * l + 2 * i + j
                if p == 0:
                    pe.wait_ge(ta_used, TURNS * t + 3)
                    pe.wait_ge(td_used, TURNS * t + 3)
                if not is_first(i, j) or p >= 2:
                    pe.wait_ge(exp_ready, PAIRS * t + p - 1)
                masks = (mask_even[:, i % 4] if j == 0 else mask_odd[:]).rearrange("p h s n -> p (h s n)")
                pe.matmul(ps_s[:, p % 2, :], ident_bf[:], masks, start=True, stop=False)
                for h2 in range(2):
                    for part in (HI, LO):
                        mm = pe.matmul(ps_s[:, p % 2, h2 * 2 * P:(h2 + 1) * 2 * P], queries[:, 2 * p + h2, :],
                                       keys[:, part, 2 * p + h2].rearrange("p s n -> p (s n)"), start=False, stop=h2 == 1 and part == LO)
                mm.then_inc(s_made, 1)

            def turn_prob(l, i, j, p):
                t = WINDOWS * l + 2 * i + j
                out, made = turned_tile(t, 3 + p // 2, p % 2 == 0)
                pe.wait_ge(p_ready, PAIRS * t + p + 1)
                for h2 in range(2):
                    for s in range(2):
                        mm = pe.transpose(out[:, (2 * h2 + s) * P:(2 * h2 + s + 1) * P], prob[p % 2][:, h2, s * P:(s + 1) * P], ident[:])
                mm.then_inc(made, 1)

            def weighted(l, i, j, p):
                t = WINDOWS * l + 2 * i + j
                if p == 0:
                    pe.wait_ge(v_kept, t + 1)
                    if not is_window(i, j, WINDOWS - 2, WINDOWS - 1):
                        pe.wait_ge(h_lo, t + 3)
                pe.wait_ge(ta_used if p % 2 == 0 else td_used, TURNS * t + 4 + p // 2)
                for s in range(2):
                    for h2 in range(2):
                        mm = pe.matmul(ps_h[h2 * DL:(h2 + 1) * DL, p * P:(p + 1) * P], values[:, s, 2 * p + h2, :],
                                       prob_t[p % 2][:, h2, s, :], start=s == 0, stop=s == 1)
                if p < 2:
                    mm.then_inc(o_part, 1)
                if p == PAIRS - 1:
                    mm.then_inc(o_made, 1)

            def project_out(l, i, j):
                t = WINDOWS * l + 2 * i + j
                pe.wait_ge(o_lo, t + 1)
                if is_window(i, j, WINDOWS - 1):
                    pe.wait_ge(y_ready, t)
                else:
                    pe.wait_ge(v_kept, t + 2)
                products(pe, ps_v[:, 0:E], lambda part, f: heads[:, part, f, :], lambda part, f: wo_s[:, part, f, :],
                         PAIRS).then_inc(y_made, 1)

            def step(l, i, j, before=True, next1=True, next2=True):
                stacks(l, i, j, 0)
                if before:
                    weighted(l, *away(i, j, -1), PAIRS - 1)
                stacks(l, i, j, 1)
                stacks(l, i, j, 2)
                if next2:
                    turn_h(l, *away(i, j, 2))
                if before:
                    project_out(l, *away(i, j, -1))
                scores(l, i, j, 0)
                scores(l, i, j, 1)
                if next1:
                    project_v(l, *away(i, j, 1))
                scores(l, i, j, 2)
                turn_prob(l, i, j, 0)
                scores(l, i, j, 3)
                turn_prob(l, i, j, 1)
                weighted(l, i, j, 0)
                if next2:
                    project_side(l, *away(i, j, 2), 1)
                turn_prob(l, i, j, 2)
                weighted(l, i, j, 1)
                if next2:
                    project_side(l, *away(i, j, 2), 0)
                turn_prob(l, i, j, 3)
                weighted(l, i, j, 2)

            def turn_f(l, i, j):
                t = CHUNKS * l + 2 * i + j
                pe.wait_ge(f_norm, t + 1)
                if not is_first(i, j):
                    pe.wait_ge(f_affine, KE * t)
                for f in range(KE):
                    for q in range(CT):
                        mm = pe.transpose(ps_ft[:, f, q * P:(q + 1) * P], fin[j][:, q, f * P:(f + 1) * P], ident[:])
                    mm.then_inc(f_turned, 1)

            def hidden_tiles(l, i, j):
                t = CHUNKS * l + 2 * i + j
                pe.wait_ge(f_lo, KE * (t + 1))
                for k in range(HT):
                    if not is_first(i, j) or k >= 2:
                        pe.wait_ge(hid_ready, HT * t + k - 1)
                    for which, made in ((1, g_made), (0, a_made)):
                        c0 = which * HIDP + k * P
                        products(pe, ps_ga[k % 2][1 - which][:], lambda part, f: w1_s[:, part, f, c0:c0 + P],
                                 lambda part, f: ft[:, part, f, :], KE).then_inc(made, 1)

            def project_hidden(l, i, j):
                t = CHUNKS * l + 2 * i + j
                pe.wait_ge(hid_lo, HT * (t + 1) - 1)
                for q in range(CT):
                    if q % 2 == 0 and not is_first(i, j):
                        pe.wait_ge(f_ready, 2 * t - 1 + q // 2)
                    for f in range(HT):
                        if q == 0 and f == HT - 1:
                            pe.wait_ge(hid_lo, HT * (t + 1))
                        for n, (a, b) in enumerate(PRODUCTS):
                            mm = pe.matmul(ps_out[:, q // 2, (q % 2) * E:(q % 2 + 1) * E], hid[:, a, f, q * P:(q + 1) * P],
                                           w2_s[:, b, f, :], start=f == 0 and n == 0,
                                           stop=f == HT - 1 and n == len(PRODUCTS) - 1)
                    if q % 2:
                        mm.then_inc(f_made, 1)

            def chunk(l, i, j, last=False):
                hidden_tiles(l, i, j)
                if not last:
                    turn_f(l, i + j, 1 - j)
                project_hidden(l, i, j)

            pe.wait_ge(masks_made, 5)
            with pe.Fori(0, DEPTH) as l:
                pe.wait_ge(weights_split, 4 * l + 2)
                turn_h(l, 0, 0)
                for s in (1, 0):
                    project_side(l, 0, 0, s)
                turn_h(l, 0, 1)
                project_v(l, 0, 0)
                for s in (1, 0):
                    project_side(l, 0, 1, s)
                step(l, 0, 0, before=False)
                step(l, 0, 1)
                with pe.Fori(1, WI - 1) as i:
                    for j in range(2):
                        step(l, i, j)
                step(l, WI - 1, 0, next2=False)
                step(l, WI - 1, 1, next1=False, next2=False)
                weighted(l, WI - 1, 1, PAIRS - 1)
                project_out(l, WI - 1, 1)
                pe.wait_ge(weights_split, 4 * l + 4)
                turn_f(l, 0, 0)
                for j in range(2):
                    chunk(l, 0, j)
                with pe.Fori(1, CI - 1) as i:
                    for j in range(2):
                        chunk(l, i, j)
                chunk(l, CI - 1, 0)
                chunk(l, CI - 1, 1, last=True)

        @block.scalar
        def _(act):
            def project(l, i, j):
                t = WINDOWS * l + 2 * i + j
                act.wait_ge(h_turned, t + 1)
                if not (isinstance(i, int) and i == 0):
                    act.wait_ge(v_made, t - 1)
                act.activation(ht[j][:, HI].rearrange("p f n -> p (f n)"), ps_h[:, 0:E], ACT.Copy).then_inc(h_hi, 1)

            def squares(l, i, j, s):
                n = 2 * (WINDOWS * l + 2 * i + j) + 1 - s
                act.wait_ge(qk_made, n + 1)
                if not is_first(i, j):
                    act.wait_ge(norm_sum, n - 1)
                act.activation(side(square, s).rearrange("p h d -> p (h d)"), ps_qk[:, s, :], ACT.Square).then_inc(sq_ready, 1)

            def unit_hi(l, i, j, s):
                t = WINDOWS * l + 2 * i + j
                act.wait_ge(u_ready, 2 * t + 2 - s)
                if not is_first(i, j):
                    act.wait_ge(ta_made, TURNS * t - 2 - s)
                    act.wait_ge(td_made, TURNS * t - 2 - s)
                if s == 0:
                    act.activation(halves_q[:, :, HI, :], unit[:, 0:HL, :], ACT.Copy).then_inc(u_hi, 1)
                else:
                    act.activation(halves_k[:, :, 0:3:2, :], unit[:, HL:2 * HL, :].unsqueeze(2).broadcast_to([P, HL, 2, DL]),
                                   ACT.Copy).then_inc(u_hi, 1)

            def stack(l, i, j, n):
                t = WINDOWS * l + 2 * i + j
                act.wait_ge(ta_made, TURNS * t + n + 1)
                if n == 0 and not is_first(i, j):
                    act.wait_ge(s_made, PAIRS * t)
                out = queries[:, 0:4, :] if n == 2 else keys[:, n, 0:4, j, :]
                act.activation(out, ps_ta[:].rearrange("p (h n) -> p h n", h=4), ACT.Copy).then_inc(ta_used, 1)

            def keep_values(l, i, j):
                t = WINDOWS * l + 2 * i + j
                act.wait_ge(v_made, t + 1)
                if not is_first(i, j):
                    act.wait_ge(o_made, t)
                act.activation(values[:, j].rearrange("p h d -> p (h d)"), ps_v[:], ACT.Copy).then_inc(v_kept, 1)

            def exponentials(l, i, j, p):
                t = WINDOWS * l + 2 * i + j
                act.wait_ge(max_ready, PAIRS * t + p + 1)
                if p >= 2:
                    act.wait_ge((ta_made, td_made)[p % 2], TURNS * t + 4)
                elif not is_first(i, j):
                    act.wait_ge((ta_made, td_made)[p % 2], TURNS * t)
                for h2 in range(2):
                    h = 2 * p + h2
                    ins = act.activation(prob[p % 2][:, h2, :], ps_s[:, p % 2, h2 * 2 * P:(h2 + 1) * 2 * P], ACT.Exp,
                                         bias=minus_max[:, h:h + 1], accum_out=row_sum[:, h:h + 1])
                ins.then_inc(exp_ready, 1)

            def turned_prob(l, i, j, p):
                t = WINDOWS * l + 2 * i + j
                act.wait_ge(ta_made, TURNS * t + 4 + p // 2)
                if p == 0 and not is_first(i, j):
                    act.wait_ge(o_made, t)
                if p == 2:
                    act.wait_ge(o_part, 2 * t + 1)
                act.activation(prob_t[0].rearrange("p h s n -> p (h s n)"), ps_ta[:], ACT.Copy).then_inc(ta_used, 1)

            def outputs_hi(l, i, j):
                t = WINDOWS * l + 2 * i + j
                act.wait_ge(o_made, t + 1)
                if not is_first(i, j):
                    act.wait_ge(y_made, t)
                act.activation(heads[:, HI].rearrange("p f n -> p (f n)"), ps_h[:], ACT.Copy).then_inc(o_hi, 1)

            def step(l, i, j, before=True, next1=True, next2=True):
                stack(l, i, j, 0)
                if before:
                    outputs_hi(l, *away(i, j, -1))
                stack(l, i, j, 1)
                keep_values(l, i, j)
                stack(l, i, j, 2)
                if next2:
                    project(l, *away(i, j, 2))
                if next1:
                    unit_hi(l, *away(i, j, 1), 1)
                exponentials(l, i, j, 0)
                exponentials(l, i, j, 1)
                turned_prob(l, i, j, 0)
                exponentials(l, i, j, 2)
                exponentials(l, i, j, 3)
                if next2:
                    squares(l, *away(i, j, 2), 1)
                turned_prob(l, i, j, 2)
                if next1:
                    unit_hi(l, *away(i, j, 1), 0)
                if next2:
                    squares(l, *away(i, j, 2), 0)

            def affine_tiles(l, i, j):
                t = CHUNKS * l + 2 * i + j
                for f in range(KE):
                    act.wait_ge(f_turned, KE * t + f + 1)
                    if not is_first(i, j):
                        act.wait_ge(f_lo, KE * t)
                    act.activation(affine[:, f, :], ps_ft[:, f, :], ACT.Identity, bias=gb[:, 1, f:f + 1],
                                   scale=gb[:, 0, f:f + 1]).then_inc(f_affine, 1)

            def hidden_hi(t, k, first):
                act.wait_ge(hid_ready, HT * t + k + 1)
                if k == 0 and not first:
                    act.wait_ge(f_made, 2 * t)
                act.activation(hid[:, HI, k, :], hidden[k % 2], ACT.Copy).then_inc(hid_hi, 1)

            def chunk(l, i, j, last=False):
                t = CHUNKS * l + 2 * i + j
                for k in range(HT):
                    act.wait_ge(g_made, HT * t + k + 1)
                    if not is_first(i, j) or k >= 2:
                        act.wait_ge(hid_ready, HT * t + k - 1)
                    act.activation(gate[k % 2], ps_ga[k % 2][0][:], ACT.Gelu, bias=b1_t[:, HT + k:HT + k + 1]).then_inc(gate_ready, 1)
                    if k:
                        hidden_hi(t, k - 1, is_first(i, j))
                hidden_hi(t, HT - 1, is_first(i, j))
                if not last:
                    affine_tiles(l, i + j, 1 - j)

            def weights_hi_parts(parts):
                at = 0
                for dst, k, cols in parts:
                    raw = w_raw[:, at:at + k * cols].rearrange("p (k n) -> p k n", k=k)
                    at += k * cols
                    act.activation(dst[:, HI], raw, ACT.Copy).then_inc(weights_hi, 1)

            with act.Fori(0, DEPTH) as l:
                act.wait_ge(weights_in, (QKV_IN + MLP_IN) * l + QKV_IN)
                weights_hi_parts(((wqkv_s, KE, 3 * INNER), (wo_s, PAIRS, E)))
                project(l, 0, 0)
                for s in (1, 0):
                    squares(l, 0, 0, s)
                project(l, 0, 1)
                for s in (1, 0):
                    unit_hi(l, 0, 0, s)
                for s in (1, 0):
                    squares(l, 0, 1, s)
                step(l, 0, 0, before=False)
                step(l, 0, 1)
                with act.Fori(1, WI - 1) as i:
                    for j in range(2):
                        step(l, i, j)
                step(l, WI - 1, 0, next2=False)
                act.wait_ge(weights_in, (QKV_IN + MLP_IN) * (l + 1))
                weights_hi_parts(((w1_s, KE, 2 * HIDP), (w2_s, HT, E)))
                step(l, WI - 1, 1, next1=False, next2=False)
                outputs_hi(l, WI - 1, 1)
                affine_tiles(l, 0, 0)
                for j in range(2):
                    chunk(l, 0, j)
                with act.Fori(1, CI - 1) as i:
                    for j in range(2):
                        chunk(l, i, j)
                chunk(l, CI - 1, 0)
                chunk(l, CI - 1, 1, last=True)

        @block.vector
        def _(dve):
            def split_weights(l, base, parts):
                at = 0
                for n, (dst, k, cols) in enumerate(parts):
                    raw = w_raw[:, at:at + k * cols].rearrange("p (k n) -> p k n", k=k)
                    at += k * cols
                    dve.wait_ge(weights_hi, 4 * l + base + n + 1)
                    dve.tensor_tensor(dst[:, LO], raw, dst[:, HI], ALU.subtract).then_inc(weights_split, 1)

            def project(l, i, j):
                t = WINDOWS * l + 2 * i + j
                dve.wait_ge(h_hi, t + 1)
                dve.tensor_tensor(ht[j][:, LO].rearrange("p f n -> p (f n)"), ps_h[:, 0:E],
                                  ht[j][:, HI].rearrange("p f n -> p (f n)"), ALU.subtract).then_inc(h_lo, 1)

            def norms(l, i, j, s):
                n = 2 * (WINDOWS * l + 2 * i + j) + 1 - s
                dve.wait_ge(sq_ready, n + 1)
                if not is_first(i, j):
                    dve.wait_ge(r_ready, n - 1)
                dve.tensor_reduce(side(norm2, s), side(square, s), AX.X, ALU.add).then_inc(norm_sum, 1)
                dve.wait_ge(norm_sum, n + 1)
                dve.tensor_scalar(side(norm2, s), side(norm2, s), 1e-24, None, ALU.max).then_inc(norm_ready, 1)

            def rotate(l, i, j, s):
                n = 2 * (WINDOWS * l + 2 * i + j) + 1 - s
                w = 2 * (i % 4) + j
                qk = ps_qk[:].rearrange("p s (h d) -> p s h d", h=HL)
                dve.wait_ge(sq_ready, n + 1)
                if not is_first(i, j):
                    dve.wait_ge(added, n - 1)
                half = DL // 2
                cos = rotary[:, w, s, 0, :].unsqueeze(1).broadcast_to([P, HL, DL])
                dve.tensor_tensor(straight[:, s], qk[:, s], cos, ALU.mult)
                for a in range(2):
                    mine, other = slice(a * half, (a + 1) * half), slice((1 - a) * half, (2 - a) * half)
                    sin = rotary[:, w, s, 1, mine].unsqueeze(1).broadcast_to([P, HL, half])
                    ins = dve.tensor_tensor(crossed[:, s, :, mine], qk[:, s, :, other], sin, ALU.mult)
                ins.then_inc(crossed_ready, 1)

            def stack(l, i, j, n):
                t = WINDOWS * l + 2 * i + j
                dve.wait_ge(td_made, TURNS * t + n + 1)
                if n == 0 and not is_first(i, j):
                    dve.wait_ge(s_made, PAIRS * t)
                out = queries[:, 4:8, :] if n == 2 else keys[:, n, 4:8, j, :]
                dve.tensor_copy(out, ps_td[:].rearrange("p (h n) -> p h n", h=4)).then_inc(td_used, 1)

            def maxima(t, p):
                dve.wait_ge(s_made, PAIRS * t + p + 1)
                dve.tensor_reduce(minus_max[:, 2 * p:2 * p + 2], ps_s[:, p % 2, :].rearrange("p (h n) -> p h n", h=2),
                                  AX.X, ALU.max, negate=True).then_inc(max_ready, 1)

            def normalise(t, p):
                dve.wait_ge(exp_ready, PAIRS * t + p + 1)
                dve.reciprocal(row_inv[:, 2 * p:2 * p + 2], row_sum[:, 2 * p:2 * p + 2]).then_inc(inv_ready, 1)
                dve.wait_ge(inv_ready, PAIRS * t + p + 1)
                for h2 in range(2):
                    h = 2 * p + h2
                    ins = dve.tensor_scalar(prob[p % 2][:, h2, :], prob[p % 2][:, h2, :], row_inv[:, h:h + 1], None, ALU.mult)
                ins.then_inc(p_ready, 1)

            def turned_prob(t, p, skip):
                dve.wait_ge(td_made, TURNS * t + 4 + p // 2)
                if p == 1 and not skip:
                    dve.wait_ge(o_made, t)
                if p == 3:
                    dve.wait_ge(o_part, 2 * t + 2)
                dve.tensor_copy(prob_t[1].rearrange("p h s n -> p (h s n)"), ps_td[:]).then_inc(td_used, 1)

            def outputs_lo(l, i, j):
                t = WINDOWS * l + 2 * i + j
                dve.wait_ge(o_hi, t + 1)
                dve.tensor_tensor(heads[:, LO].rearrange("p f n -> p (f n)"), ps_h[:],
                                  heads[:, HI].rearrange("p f n -> p (f n)"), ALU.subtract).then_inc(o_lo, 1)

            def add_residual(l, i, j):
                t = WINDOWS * l + 2 * i + j
                dve.wait_ge(y_made, t + 1)
                dve.wait_ge(res_in[j], 16 * (WI * l + i + 1))
                if not is_window(i, j, 0, 1):
                    dve.wait_ge(mid_out[j], 16 * (WI * l + i))
                dve.tensor_tensor(mid[j], ps_v[:, 0:E], res[j], ALU.add).then_inc(y_ready, 1)

            def step(l, i, j, before=True, next1=True, next2=True):
                t = WINDOWS * l + 2 * i + j
                stack(l, i, j, 0)
                if next1:
                    norms(l, *away(i, j, 1), 0)
                stack(l, i, j, 1)
                if before:
                    outputs_lo(l, *away(i, j, -1))
                stack(l, i, j, 2)
                if next2:
                    project(l, *away(i, j, 2))
                if before:
                    add_residual(l, *away(i, j, -1))
                maxima(t, 0)
                maxima(t, 1)
                normalise(t, 0)
                normalise(t, 1)
                maxima(t, 2)
                turned_prob(t, 1, is_first(i, j))
                maxima(t, 3)
                normalise(t, 2)
                if next1:
                    rotate(l, *away(i, j, 1), 0)
                normalise(t, 3)
                if next2:
                    rotate(l, *away(i, j, 2), 1)
                    norms(l, *away(i, j, 2), 1)
                turned_prob(t, 3, is_first(i, j))

            def deviation(l, i, j):
                t = CHUNKS * l + 2 * i + j
                dve.wait_ge(f_in[j], 32 * (CI * l + i + 1))
                for q in range(CT):
                    dve.bn_stats(stats[:, q, :], fin[j][:, q, :]).then_inc(f_stats, 1)
                dve.wait_ge(f_stats, CT * (t + 1))
                dve.sem_inc(f_counted, 1)
                for q in range(CT):
                    dve.bn_aggr(mean_var[:, q, :], stats[:, q, :]).then_inc(f_aggr, 1)
                dve.wait_ge(f_aggr, CT * (t + 1))
                dve.tensor_scalar(var_eps, mean_var[:, :, 1], EPS, None, ALU.add).then_inc(f_var, 1)

            def layer_norm(l, i, j):
                t = CHUNKS * l + 2 * i + j
                dve.wait_ge(f_rstd, t + 1)
                for q in range(CT):
                    ins = dve.tensor_scalar(fin[j][:, q, :], fin[j][:, q, :], mean_var[:, q, 0:1], rstd[:, q:q + 1],
                                            ALU.subtract, ALU.mult)
                ins.then_inc(f_norm, 1)

            def split_input(l, i, j):
                t = CHUNKS * l + 2 * i + j
                for f in range(KE):
                    dve.wait_ge(f_affine, KE * t + f + 1)
                    dve.tensor_copy(ft[:, HI, f, :], affine[:, f, :]).then_inc(f_hi, 1)

            def chunk(l, i, j, last=False):
                t = CHUNKS * l + 2 * i + j
                for k in range(HT):
                    dve.wait_ge(a_made, HT * t + k + 1)
                    dve.wait_ge(gate_ready, HT * t + k + 1)
                    if not is_first(i, j) or k >= 2:
                        dve.wait_ge(hid_lo, HT * t + k - 1)
                    dve.scalar_tensor_tensor(out=hidden[k % 2], in0=ps_ga[k % 2][1][:], scalar=b1_t[:, k:k + 1],
                                             in1=gate[k % 2], op0=ALU.add, op1=ALU.mult).then_inc(hid_ready, 1)
                    if k == 0 and not last:
                        deviation(l, i + j, 1 - j)
                    if k == 2 and not last:
                        layer_norm(l, i + j, 1 - j)
                if not last:
                    split_input(l, i + j, 1 - j)
                dve.wait_ge(f_res, t + 1)
                if not (isinstance(i, int) and i == 0):
                    dve.wait_ge(f_out[j], 16 * (CI * l + i))
                for half in range(2):
                    dve.wait_ge(f_made, 2 * t + half + 1)
                    dve.tensor_tensor(fout[j][:, 2 * half:2 * half + 2, :], ps_out[:, half, :].rearrange("p (q e) -> p q e", q=2),
                                      fres[j][:, 2 * half:2 * half + 2, :], ALU.add).then_inc(f_ready, 1)

            dve.wait_ge(const_made, 5)
            both = lambda tile: tile[:].unsqueeze(1).broadcast_to([P, 2, P])
            dve.memset(mask_even[:, 0, :, 1, :], NEG).then_inc(masks_made, 1)
            for g in range(4):
                dve.tensor_copy(mask_even[:, g, :, 0, :], both(own_mask))
                if g:
                    dve.tensor_copy(mask_even[:, g, :, 1, :], both(before_mask))
            dve.tensor_copy(mask_odd[:, :, 0, :], both(before_mask)).then_inc(masks_made, 1)
            dve.tensor_copy(mask_odd[:, :, 1, :], both(own_mask)).then_inc(masks_made, 1)
            dve.memset(keys[:, :, :, 1, :].bitcast(F32), 0.0).then_inc(masks_made, 1)
            dve.memset(values[:, 1], 0.0).then_inc(masks_made, 1)
            dve.wait_ge(trig_in, 16)
            with dve.Fori(0, DEPTH) as l:
                dve.wait_ge(weights_in, (QKV_IN + MLP_IN) * l + QKV_IN)
                split_weights(l, 0, ((wqkv_s, KE, 3 * INNER), (wo_s, PAIRS, E)))
                dve.tensor_tensor(rotary[:].rearrange("p w s c d -> p w (s c) d"), trig_t[:],
                                  scale_t[:].unsqueeze(1).broadcast_to([P, PER_BATCH, 4, DL]), ALU.mult).then_inc(trig_scaled, 1)
                dve.wait_ge(trig_scaled, l + 1)
                project(l, 0, 0)
                for s in (1, 0):
                    rotate(l, 0, 0, s)
                    norms(l, 0, 0, s)
                project(l, 0, 1)
                rotate(l, 0, 1, 1)
                norms(l, 0, 1, 1)
                step(l, 0, 0, before=False)
                for m in range(1, 4):
                    step(l, m // 2, m % 2)
                with dve.Fori(2, WI - 1) as i:
                    for j in range(2):
                        step(l, i, j)
                step(l, WI - 1, 0, next2=False)
                step(l, WI - 1, 1, next1=False, next2=False)
                outputs_lo(l, WI - 1, 1)
                add_residual(l, WI - 1, 1)
                dve.wait_ge(weights_in, (QKV_IN + MLP_IN) * (l + 1))
                split_weights(l, 2, ((w1_s, KE, 2 * HIDP), (w2_s, HT, E)))
                deviation(l, 0, 0)
                layer_norm(l, 0, 0)
                split_input(l, 0, 0)
                for j in range(2):
                    chunk(l, 0, j)
                with dve.Fori(1, CI - 1) as i:
                    for j in range(2):
                        chunk(l, i, j)
                chunk(l, CI - 1, 0)
                chunk(l, CI - 1, 1, last=True)


def finish(nc, ctx, tensor, psum, sem, x, layer_in, attn_out, ident, wout_s, out):
    ain = [tensor(ctx, f"ain{j}", [P, CT, E]) for j in range(2)]
    xres = [tensor(ctx, f"xres{j}", [P, CT, E]) for j in range(2)]
    lres = [tensor(ctx, f"lres{j}", [P, CT, E]) for j in range(2)]
    yout = [tensor(ctx, f"yout{j}", [P, CT, E]) for j in range(2)]
    at = [tensor(ctx, f"at{j}", [P, 2, KE, CHUNK], F32R) for j in range(2)]
    ps_at = psum(ctx, "ps_at", [P, KE, CHUNK])
    ps_y = psum(ctx, "ps_y", [P, 2, 2, E])
    a_in, r_in, stored = ([sem(f"o_{n}{j}") for j in range(2)] for n in ("a_in", "r_in", "stored"))
    turned, hi, lo, added, made, ready = (sem("o_" + n) for n in ("turned", "hi", "lo", "added", "made", "ready"))

    with nc.Block() as block:

        @block.sync
        def _(sp):
            def load(i, j):
                rows = slice(j * CHUNK, (j + 1) * CHUNK)
                sp.dma_start(ain[j][:], attn_out[bass.ds(2 * CT * i + CT * j, CT)].rearrange("q p e -> p q e")).then_inc(a_in[j], 16)
                sp.dma_start(xres[j][:], x[i, rows, :].rearrange("(q p) e -> p q e", p=P)).then_inc(r_in[j], 16)
                sp.dma_start(lres[j][:], layer_in[DEPTH, i, 1 + j * CHUNK:1 + (j + 1) * CHUNK, :]
                             .rearrange("(q p) e -> p q e", p=P)).then_inc(r_in[j], 16)

            def store(i, j):
                sp.wait_ge(ready, 2 * (2 * i + j + 1))
                sp.dma_start(out[i, j * CHUNK:(j + 1) * CHUNK, :].rearrange("(q p) e -> p q e", p=P), yout[j][:]).then_inc(stored[j], 16)

            for j in range(2):
                load(0, j)
            with sp.Fori(0, B - 1) as i:
                for j in range(2):
                    store(i, j)
                    load(i + 1, j)
            for j in range(2):
                store(B - 1, j)
            for j in range(2):
                sp.wait_ge(stored[j], 16 * B)

        @block.gpsimd
        def _(pool):
            with pool.Fori(0, B) as i:
                for j in range(2):
                    pool.wait_ge(r_in[j], 32 * (i + 1))
                    pool.tensor_tensor(xres[j][:], xres[j][:], lres[j][:], ALU.add).then_inc(added, 1)

        @block.tensor
        def _(pe):
            def chunk(i, j):
                c = 2 * i + j
                pe.wait_ge(a_in[j], 16 * (i + 1))
                if not is_zero(c):
                    pe.wait_ge(lo, KE * c)
                for f in range(KE):
                    for q in range(CT):
                        mm = pe.transpose(ps_at[:, f, q * P:(q + 1) * P], ain[j][:, q, f * P:(f + 1) * P], ident[:])
                    mm.then_inc(turned, 1)
                pe.wait_ge(lo, KE * (c + 1))
                if not is_zero(c):
                    pe.wait_ge(ready, 2 * c)
                for q in range(CT):
                    mm = products(pe, ps_y[:, q // 2, q % 2, :], lambda part, f: at[j][:, part, f, q * P:(q + 1) * P],
                                  lambda part, f: wout_s[:, part, f, :], KE)
                    if q % 2:
                        mm.then_inc(made, 1)

            for j in range(2):
                chunk(0, j)
            with pe.Fori(1, B) as i:
                for j in range(2):
                    chunk(i, j)

        @block.scalar
        def _(act):
            def chunk(i, j):
                c = 2 * i + j
                for f in range(KE):
                    act.wait_ge(turned, KE * c + f + 1)
                    if not is_zero(i):
                        act.wait_ge(made, 4 * i)
                    act.activation(at[j][:, HI, f, :], ps_at[:, f, :], ACT.Copy).then_inc(hi, 1)

            for j in range(2):
                chunk(0, j)
            with act.Fori(1, B) as i:
                for j in range(2):
                    chunk(i, j)

        @block.vector
        def _(dve):
            def chunk(i, j):
                c = 2 * i + j
                for f in range(KE):
                    dve.wait_ge(hi, KE * c + f + 1)
                    dve.tensor_tensor(at[j][:, LO, f, :], ps_at[:, f, :], at[j][:, HI, f, :], ALU.subtract).then_inc(lo, 1)
                dve.wait_ge(added, c + 1)
                if not is_zero(i):
                    dve.wait_ge(stored[j], 16 * i)
                for half in range(2):
                    dve.wait_ge(made, 2 * c + half + 1)
                    dve.tensor_tensor(yout[j][:, 2 * half:2 * half + 2, :], ps_y[:, half], xres[j][:, 2 * half:2 * half + 2, :],
                                      ALU.add).then_inc(ready, 1)

            for j in range(2):
                chunk(0, j)
            with dve.Fori(1, B) as i:
                for j in range(2):
                    chunk(i, j)

def rotary_constants():
    import numpy as np
    half_idx = np.arange(0, DL, 2, dtype=np.float32)
    inv_freq = 1.0 / np.float32(10000.0) ** (half_idx / np.float32(DL))
    t = np.arange(T, dtype=np.float32)
    freqs = t[:, None] * inv_freq[None, :]
    freqs = np.concatenate([freqs, freqs], axis=-1)
    base = (half_idx + np.float32(0.4 * DL)) / np.float32(1.4 * DL)
    power = (t - T // 2) / np.float32(P // 2)
    scale = base[None, :] ** power[:, None]
    scale = np.concatenate([scale, scale], axis=-1)
    sign = np.where(np.arange(DL) < DL // 2, np.float32(-1), np.float32(1))
    cos, sin = np.cos(freqs), np.sin(freqs) * sign
    tables = np.stack([cos * scale * 8, sin * scale * 8, cos / scale, sin / scale], axis=1).astype(np.float32)
    return np.ascontiguousarray(tables.reshape(PER_BATCH, P, 4, DL).transpose(1, 0, 2, 3))


def kernel(L0_attn_query, L0_attn_key, L0_attn_value, L0_attn_in_proj_weight, L0_attn_out_proj_weight,
           L0_ffn_wqkv, L0_ffn_q_scale, L0_ffn_k_scale, L0_ffn_wo, L0_ffn_ln_g, L0_ffn_ln_b,
           L0_ffn_w1, L0_ffn_b1, L0_ffn_w2, L0_ffn_b2):
    import numpy as np
    import concourse.bacc as bacc
    from concourse.bass_utils import run_bass_kernel_spmd

    def padded(a, axis):
        widths = [(0, 0)] * a.ndim
        widths[axis] = (0, HIDP - HID)
        return np.pad(a, widths)

    def on_partitions(a, tiles):
        return a.reshape(DEPTH, tiles, P).transpose(0, 2, 1)

    def repeated(a):
        return np.broadcast_to(a[:, None], (DEPTH, P) + a.shape[1:])

    w1, b1 = np.asarray(L0_ffn_w1), np.asarray(L0_ffn_b1)
    qs, ks = np.asarray(L0_ffn_q_scale), np.asarray(L0_ffn_k_scale)
    swap = np.r_[DL // 2:DL, 0:DL // 2]
    arrays = {
        "x": np.asarray(L0_attn_query),
        "w_in": np.asarray(L0_attn_in_proj_weight).T,
        "w_out": np.asarray(L0_attn_out_proj_weight).T,
        "w_qkv": np.asarray(L0_ffn_wqkv),
        "w_o": np.asarray(L0_ffn_wo),
        "w1": np.concatenate([padded(w1[..., :HID], 2), padded(w1[..., HID:], 2)], axis=2),
        "w2": padded(np.asarray(L0_ffn_w2), 1),
        "ln_gb": np.stack([on_partitions(np.asarray(L0_ffn_ln_g), KE), on_partitions(np.asarray(L0_ffn_ln_b), KE)], axis=2),
        "b1": np.concatenate([on_partitions(padded(b1[:, :HID], 1), HT), on_partitions(padded(b1[:, HID:], 1), HT)], axis=2),
        "b2": repeated(np.asarray(L0_ffn_b2)),
        "qk_scale": repeated(np.stack([qs, qs[:, swap], ks, ks[:, swap]], axis=1)),
        "trig": rotary_constants(),
    }
    nc = bacc.Bacc("TRN2", target_bir_lowering=False, num_devices=1)
    aps = {}
    for name, a in arrays.items():
        arrays[name] = np.ascontiguousarray(a)
        aps[name] = nc.dram_tensor("in_" + name, a.shape, mybir.dt.from_np(a.dtype), kind="ExternalInput").ap()
    aps["out"] = nc.dram_tensor("out_0", (B, T, E), F32, kind="ExternalOutput").ap()
    build(nc, **aps)
    r = run_bass_kernel_spmd(nc, [{"in_" + name: a for name, a in arrays.items()}], core_ids=[0])
    return r.results[0]["out_0"]
```
